# Optimizing a Trainium2 kernel written in Bass

```python
import numpy as np
import jax
import jax.numpy as jnp

def _softmax(x, axis=-1):
    return jax.nn.softmax(x, axis=axis)

def _gelu(x):
    return jax.nn.gelu(x, approximate=True)

def _silu(x):
    return jax.nn.silu(x)

def _sigmoid(x):
    return jax.nn.sigmoid(x)

def _layernorm(x, axis=-1, eps=1e-05):
    m = jnp.mean(x, axis=axis, keepdims=True)
    v = jnp.var(x, axis=axis, keepdims=True)
    return (x - m) / jnp.sqrt(v + eps)

def _scatter_add(tgt, idx, src, axis=0):
    return tgt.at[idx].add(src)

def _segment_sum(src, seg, n):
    return jax.ops.segment_sum(src, seg, n)
kernel_name = 'mk_gnn_resnorm_d2_gnn_r64_9135b1'

def setup_inputs(seed: int=0):
    np.random.seed(seed)
    _w = jnp.asarray

    def _rec_inputs():
        import jax
        import jax.numpy as jnp
        _gk = jax.random.key(seed)
        x = -0.000202 + 1 * jax.random.normal(jax.random.fold_in(_gk, 1), (50000, 128), jnp.float32)
        src = jax.random.randint(jax.random.fold_in(_gk, 2), (12500,), 0, 50000, jnp.int32)
        dst = jnp.minimum((50000 * jax.random.uniform(jax.random.fold_in(_gk, 3), (12500,)) ** 2.0).astype(jnp.int32), 49999)
        _o = jnp.argsort(dst, stable=True)
        src = src[_o]
        dst = dst[_o]
        edge_type_8 = jax.random.randint(jax.random.fold_in(_gk, 13), (12500,), 0, 8, jnp.int32)
        return (x, src, dst, edge_type_8)
    x, src, dst, edge_type_8 = _rec_inputs()

    def _L0_gnn_setup():
        import jax, jax.numpy as jnp
        import numpy as np
        N = 50000
        E = 12500
        D = 128
        R = 8
        B = 4
        L = 2
        BN_EPS = 0.001

        def _edge_norm(etype, dst, dtype):
            node_norm = jnp.zeros((N,), dtype=dtype)
            for r in range(R):
                mask = (etype == r).astype(dtype)
                cnt = jax.ops.segment_sum(mask, dst, num_segments=N)
                node_norm = jnp.where(cnt > 0, 1.0 / jnp.maximum(cnt, 1.0), node_norm)
            return node_norm[dst][:, None]
        key = jax.random.key(seed)
        ks = jax.random.split(key, 10)
        node_feat = jax.random.normal(ks[0], (N, D), dtype=jnp.float32)
        src = jax.random.randint(ks[1], (E,), 0, N)
        dst = jax.random.randint(ks[2], (E,), 0, N)
        etype = jax.random.randint(ks[3], (E,), 0, R)
        s = 1.0 / np.sqrt(D)
        W_emb = jax.random.normal(ks[4], (D, D), dtype=jnp.float32) * s
        b_emb = jnp.zeros((D,), dtype=jnp.float32)
        bases = jax.random.normal(ks[5], (L, B, D, D), dtype=jnp.float32) * s
        w_coe = jax.random.normal(ks[6], (L, R, B), dtype=jnp.float32) * 0.3
        self_loop = jax.random.normal(ks[7], (L, D, D), dtype=jnp.float32) * s
        bn_gamma = jnp.ones((L, D), dtype=jnp.float32)
        bn_beta = jnp.zeros((L, D), dtype=jnp.float32)
        bn_mean = jnp.zeros((L, D), dtype=jnp.float32)
        bn_var = jnp.ones((L, D), dtype=jnp.float32)
        return {'node_feat': node_feat, 'W_emb': W_emb, 'b_emb': b_emb, 'bases': bases, 'w_coe': w_coe, 'self_loop': self_loop, 'bn_gamma': bn_gamma, 'bn_beta': bn_beta, 'bn_mean': bn_mean, 'bn_var': bn_var, 'src': src, 'dst': dst, 'etype': etype}
    _L0_gnn_all = _L0_gnn_setup()
    _L0_gnn_in = {k: v for k, v in _L0_gnn_all.items() if k in ('W_emb', 'b_emb', 'bases', 'w_coe', 'self_loop', 'bn_gamma', 'bn_beta', 'bn_mean', 'bn_var')}
    del _L0_gnn_all

    def _L1_gnn_setup():
        import jax, jax.numpy as jnp
        import numpy as np
        N = 50000
        E = 12500
        G_DIM = 128
        H1 = 128
        H2 = 32
        HEADS = 4
        R = 8
        NUM_BASES = 20
        NEG_SLOPE = 0.2

        def _rgcn(x, src, dst, edge_type, comp, basis, root, bias):
            W = jnp.einsum('rb,bio->rio', comp, basis)
            xj = x[src]
            out0 = jnp.zeros((N, W.shape[2]), dtype=x.dtype)

            def step(out, wr):
                Wr, r = wr
                mask = (edge_type == r).astype(x.dtype)
                ssum = jax.ops.segment_sum(xj * mask[:, None], dst, num_segments=N)
                cnt = jax.ops.segment_sum(mask, dst, num_segments=N)
                mean = jnp.where(cnt[:, None] > 0, ssum / jnp.maximum(cnt, 1.0)[:, None], 0.0)
                return (out + mean @ Wr, None)
            out, _ = jax.lax.scan(step, out0, (W, jnp.arange(R)))
            return out + x @ root + bias

        def _gat(x, src, dst, gat_w, att_src, att_dst, gat_bias):
            xl = (x @ gat_w).reshape(N, HEADS, H2)
            a_src = jnp.einsum('nhd,hd->nh', xl, att_src)
            a_dst = jnp.einsum('nhd,hd->nh', xl, att_dst)
            loop = jnp.arange(N)
            s2 = jnp.concatenate([src, loop])
            d2 = jnp.concatenate([dst, loop])
            valid = jnp.concatenate([src != dst, jnp.ones((N,), dtype=bool)])
            alpha = jax.nn.leaky_relu(a_src[s2] + a_dst[d2], NEG_SLOPE)
            alpha = jnp.where(valid[:, None], alpha, -jnp.inf)
            m = jax.ops.segment_max(alpha, d2, num_segments=N)
            ea = jnp.exp(alpha - m[d2])
            denom = jax.ops.segment_sum(ea, d2, num_segments=N)
            alpha = ea / denom[d2]
            msg = xl[s2] * alpha[:, :, None]
            out = jax.ops.segment_sum(msg, d2, num_segments=N)
            return out.reshape(N, HEADS * H2) + gat_bias
        key = jax.random.key(seed)
        ks = jax.random.split(key, 12)
        node_features = jax.random.normal(ks[0], (N, G_DIM), dtype=jnp.float32)
        edge_index = jax.random.randint(ks[1], (2, E), 0, N, dtype=jnp.int64)
        edge_type = jax.random.randint(ks[2], (E,), 0, R, dtype=jnp.int64)
        s = 0.1
        comp = jax.random.normal(ks[3], (R, NUM_BASES), dtype=jnp.float32) * s
        basis = jax.random.normal(ks[4], (NUM_BASES, G_DIM, H1), dtype=jnp.float32) * s
        root = jax.random.normal(ks[5], (G_DIM, H1), dtype=jnp.float32) * s
        bias1 = jax.random.normal(ks[6], (H1,), dtype=jnp.float32) * s
        gat_w = jax.random.normal(ks[7], (H1, HEADS * H2), dtype=jnp.float32) * s
        att_src = jax.random.normal(ks[8], (HEADS, H2), dtype=jnp.float32) * s
        att_dst = jax.random.normal(ks[9], (HEADS, H2), dtype=jnp.float32) * s
        gat_bias = jax.random.normal(ks[10], (HEADS * H2,), dtype=jnp.float32) * s
        return {'node_features': node_features, 'edge_index': edge_index, 'edge_type': edge_type, 'comp': comp, 'basis': basis, 'root': root, 'bias1': bias1, 'gat_w': gat_w, 'att_src': att_src, 'att_dst': att_dst, 'gat_bias': gat_bias}
    _L1_gnn_all = _L1_gnn_setup()
    _L1_gnn_in = {k: v for k, v in _L1_gnn_all.items() if k in ('comp', 'basis', 'root', 'bias1', 'gat_w', 'att_src', 'att_dst', 'gat_bias')}
    del _L1_gnn_all
    return {'x': x, 'src': src, 'dst': dst, 'edge_type_8': edge_type_8, 'L0_gnn_W_emb': _L0_gnn_in['W_emb'], 'L0_gnn_b_emb': _L0_gnn_in['b_emb'], 'L0_gnn_bases': _L0_gnn_in['bases'], 'L0_gnn_w_coe': _L0_gnn_in['w_coe'], 'L0_gnn_self_loop': _L0_gnn_in['self_loop'], 'L0_gnn_bn_gamma': _L0_gnn_in['bn_gamma'], 'L0_gnn_bn_beta': _L0_gnn_in['bn_beta'], 'L0_gnn_bn_mean': _L0_gnn_in['bn_mean'], 'L0_gnn_bn_var': _L0_gnn_in['bn_var'], 'L1_gnn_comp': _L1_gnn_in['comp'], 'L1_gnn_basis': _L1_gnn_in['basis'], 'L1_gnn_root': _L1_gnn_in['root'], 'L1_gnn_bias1': _L1_gnn_in['bias1'], 'L1_gnn_gat_w': _L1_gnn_in['gat_w'], 'L1_gnn_att_src': _L1_gnn_in['att_src'], 'L1_gnn_att_dst': _L1_gnn_in['att_dst'], 'L1_gnn_gat_bias': _L1_gnn_in['gat_bias']}

def reference(x, src, dst, edge_type_8, L0_gnn_W_emb, L0_gnn_b_emb, L0_gnn_bases, L0_gnn_w_coe, L0_gnn_self_loop, L0_gnn_bn_gamma, L0_gnn_bn_beta, L0_gnn_bn_mean, L0_gnn_bn_var, L1_gnn_comp, L1_gnn_basis, L1_gnn_root, L1_gnn_bias1, L1_gnn_gat_w, L1_gnn_att_src, L1_gnn_att_dst, L1_gnn_gat_bias):
    import jax
    import jax.numpy as jnp

    def _L0_gnn_ref(node_feat, W_emb, b_emb, bases, w_coe, self_loop, bn_gamma, bn_beta, bn_mean, bn_var, src, dst, etype):
        import jax, jax.numpy as jnp
        import numpy as np
        N = 50000
        E = 12500
        D = 128
        R = 8
        B = 4
        L = 2
        BN_EPS = 0.001

        def _edge_norm(etype, dst, dtype):
            node_norm = jnp.zeros((N,), dtype=dtype)
            for r in range(R):
                mask = (etype == r).astype(dtype)
                cnt = jax.ops.segment_sum(mask, dst, num_segments=N)
                node_norm = jnp.where(cnt > 0, 1.0 / jnp.maximum(cnt, 1.0), node_norm)
            return node_norm[dst][:, None]
        h = node_feat @ W_emb + b_emb
        norm = _edge_norm(etype, dst, h.dtype)
        for l in range(L):
            W = jnp.einsum('rb,bdf->rdf', w_coe[l], bases[l])
            T = jnp.einsum('nd,rdf->rnf', h, W)
            msg = T[etype, src] * norm
            agg = jax.ops.segment_sum(msg, dst, num_segments=N)
            h = agg + h @ self_loop[l]
            h = bn_gamma[l] * (h - bn_mean[l]) * jax.lax.rsqrt(bn_var[l] + BN_EPS) + bn_beta[l]
            h = jax.nn.relu(h)
        return h

    def _L1_gnn_ref(node_features, edge_index, edge_type, comp, basis, root, bias1, gat_w, att_src, att_dst, gat_bias):
        import jax, jax.numpy as jnp
        import numpy as np
        N = 50000
        E = 12500
        G_DIM = 128
        H1 = 128
        H2 = 32
        HEADS = 4
        R = 8
        NUM_BASES = 20
        NEG_SLOPE = 0.2

        def _rgcn(x, src, dst, edge_type, comp, basis, root, bias):
            W = jnp.einsum('rb,bio->rio', comp, basis)
            xj = x[src]
            out0 = jnp.zeros((N, W.shape[2]), dtype=x.dtype)

            def step(out, wr):
                Wr, r = wr
                mask = (edge_type == r).astype(x.dtype)
                ssum = jax.ops.segment_sum(xj * mask[:, None], dst, num_segments=N)
                cnt = jax.ops.segment_sum(mask, dst, num_segments=N)
                mean = jnp.where(cnt[:, None] > 0, ssum / jnp.maximum(cnt, 1.0)[:, None], 0.0)
                return (out + mean @ Wr, None)
            out, _ = jax.lax.scan(step, out0, (W, jnp.arange(R)))
            return out + x @ root + bias

        def _gat(x, src, dst, gat_w, att_src, att_dst, gat_bias):
            xl = (x @ gat_w).reshape(N, HEADS, H2)
            a_src = jnp.einsum('nhd,hd->nh', xl, att_src)
            a_dst = jnp.einsum('nhd,hd->nh', xl, att_dst)
            loop = jnp.arange(N)
            s2 = jnp.concatenate([src, loop])
            d2 = jnp.concatenate([dst, loop])
            valid = jnp.concatenate([src != dst, jnp.ones((N,), dtype=bool)])
            alpha = jax.nn.leaky_relu(a_src[s2] + a_dst[d2], NEG_SLOPE)
            alpha = jnp.where(valid[:, None], alpha, -jnp.inf)
            m = jax.ops.segment_max(alpha, d2, num_segments=N)
            ea = jnp.exp(alpha - m[d2])
            denom = jax.ops.segment_sum(ea, d2, num_segments=N)
            alpha = ea / denom[d2]
            msg = xl[s2] * alpha[:, :, None]
            out = jax.ops.segment_sum(msg, d2, num_segments=N)
            return out.reshape(N, HEADS * H2) + gat_bias
        src, dst = (edge_index[0], edge_index[1])
        h = _rgcn(node_features, src, dst, edge_type, comp, basis, root, bias1)
        return _gat(h, src, dst, gat_w, att_src, att_dst, gat_bias)
    edge_index = jnp.stack([src, dst])
    x = _layernorm(x + _L0_gnn_ref(x, L0_gnn_W_emb, L0_gnn_b_emb, L0_gnn_bases, L0_gnn_w_coe, L0_gnn_self_loop, L0_gnn_bn_gamma, L0_gnn_bn_beta, L0_gnn_bn_mean, L0_gnn_bn_var, src, dst, edge_type_8), axis=-1)
    x = _layernorm(x + _L1_gnn_ref(x, edge_index, edge_type_8, L1_gnn_comp, L1_gnn_basis, L1_gnn_root, L1_gnn_bias1, L1_gnn_gat_w, L1_gnn_att_src, L1_gnn_att_dst, L1_gnn_gat_bias), axis=-1)
    return x

_drawn_inputs = setup_inputs


def setup_inputs(seed=0):
    import zlib

    import numpy as np

    out = dict(_drawn_inputs(seed))
    spreads = {'L0_gnn_b_emb': (0.0, 0.1),
     'L0_gnn_bn_gamma': (1.0, 0.2),
     'L0_gnn_bn_beta': (0.0, 0.1),
     'L0_gnn_bn_mean': (0.0, 0.1),
     'L0_gnn_bn_var': (1.0, 0.2)}
    factors = {}
    for name, (base, spread) in spreads.items():
        noise = np.random.default_rng([zlib.crc32(name.encode()), seed]).standard_normal(out[name].shape)
        drawn = base * np.exp(spread * noise) if base else spread * noise
        out[name] = jnp.asarray(drawn.astype(out[name].dtype))
    for name, factor in factors.items():
        out[name] = (out[name] * factor).astype(out[name].dtype)
    return out
```

```python
import concourse.bass as bass
from concourse import mybir
from contextlib import ExitStack


def gnn_program(nc, x, src, dst, etype, W_emb, b_emb, bases, w_coe, self_loop, bn_gamma, bn_beta,
                bn_mean, bn_var, comp, basis, root, bias1, gat_w, att_src, att_dst, gat_bias, out):
    f32, bf16, i32 = mybir.dt.float32, mybir.dt.bfloat16, mybir.dt.int32
    ALU, ACT, AX = mybir.AluOpType, mybir.ActivationFunctionType, mybir.AxisListType
    ds = bass.ds

    P = 128
    N, D = x.shape
    E = src.shape[0]
    R = comp.shape[0]
    NB = comp.shape[1]
    B = bases.shape[1]
    H = att_src.shape[0]
    HD = D // H
    T = -(-E // P)
    CT = 7
    IT = T // (2 * CT)
    SL = 2 * CT
    assert T == IT * SL
    EP = T * P
    TAIL = E - (T - 1) * P
    CW = CT * D
    UW = D + H
    BIG = 1 << 20
    NEG = -1.0e30
    SENT = 60000.0
    assert N - 1 < SENT
    LN_EPS, BN_EPS, SLOPE = 1e-5, 1e-3, 0.2

    NT = N // P
    SUB = 3
    CS = 5
    DI = NT // (SUB * CS * 2)
    NSUB = DI * CS * 2
    assert NSUB * SUB == NT
    SW = SUB * D
    XW = CS * SW
    REST = N - NT * P

    ctx = ExitStack()
    with ctx:
        def sb(name, shape, dt=f32):
            return ctx.enter_context(nc.sbuf_tensor(name, shape, dt))

        def sem(name):
            return ctx.enter_context(nc.semaphore(name))

        def dram(name, shape, dt=f32):
            return nc.dram_tensor(name, shape, dt, kind="Internal").ap()

        dstf_d = dram("dstf_d", (EP,))
        fl_d = dram("fl_d", (3, EP))
        xs_d = dram("xs_d", (EP, D))
        xd_d = dram("xd_d", (EP, D))
        hs_d = dram("hs_d", (EP, D))
        ys_d = dram("ys_d", (EP, D))
        ls_d = dram("ls_d", (EP, D))
        lm_d = dram("lm_d", (EP, D))
        h_d = dram("h_d", (EP, D))
        y_d = dram("y_d", (EP, D))
        l_d = dram("l_d", (EP, D))
        u_d = [dram(f"u{r}_d", (EP, D)) for r in range(3)]
        ua_d = dram("ua_d", (EP, UW))
        cr_d = [dram(f"cr{r}_d", (3, T, D)) for r in range(3)]
        cra_d = dram("cra_d", (2, T, UW))
        cc_d = dram("cc_d", (2, T, R))
        ce_d = dram("ce_d", (2, T, R))
        sm_d = dram("sm_d", (N, 1), i32)

        def chunk(a, c, w=D):
            return a[ds(c * CT * P, CT * P), :].rearrange("(t p) f -> p t f", p=P)

        ident = sb("ident", [P, P])
        ones = sb("ones", [P, P])
        ones3 = sb("ones3", [3, P], bf16)
        Wemb = sb("Wemb", [P, D])
        bemb = sb("bemb", [P, 1])
        bs = sb("bs", [P, 2 * B * D])
        slf = sb("slf", [P, 2 * D])
        bng = sb("bng", [P, 2 * D])
        bnb = sb("bnb", [P, 2 * D])
        bnm = sb("bnm", [P, 2 * D])
        bnv = sb("bnv", [P, 2 * D])
        rt = sb("rt", [P, D])
        b1c = sb("b1c", [P, 1])
        gw = sb("gw_sb", [P, D])
        bass_ = sb("basis_sb", [P, NB * D])
        gbb = sb("gbb", [P, D])
        attb = sb("attb", [P, 2 * D])
        cmpb = sb("cmpb", [P, R * NB])
        wcb = sb("wcb", [P, 2 * R * B])
        V = [sb("V0", [P, B * D]), sb("V1", [P, B * D]), sb("V2", [P, R * D])]
        M = [sb(f"M{l}", [P, D]) for l in range(3)]
        BR = sb("BR", [P, B * D + 4 * D])
        B3h = sb("B3h", [1, 3 * (B * D + 4 * D)], bf16)
        B3 = sb("B3", [3, B * D + 4 * D], bf16)
        b0c = sb("b0c", [P, 1])
        sc = sb("sc", [P, 2 * D])
        vt = sb("vt", [P, 2 * D])
        Wr = sb("Wr", [P, R * D])
        WrT = sb("WrT", [P, R * D])
        wT = sb("wT", [P, 2 * D])
        wbc = sb("wbc", [P, 2 * P])
        bsp = sb("bsp", [1, 2 * (B * D + 4 * D)])

        ei = sb("ei", [T, 4 * P], i32)
        ef = sb("ef", [T, 4 * P])
        fle = sb("fle", [T, 3 * P])
        lead = sb("lead", [T, P])
        fld = sb("fld", [T, 2 * T])
        FBC = sb("FBC", [P, 2 * T])
        mk_in = sb("mk_in", [T, T])
        mk_out = sb("mk_out", [T, T])
        EC = sb("EC", [P, 4 * T])
        src_i = sb("src_i", [P, T], i32)
        dst_i = sb("dst_i", [P, T], i32)
        lead_i = sb("lead_i", [P, T], i32)
        slot_i = sb("slot_i", [P, T], i32)
        iota_i = sb("iota_i", [P, T], i32)
        big_i = sb("big_i", [P, 512], i32)
        OH = sb("OH", [P, T * R])
        CNT = sb("CNT", [P, T * R])
        CB = sb("CB", [P, 2 * T * R])
        ct = sb("ct", [T, 2 * R])
        cti = sb("cti", [T, 2 * R])
        q1 = sb("q1", [P, T * R])
        q2 = sb("q2", [P, T * R])
        eqc = sb("eqc", [P, 2 * T])
        nrm = sb("nrm", [P, T])
        nz = sb("nz", [P, T])
        wq = sb("wq", [P, T])
        C = [sb("C0", [P, T * B]), sb("C1", [P, T * B]), sb("C2", [P, T * R])]
        AS = sb("AS", [P, T * H])
        AD = sb("AD", [P, 2 * T * H])
        MX = sb("MX", [P, T * H])
        EA = sb("EA", [P, T * H])
        ES = sb("ES", [P, T * H])

        G = sb("G", [P, SL * D])
        ZT = [sb(f"ZT{k}", [P, D]) for k in range(2)]
        EQ = [sb(f"EQ{k}", [P, P]) for k in range(2)]
        MS = [sb(f"MS{k}", [P, UW]) for k in range(2)]
        UFL = sb("UFL", [T, 2 * UW])
        CIO = sb("CIO", [T, 2 * UW])
        st = sb("st", [P, SL * 6])
        mv = sb("mv", [P, SL * 2])
        sd = sb("sd", [P, SL])
        rs = sb("rs", [P, SL])
        idx_s = sb("idx_s", [P, SL], i32)
        red = [sb(f"red{k}", [P, 2 * CT * H]) for k in range(2)]
        W1 = sb("W1", [P, CT * UW])

        XB = [sb(f"XB{k}", [P, XW]) for k in range(2)]
        OB = [sb(f"OB{k}", [P, XW]) for k in range(2)]
        xT = [sb(f"xT{k}", [P, SW]) for k in range(2)]
        hT = [sb(f"hT{k}", [P, SW]) for k in range(2)]
        yT = [sb(f"yT{k}", [P, SW]) for k in range(2)]
        YA = sb("YA", [P, 5 * SW])
        ZA = sb("ZA", [P, 5 * SW])
        Y = [YA[:, k * SW:(k + 1) * SW] for k in range(5)]
        Z = [ZA[:, k * SW:(k + 1) * SW] for k in range(5)]
        dst1 = [sb(f"dst1_{k}", [P, SUB * 6]) for k in range(2)]
        dmv1 = [sb(f"dmv1_{k}", [P, SUB * 2]) for k in range(2)]
        dsd1 = [sb(f"dsd1_{k}", [P, SUB]) for k in range(2)]
        drs1 = [sb(f"drs1_{k}", [P, SUB]) for k in range(2)]
        dst2 = [sb(f"dst2_{k}", [P, SUB * 6]) for k in range(2)]
        dmv2 = [sb(f"dmv2_{k}", [P, SUB * 2]) for k in range(2)]
        dsd2 = [sb(f"dsd2_{k}", [P, SUB]) for k in range(2)]
        drs2 = [sb(f"drs2_{k}", [P, SUB]) for k in range(2)]
        dnb2 = [sb(f"dnb2_{k}", [P, SUB]) for k in range(2)]
        eps = sb("eps", [P, 1])

        DB = [b[:, 0:CW] for b in XB]
        XR = [b[:, CW:2 * CW] for b in XB]
        HB = [b[:, 0:CW] for b in OB]
        FLc = [b[0:3, CW:2 * CW] for b in OB]
        UB = [b[:, 0:CT * UW] for b in (YA, ZA)]
        CRc = [b[0:3, CT * UW:2 * CT * UW] for b in (YA, ZA)]

        BK = [ctx.enter_context(nc.psum_tensor(f"BK{k}", [P, 512], f32)) for k in range(8)]

        s_ms = sem("s_ms")
        s_le = sem("s_le")
        s_lw = sem("s_lw")
        s_id = sem("s_id")
        s_ep = sem("s_ep")
        s_fb = sem("s_fb")
        s_fs = sem("s_fs")
        s_mk = sem("s_mk")
        s_ix = sem("s_ix")
        s_cn = sem("s_cn")
        s_smf = sem("s_smf")
        s_smw = sem("s_smw")
        s_pst = [sem(f"s_pst{k}") for k in range(2)]
        s_ga = [sem(f"s_ga{j}") for j in range(SL)]
        s_ik = sem("s_ik")
        s_tick = sem("s_tick")
        s_w1 = sem("s_w1")
        s_wa = sem("s_wa")
        s_wv = sem("s_wv")
        s_b3 = sem("s_b3")
        s_dv = sem("s_dv")
        s_wr = sem("s_wr")
        s_xl = [sem(f"s_xl{k}") for k in range(2)]
        s_os = [sem(f"s_os{k}") for k in range(2)]
        s_tx, s_xt, s_hp, s_ht, s_yp = (sem(n) for n in ("s_tx", "s_xt", "s_hp", "s_ht", "s_yp"))
        s_pre, s_ag1, s_sq1, s_y, s_ty = (sem(n) for n in ("s_pre", "s_ag1", "s_sq1", "s_y", "s_ty"))
        s_yt, s_zp, s_z, s_ag2, s_sq2 = (sem(n) for n in ("s_yt", "s_zp", "s_z", "s_ag2", "s_sq2"))
        s_nb2, s_o = sem("s_nb2"), sem("s_o")
        s_ph = sem("s_ph")
        s_gb = [sem(f"s_gb{k}") for k in range(2)]
        s_db = [sem(f"s_db{k}") for k in range(2)]
        s_xr = [sem(f"s_xr{k}") for k in range(2)]
        s_cl = [sem(f"s_cl{k}") for k in range(2)]
        s_st = [sem(f"s_st{k}") for k in range(2)]
        s_tr = sem("s_tr")
        s_zt = sem("s_zt")
        s_pj = sem("s_pj")
        s_sp = sem("s_sp")
        s_hb = sem("s_hb")
        s_he = sem("s_he")
        s_eq = sem("s_eq")
        s_cm = sem("s_cm")
        s_u = sem("s_u")
        s_ue = sem("s_ue")
        s_ad = sem("s_ad")
        s_sq = sem("s_sq")
        s_ag = sem("s_ag")
        s_cf = sem("s_cf")
        s_cp = sem("s_cp")
        s_ca = sem("s_ca")
        s_cs = sem("s_cs")
        s_cq = sem("s_cq")
        s_ce = sem("s_ce")
        s_g1 = sem("s_g1")
        s_aa = sem("s_aa")
        s_gv = sem("s_gv")
        s_sc = [sem(f"s_sc{j}") for j in range(SL)]
        s_sg = sem("s_sg")

        block = ctx.enter_context(nc.Block())

        def run(eng, its, per, lead, tail, body):
            for s in range(-lead, per):
                body(0, s)
            with eng.Fori(1, its - 1) as i:
                for s in range(per):
                    body(i, s)
            for s in range(per + tail):
                body(its - 1, s)

        def at(i, s, per, count):
            q = i * per + s
            if isinstance(i, int) and not 0 <= q < count:
                return None
            return i + s // per, s % per, q

        def three(a):
            return a.rearrange("p (a f) -> p a f", f=D)

        OFF_BV, OFF_B = 0, B * D
        OFF_DX = OFF_B + 3 * D
        BRW = OFF_DX + D

        def col(k):
            return EC[:, k * T:(k + 1) * T]

        def bc_mid(a, n):
            return a.unsqueeze(1).broadcast_to([a.shape[0], n, a.shape[1]])

        def bc_in(a, n):
            return a.unsqueeze(2).broadcast_to([a.shape[0], a.shape[1], n])

        def four(a):
            return a.rearrange("p (b f) -> p b f", f=D)

        val_s = sb("val_s", [P, SL], i32)
        s_bs1, s_bs2, s_rc1, s_rc2 = (sem(n) for n in ("s_bs1", "s_bs2", "s_rc1", "s_rc2"))
        s_vtick, s_atick = sem("s_vtick"), sem("s_atick")

        def bcast(a):
            return a.partition_broadcast(P)

        LOAD_LIST = [
            (Wemb[:, :], W_emb), (bemb[:, :], b_emb.rearrange("(k o) -> k o", o=1)),
            (four(bs[:, :]), bases.rearrange("l b k f -> k (l b) f")),
            (four(slf[:, :]), self_loop.rearrange("l k f -> k l f")),
            (bng[:, :], bcast(bn_gamma.rearrange("l f -> (l f)"))),
            (bnb[:, :], bcast(bn_beta.rearrange("l f -> (l f)"))),
            (bnm[:, :], bcast(bn_mean.rearrange("l f -> (l f)"))),
            (bnv[:, :], bcast(bn_var.rearrange("l f -> (l f)"))),
            (rt[:, :], root), (b1c[:, :], bias1.rearrange("(k o) -> k o", o=1)), (gw[:, :], gat_w),
            (four(bass_[:, :]), basis.rearrange("b i o -> i b o")),
            (gbb[:, :], bcast(gat_bias)),
            (attb[:, 0:D], bcast(att_src.rearrange("h d -> (h d)"))),
            (attb[:, D:2 * D], bcast(att_dst.rearrange("h d -> (h d)"))),
            (cmpb[:, :], bcast(comp.rearrange("r b -> (r b)"))),
            (wcb[:, :], bcast(w_coe.rearrange("l r b -> (l r b)"))),
        ]
        LOADS = len(LOAD_LIST)

        N_A, N_B = (0, 2, 4), (1, 3, 5)
        HB_N = dict(A1=1, B=(0, 2, 3), O=4)
        LD = dict(A=(0, 2, 4), B=(1, 3, 5, 8), S=6, W=7)
        ST = dict(A=(0, 3, 6), B=(2, 5, 8), S=9, W=10)
        J = (B, B, R)
        src_rows = (xs_d, hs_d, ys_d)
        src_next = (hs_d, ys_d, ls_d)
        table = (None, h_d, y_d, l_d)
        dst_rows = (xd_d, h_d, y_d)
        dst_next = (h_d, y_d, l_d)
        CH = IT * 2

        s_stick = sem("s_stick")
        s_cu = sem("s_cu")
        s_bd = sem("s_bd")
        s_mt = sem("s_mt")
        s_lc = sem("s_lc")

        SMX, TF, TB = (XB[0][0:T, k * H * P:(k + 1) * H * P] for k in range(3))
        pen = XB[1][0:T, 0:P]
        DG = [XB[1][0:T, P + k * H * T:P + (k + 1) * H * T] for k in range(2)]
        PN = [XB[1][0:T, P + 2 * H * T + k * T:P + 2 * H * T + (k + 1) * T] for k in range(2)]
        PF = [OB[0][0:T, k * P:(k + 1) * P] for k in range(2)]
        CI = [OB[1][0:T, k * H:(k + 1) * H] for k in range(2)]
        CX = [OB[0][0:T, 2 * P + k * H * T:2 * P + (k + 1) * H * T] for k in range(2)]

        def EDGE_SP(sp):
            sp.wait_ge(s_fs, 64)

            def phase(load, done, store):
                for k in range(2):
                    load(k, k)

                def step(i, k):
                    c = i * 2 + k
                    done(c)
                    sp.sem_inc(s_stick, 1)
                    store(c, k)
                    if not isinstance(i, int) or i < IT - 1:
                        load(c + 2, k)

                with sp.Fori(0, IT - 1) as i:
                    for k in range(2):
                        step(i, k)
                for k in range(2):
                    step(IT - 1, k)

            def load_g(rows_d, c, k):
                a = k * CT * D
                sp.dma_start(three(G[:, a:a + CW]), chunk(rows_d, c)).then_inc(s_gb[k], 16)

            def load_db(c, k):
                sp.dma_start(DB[k], dstf_d[ds(c * CT * P, CT * P)].partition_broadcast(P)).then_inc(s_db[k], 16)

            phase(load_db, lambda c: sp.wait_ge(s_eq, (c + 1) * CT), lambda c, k: None)
            sp.wait_ge(s_ce, CH)
            for k, p in enumerate((0, P - 1)):
                sp.dma_start(ce_d[k:k + 1].rearrange("o t r -> o (t r)"), CNT[p:p + 1, :]).then_inc(s_cs, 16)
            sp.wait_ge(s_cs, 32)
            for k in range(2):
                sp.dma_start(ct[:, k * R:(k + 1) * R], ce_d[k]).then_inc(s_cf, 16)
            sp.wait_ge(s_ca, 1)
            for k in range(2):
                sp.dma_start(cc_d[k], cti[:, k * R:(k + 1) * R]).then_inc(s_cs, 16)
            sp.wait_ge(s_cs, 64)
            for k in range(2):
                sp.dma_start(CB[:, k * T * R:(k + 1) * T * R],
                             cc_d[k].rearrange("t r -> (t r)").partition_broadcast(P)).then_inc(s_cf, 16)

            def carries(r, rows_d, w, to_d):
                v3 = rows_d.rearrange("(t e) f -> t e f", e=P)
                for k, e in enumerate((0, P - 1)):
                    sp.dma_start(UFL[:, k * w:(k + 1) * w], v3[:, e, :]).then_inc(s_cf, 16)
                sp.wait_ge(s_ca, r + 2)
                for k in range(2):
                    sp.dma_start(to_d[k], CIO[:, k * w:(k + 1) * w]).then_inc(s_cs, 16)
                if r < 3:
                    sp.dma_start(to_d[2], BR[0:T, OFF_B + r * D:OFF_B + (r + 1) * D]).then_inc(s_cs, 16)
                sp.wait_ge(s_cs, 64 + 48 * min(r + 1, 3) + (32 if r == 3 else 0))

            def stored(upto):
                for k in range(2):
                    sp.wait_ge(s_st[k], upto * IT * 16)

            for k in range(2):
                sp.wait_ge(s_pst[k], 2 * IT * 16)
            for r in range(3):
                def load_a(c, k):
                    load_g(src_rows[r], c, k)
                    load_db(c, k)
                    if r == 1:
                        sp.dma_start(three(XR[k]), chunk(xs_d, c)).then_inc(s_xr[k], 16)

                def done_a(c):
                    sp.wait_ge(s_ue, r * T + (c + 1) * CT)
                    if r == 1:
                        sp.wait_ge(s_hb, HB_N["A1"] * T + (c + 1) * CT)
                    else:
                        sp.wait_ge(s_he, r * T + (c + 1) * CT)

                def store_a(c, k):
                    sp.dma_start(chunk(u_d[r], c), three(UB[k][:, 0:CW])).then_inc(s_st[k], 16)
                    sp.dma_start(chunk(src_next[r], c), three(HB[k])).then_inc(s_st[k], 16)

                phase(load_a, done_a, store_a)
                stored(ST["A"][r] + 2)
                carries(r, u_d[r], D, cr_d[r])

                def load_b(c, k):
                    load_g(dst_rows[r], c, k)
                    sp.dma_start(three(UB[k][:, 0:CW]), chunk(u_d[r], c)).then_inc(s_cl[k], 16)
                    sp.dma_start(FLc[k], fl_d[:, ds(c * CT * P, CT * P)]).then_inc(s_cl[k], 16)
                    sp.dma_start(three(CRc[k][:, 0:CW]), cr_d[r][:, ds(c * CT, CT), :]).then_inc(s_cl[k], 16)
                    if r == 1:
                        sp.dma_start(three(XR[k]), chunk(xd_d, c)).then_inc(s_xr[k], 16)

                phase(load_b, lambda c: sp.wait_ge(s_hb, HB_N["B"][r] * T + (c + 1) * CT),
                      lambda c, k: sp.dma_start(chunk(dst_next[r], c), three(HB[k])).then_inc(s_st[k], 16))
                stored(ST["B"][r] + 1)

            phase(lambda c, k: load_g(ls_d, c, k), lambda c: sp.wait_ge(s_sg, c + 1),
                  lambda c, k: store_merged(sp, c, k))
            stored(ST["S"] + 1)

            sp.wait_ge(s_aa, 2)

            def load_w(c, k):
                load_g(lm_d, c, k)
                load_db(c, k)

            phase(load_w, lambda c: sp.wait_ge(s_ue, 3 * T + (c + 1) * CT),
                  lambda c, k: sp.dma_start(chunk(ua_d, c), UB[k].rearrange("p (t f) -> p t f", f=UW)
                                            ).then_inc(s_st[k], 16))
            stored(ST["W"] + 1)
            carries(3, ua_d, UW, cra_d)

            def load_o(c, k):
                load_g(l_d, c, k)
                sp.dma_start(UB[k].rearrange("p (t f) -> p t f", f=UW), chunk(ua_d, c)).then_inc(s_cl[k], 16)
                sp.dma_start(FLc[k][0:2, :], fl_d[0:2, ds(c * CT * P, CT * P)]).then_inc(s_cl[k], 16)
                sp.dma_start(CRc[k][0:2, :].rearrange("p (t f) -> p t f", f=UW),
                             cra_d[:, ds(c * CT, CT), :]).then_inc(s_cl[k], 16)
                sp.dma_start(three(XR[k]), chunk(y_d, c)).then_inc(s_xr[k], 16)

            phase(load_o, lambda c: sp.wait_ge(s_hb, HB_N["O"] * T + (c + 1) * CT), lambda c, k: None)

        def store_merged(sp, c, k):
            sp.dma_start(chunk(lm_d, c), three(G[:, k * CW:(k + 1) * CW])).then_inc(s_st[k], 16)
            sp.wait_ge(s_st[k], ST["S"] * IT * 16 + ((c - k) // 2 + 1) * 16 if isinstance(c, int)
                       else (c - k) * 8 + 16 + ST["S"] * IT * 16)
            sp.sem_inc(s_stick, 1)

        def EDGE_POOL(g, node_bound, slot_bound, gate):
            for n, (tab, ld) in enumerate(((h_d, LD["A"][1]), (y_d, LD["A"][2]), (l_d, LD["S"]))):
                with g.Fori(0, IT) as i:
                    for k in range(2):
                        a = k * CT
                        gate(s_gb[k], (ld * IT + i + 1) * 16)
                        for j in range(a, a + CT):
                            gate(s_ga[j], ((4 + n) * IT + i) * 16)
                        g.tensor_copy(idx_s[:, a:a + CT], slot_i[:, ds(i * SL + a, CT)]).then_inc(s_ik, 1)
                        gate(s_ik, 7 * IT + n * 2 * IT + i * 2 + k + 1)
                        for j in range(a, a + CT):
                            g.indirect_dma_start(
                                out=G[:, j * D:(j + 1) * D], out_offset=None, in_=tab,
                                in_offset=bass.IndirectOffsetOnAxis(ap=idx_s[:, j:j + 1], axis=0),
                                bounds_check=slot_bound, oob_is_err=False).then_inc(s_ga[j], 16)
            for j in range(SL):
                g.wait_ge(s_ga[j], 7 * IT * 16)
            def scatter(i, k):
                a = k * CT
                if not isinstance(i, int):
                    for j in range(a, a + CT):
                        gate(s_sc[j], i * 16)
                g.tensor_copy(idx_s[:, a:a + CT], lead_i[:, ds(i * SL + a, CT)]).then_inc(s_ik, 1)
                gate(s_ik, 13 * IT + i * 2 + k + 1)
                for j in range(a, a + CT):
                    gate(s_hb, HB_N["O"] * T + i * SL + j + 1)
                    g.indirect_dma_start(
                        out=out, out_offset=bass.IndirectOffsetOnAxis(ap=idx_s[:, j:j + 1], axis=0),
                        in_=HB[k][:, (j - a) * D:(j - a + 1) * D], in_offset=None,
                        bounds_check=node_bound, oob_is_err=False).then_inc(s_sc[j], 16)

            for k in range(2):
                scatter(0, k)
            with g.Fori(1, IT) as i:
                for k in range(2):
                    scatter(i, k)
            for j in range(SL):
                g.wait_ge(s_sc[j], IT * 16)

        def EDGE_PE(pe):
            pe.wait_ge(s_wr, NB * R)
            for r in range(R):
                last = nc.tensor.transpose(BK[r // 4][:, (r % 4) * D:(r % 4 + 1) * D],
                                           Wr[:, r * D:(r + 1) * D], ident[:, :])
            last.then_inc(s_w1, 1)
            pe.wait_ge(s_wa, 4)
            for r in range(R):
                last = nc.tensor.matmul(BK[2 + r // 4][:, (r % 4) * D:(r % 4 + 1) * D],
                                        WrT[:, r * D:(r + 1) * D], gw[:, :], start=True, stop=True)
            last.then_inc(s_w1, 1)
            pe.wait_ge(s_wa, 6)

            def count(i, s):
                if (a := at(i, s, SL, T)):
                    it, z, q = a
                    k, j = z // CT, z % CT
                    pe.wait_ge(s_eq, q + 1)
                    if j == 0 and (not isinstance(it, int) or it >= 1):
                        pe.wait_ge(s_ce, it * 2 + k - 1)
                    m = nc.tensor.matmul(BK[4 + k][:, j * R:(j + 1) * R], EQ[z % 2][:, :], OH[:, ds(q * R, R)],
                                         start=True, stop=True).then_inc(s_cu, 1)

            run(pe, IT, SL, 0, 0, count)

            def carries(r, ufl, w, bank):
                pe.wait_ge(s_cf, 32 if r < 0 else 96 + 32 * r)
                nc.tensor.matmul(bank[0:T, 0:w], mk_in[:, :], ufl[:, w:2 * w], start=True, stop=True)
                nc.tensor.matmul(bank[0:T, w:2 * w], mk_out[:, :], ufl[:, 0:w], start=True, stop=True).then_inc(s_cp, 1)

            pe.wait_ge(s_mk, 1)
            carries(-1, ct, R, BK[6])

            def transpose(n, a, waits):
                it, z, q = a
                waits(it, z)
                if not isinstance(q, int) or q >= 2:
                    pe.wait_ge(s_zt, n * T + q - 1)
                nc.tensor.transpose(BK[z % 2][:, 0:D], G[:, z * D:(z + 1) * D], ident[:, :]).then_inc(s_tr, 1)

            for r in range(3):
                def loaded_a(it, z):
                    if r == 0:
                        pe.wait_ge(s_gb[z // CT], (LD["A"][0] * IT + it + 1) * 16)
                    else:
                        pe.wait_ge(s_ga[z], ((3 + r) * IT + it + 1) * 16)

                def a_phase(i, s):
                    if (a := at(i, s + 1, SL, T)):
                        transpose(N_A[r], a, loaded_a)
                    if (a := at(i, s, SL, T)):
                        it, z, q = a
                        pe.wait_ge(s_zt, N_A[r] * T + q + 1)
                        nb = J[r] // 4
                        if not isinstance(q, int) or q >= 2:
                            pe.wait_ge(s_cm, sum(J[:r]) * T + (q - 1) * J[r])
                        for h in range(nb):
                            bank = BK[2 + z % 2] if nb == 1 else BK[2 + 2 * (z % 2) + h]
                            last = nc.tensor.matmul(bank[:, :], ZT[z % 2][:, :], V[r][:, h * 4 * D:(h + 1) * 4 * D],
                                                    start=True, stop=r > 0)
                            if r == 0:
                                last = nc.tensor.matmul(bank[:, :], ones3[:, :], B3[:, OFF_BV:OFF_BV + B * D],
                                                        start=False, stop=True)
                        last.then_inc(s_pj, 1)
                        pe.wait_ge(s_he, r * T + q)
                        nc.tensor.matmul(BK[6][:, 0:D], ZT[z % 2][:, :], M[r][:, :], start=True, stop=False)
                        nc.tensor.matmul(BK[6][:, 0:D], ones3[:, :], B3[:, OFF_B + r * D:OFF_B + (r + 1) * D],
                                         start=False, stop=True).then_inc(s_sp, 1)
                    if (a := at(i, s - 1, SL, T)):
                        it, z, q = a
                        pe.wait_ge(s_cm, sum(J[:r]) * T + (q + 1) * J[r])
                        pe.wait_ge(s_ue, r * T + q)
                        nc.tensor.matmul(BK[7][:, 0:D], EQ[z % 2][:, :], MS[z % 2][:, 0:D],
                                         start=True, stop=True).then_inc(s_u, 1)

                run(pe, IT, SL, 1, 1, a_phase)
                carries(r, UFL, D, BK[4])

                def loaded_b(it, z):
                    if z % CT == 0:
                        pe.wait_ge(s_gb[z // CT], (LD["B"][r] * IT + it + 1) * 16)

                def b_phase(i, s):
                    if (a := at(i, s + 1, SL, T)):
                        transpose(N_B[r], a, loaded_b)
                    if (a := at(i, s, SL, T)):
                        it, z, q = a
                        k, j = z // CT, z % CT
                        pe.wait_ge(s_zt, N_B[r] * T + q + 1)
                        if j == 0:
                            pe.wait_ge(s_cl[k], (r * IT + it + 1) * 48)
                        if not isinstance(q, int) or q >= 2:
                            pe.wait_ge(s_ad, r * T + q - 1)
                        bank = BK[2 + z % 2]
                        nc.tensor.matmul(bank[:, 0:D], ZT[z % 2][:, :], M[r][:, :], start=True, stop=False)
                        nc.tensor.matmul(bank[:, 0:D], FLc[k][:, j * P:(j + 1) * P], CRc[k][:, j * D:(j + 1) * D],
                                         start=False, stop=True).then_inc(s_bd, 1)

                run(pe, IT, SL, 1, 0, b_phase)

            pe.wait_ge(s_gv, 1)
            for h in range(H):
                last = nc.tensor.transpose(BK[4][0:T, h * P:(h + 1) * P], AS[:, h * T:(h + 1) * T], ident[:, :])
            nc.tensor.transpose(BK[7][0:T, 0:T], mk_in[:, :], ident[0:T, 0:T])
            nc.tensor.transpose(BK[7][0:T, T:2 * T], mk_out[:, :], ident[0:T, 0:T]).then_inc(s_g1, 1)
            pe.wait_ge(s_gv, 2)
            for k in range(2):
                last = nc.tensor.matmul(BK[5 + k][0:T, 0:H * T], ones[0:T, 0:T], DG[k], start=True, stop=True)
            last.then_inc(s_g1, 1)
            pe.wait_ge(s_gv, 3)
            for h in range(H):
                last = nc.tensor.transpose(BK[3][:, h * T:(h + 1) * T], SMX[:, h * P:(h + 1) * P], ident[0:T, 0:T])
            last.then_inc(s_g1, 1)

            def w_phase(i, s):
                if (a := at(i, s, SL, T)):
                    it, z, q = a
                    pe.wait_ge(s_mt, q + 1)
                    if not isinstance(q, int) or q >= 2:
                        pe.wait_ge(s_ue, 3 * T + q - 1)
                    nc.tensor.matmul(BK[6 + z % 2][:, 0:UW], EQ[z % 2][:, :], MS[z % 2][:, :],
                                     start=True, stop=True).then_inc(s_u, 1)

            run(pe, IT, SL, 0, 0, w_phase)
            carries(3, UFL, UW, BK[4])

            def o_phase(i, s):
                if (a := at(i, s, SL, T)):
                    it, z, q = a
                    k, j = z // CT, z % CT
                    if j == 0:
                        pe.wait_ge(s_cl[k], (3 * IT + it + 1) * 48)
                    if not isinstance(q, int) or q >= 2:
                        pe.wait_ge(s_ad, 3 * T + q - 1)
                    nc.tensor.matmul(BK[2 + z % 2][:, 0:UW], FLc[k][0:2, j * P:(j + 1) * P],
                                     CRc[k][0:2, j * UW:(j + 1) * UW], start=True, stop=True).then_inc(s_bd, 1)

            run(pe, IT, SL, 0, 0, o_phase)

        def EDGE_ACT(act):
            act.wait_ge(s_w1, 4)
            for k in range(2):
                nc.scalar.copy(WrT[:, k * 4 * D:(k + 1) * 4 * D], BK[k][:, :]).then_inc(s_wa, 1)
            act.wait_ge(s_w1, 5)
            for k in range(2):
                nc.scalar.copy(V[2][:, k * 4 * D:(k + 1) * 4 * D], BK[2 + k][:, :]).then_inc(s_wa, 1)

            with act.Fori(0, IT) as i:
                for k in range(2):
                    act.wait_ge(s_cu, (i * 2 + k + 1) * CT)
                    act.sem_inc(s_atick, 1)
                    nc.scalar.copy(CNT[:, ds((i * 2 + k) * CT * R, CT * R)], BK[4 + k][:, 0:CT * R]).then_inc(s_ce, 1)

            def carries(r, bank, w, to):
                act.wait_ge(s_cp, r + 2)
                nc.scalar.copy(to[:, 0:2 * w], bank[0:T, 0:2 * w]).then_inc(s_ca, 1)

            carries(-1, BK[6], R, cti)

            def transposed(n, a, reader):
                it, z, q = a
                act.wait_ge(s_tr, n * T + q + 1)
                reader(q)
                nc.scalar.copy(ZT[z % 2][:, :], BK[z % 2][:, 0:D]).then_inc(s_zt, 1)

            def deviation(n, z):
                k = z // CT
                act.wait_ge(s_ag, n)
                nc.scalar.activation(sd[:, k * CT:(k + 1) * CT], mv[:, 2 * k * CT + 1:2 * (k + 1) * CT:2],
                                     ACT.Sqrt, bias=eps[:, 0:1]).then_inc(s_sq, 1)

            def out_free(it, k, count, before):
                if not isinstance(it, int) or it >= 1:
                    act.wait_ge(s_st[k], (before * IT + count * it) * 16)

            for r in range(3):
                def read_a(q):
                    if not isinstance(q, int) or q >= 2:
                        act.wait_ge(s_sp, r * T + q - 1)

                def a_phase(i, s):
                    if (a := at(i, s + 1, SL, T)):
                        transposed(N_A[r], a, read_a)
                    if (a := at(i, s, SL, T)):
                        it, z, q = a
                        k, j = z // CT, z % CT
                        if r != 1:
                            act.wait_ge(s_sp, r * T + q + 1)
                            if j == 0:
                                out_free(it, k, 2, ST["A"][r])
                            nc.scalar.activation(HB[k][:, j * D:(j + 1) * D], BK[6][:, 0:D],
                                                 ACT.Relu if r == 0 else ACT.Copy).then_inc(s_he, 1)
                    if (a := at(i, s - 1, SL, T)):
                        it, z, q = a
                        k, j = z // CT, z % CT
                        act.wait_ge(s_u, r * T + q + 1)
                        if j == 0:
                            out_free(it, k, 2, ST["A"][r])
                        nc.scalar.copy(UB[k][:, j * D:(j + 1) * D], BK[7][:, 0:D]).then_inc(s_ue, 1)
                    if r == 1 and (a := at(i, s, SL, T)) and a[1] % CT == CT - 1:
                        deviation(a[0] * 2 + a[1] // CT + 1, a[1])

                run(act, IT, SL, 1, 1, a_phase)
                carries(r, BK[4], D, CIO)

                def read_b(q):
                    if not isinstance(q, int) or q >= 2:
                        act.wait_ge(s_bd, r * T + q - 1)

                def b_phase(i, s):
                    if (a := at(i, s + 1, SL, T)):
                        transposed(N_B[r], a, read_b)
                    if (a := at(i, s, SL, T)) and a[1] % CT == CT - 1:
                        it, z, q = a
                        k = z // CT
                        if r == 0:
                            act.wait_ge(s_ad, q + 1)
                            nc.scalar.activation(HB[k], HB[k], ACT.Relu).then_inc(s_hb, CT)
                        if r == 1:
                            deviation(CH + it * 2 + k + 1, z)

                run(act, IT, SL, 1, 0, b_phase)

            act.wait_ge(s_g1, 1)
            nc.scalar.copy(SMX, BK[4][0:T, :]).then_inc(s_aa, 1)
            act.wait_ge(s_gv, 4)
            nc.scalar.activation(EA[:, :], EA[:, :], ACT.Exp)
            nc.scalar.activation(ES[:, :], ES[:, :], ACT.Exp).then_inc(s_aa, 1)

            def w_phase(i, s):
                if (a := at(i, s, SL, T)):
                    it, z, q = a
                    k, j = z // CT, z % CT
                    act.wait_ge(s_u, 3 * T + q + 1)
                    if j == 0:
                        out_free(it, k, 1, ST["W"])
                    nc.scalar.copy(UB[k][:, j * UW:(j + 1) * UW], BK[6 + z % 2][:, 0:UW]).then_inc(s_ue, 1)

            run(act, IT, SL, 0, 0, w_phase)
            carries(3, BK[4], UW, CIO)

            def o_phase(i, s):
                if (a := at(i, s, SL, T)) and a[1] % CT == CT - 1:
                    deviation(2 * CH + a[0] * 2 + a[1] // CT + 1, a[1])

            run(act, IT, SL, 0, 0, o_phase)

        class LoopChain:

            def __init__(self, v):
                self.v, self.base, self.n, self.per = v, 0, 0, 0

            def loop(self, per):
                self.base += self.per * IT
                self.per = per

            def start(self, i, s):
                if s == 0:
                    self.i, self.n = i, 0

            def __call__(self, ins):
                self.n += 1
                assert self.n <= self.per
                ins.then_inc(s_lc, 1)
                self.v.wait_ge(s_lc, self.i * self.per + self.base + self.n)

        def EDGE_DVE(v, link):
            for b in range(NB):
                for r in range(R):
                    o = Wr[:, r * D:(r + 1) * D]
                    if b:
                        v.wait_ge(s_wr, (b - 1) * R + r + 1)
                        nc.vector.scalar_tensor_tensor(
                            out=o, in0=bass_[:, b * D:(b + 1) * D], scalar=cmpb[:, r * NB + b:r * NB + b + 1],
                            in1=o, op0=ALU.mult, op1=ALU.add).then_inc(s_wr, 1)
                    else:
                        nc.vector.tensor_scalar(o, bass_[:, 0:D], cmpb[:, r * NB:r * NB + 1], None,
                                                ALU.mult).then_inc(s_wr, 1)

            def equal(n, a, done):
                it, z, q = a
                k, j = z // CT, z % CT
                if j == 0:
                    v.wait_ge(s_db[k], (n * IT + it + 1) * 16)
                if not isinstance(q, int) or q >= 2:
                    v.wait_ge(*done(q))
                nc.vector.tensor_scalar(EQ[z % 2][:, :], DB[k][:, j * P:(j + 1) * P], EC[:, ds(q, 1)], None,
                                        ALU.is_equal).then_inc(s_eq, 1)

            run(v, IT, SL, 0, 0, lambda i, s: equal(0, at(i, s, SL, T), lambda q: (s_cu, q - 1)))

            v.wait_ge(s_cf, 64)
            q13, cnt3, oh3 = (a[:, :].rearrange("p (t r) -> p t r", r=R) for a in (q1, CNT, OH))
            q23 = q2[:, :].rearrange("p (t r) -> p t r", r=R)
            for k in range(2):
                link(nc.vector.tensor_tensor(q13, CB[:, k * T * R:(k + 1) * T * R].rearrange("p (t r) -> p t r", r=R),
                                             bc_in(eqc[:, k * T:(k + 1) * T], R), ALU.mult))
                link(nc.vector.tensor_tensor(CNT[:, :], CNT[:, :], q1[:, :], ALU.add))
            link(nc.vector.tensor_scalar(q1[:, :], CNT[:, :], 1.0, None, ALU.max))
            link(nc.vector.reciprocal(q1[:, :], q1[:, :]))
            nc.vector.memset(nz[:, :], 1.0)
            link(nc.vector.memset(nrm[:, :], 0.0))
            for r in reversed(range(R)):
                link(nc.vector.scalar_tensor_tensor(out=wq[:, :], in0=cnt3[:, :, r], scalar=0.0, in1=nz[:, :],
                                                    op0=ALU.is_gt, op1=ALU.mult))
                nc.vector.tensor_tensor(nz[:, :], nz[:, :], wq[:, :], ALU.subtract)
                link(nc.vector.tensor_tensor(q2[:, 0:T], wq[:, :], q13[:, :, r], ALU.mult))
                link(nc.vector.tensor_tensor(nrm[:, :], nrm[:, :], q2[:, 0:T], ALU.add))
            for l in range(2):
                for b in range(B):
                    w = wcb[:, l * R * B:(l + 1) * R * B].rearrange("p (r b) -> p r b", b=B)[:, :, b]
                    link(nc.vector.tensor_tensor(q23, oh3, bc_mid(w, T), ALU.mult))
                    link(nc.vector.tensor_reduce(wq[:, :], q23, AX.X, ALU.add))
                    link(nc.vector.tensor_tensor(C[l][:, :].rearrange("p (t b) -> p t b", b=B)[:, :, b],
                                                 wq[:, :], nrm[:, :], ALU.mult))
            link(nc.vector.tensor_tensor(C[2][:, :], OH[:, :], q1[:, :], ALU.mult))

            lc = LoopChain(v)

            def norm_chunk(z, n, rows_):
                k = z // CT
                for t in range(CT):
                    o = k * CT + t
                    last = nc.vector.bn_stats(st[:, 6 * o:6 * o + 6], rows_[:, t * D:(t + 1) * D])
                lc(last)
                v.sem_inc(s_vtick, 1)
                for t in range(CT):
                    o = k * CT + t
                    last = nc.vector.bn_aggr(mv[:, 2 * o:2 * o + 2], st[:, 6 * o:6 * o + 6])
                last.then_inc(s_ag, 1)
                v.wait_ge(s_sq, n)
                lc(nc.vector.reciprocal(rs[:, k * CT:(k + 1) * CT], sd[:, k * CT:(k + 1) * CT]))
                for t in range(CT):
                    o = k * CT + t
                    w = rows_[:, t * D:(t + 1) * D]
                    nc.vector.tensor_scalar(w, w, mv[:, 2 * o:2 * o + 1], rs[:, o:o + 1], ALU.subtract,
                                            ALU.mult).then_inc(s_hb, 1)

            def scores(rows_, m, c, k, to):
                lc(nc.vector.tensor_tensor(three(W1[:, 0:CW]), three(rows_), bc_mid(attb[:, m * D:(m + 1) * D], CT),
                                           ALU.mult))
                rd = red[k][:, m * CT * H:(m + 1) * CT * H]
                lc(nc.vector.tensor_reduce(rd, W1[:, 0:CW].rearrange("p (a d) -> p a d", d=HD), AX.X, ALU.add))
                return nc.vector.tensor_scalar(to.rearrange("p (h t) -> p t h", t=T)[:, ds(c * CT, CT), :],
                                               rd.rearrange("p (t h) -> p t h", h=H), 1.0, None, ALU.mult)

            def out_free(it, k, count, before):
                if not isinstance(it, int) or it >= 1:
                    v.wait_ge(s_st[k], (before * IT + count * it) * 16)

            for r in range(3):
                lc.loop(4 if r == 1 else 0)

                def a_phase(i, s):
                    if r == 1:
                        lc.start(i, s)
                    a = at(i, s, SL, T)
                    it, z, q = a
                    k, j = z // CT, z % CT
                    equal(1 + r, a, lambda q: (s_u, r * T + q - 1))
                    v.wait_ge(s_pj, r * T + q + 1)
                    o = MS[z % 2][:, 0:D]
                    n = J[r]
                    for b in range(n):
                        bank = BK[2 + z % 2] if n == 4 else BK[2 + 2 * (z % 2) + b // 4]
                        pj = bank[:, (b % 4) * D:(b % 4 + 1) * D]
                        c = C[r][:, ds(q * n + b, 1)]
                        if b == 0:
                            nc.vector.tensor_scalar(o, pj, c, None, ALU.mult).then_inc(s_cm, 1)
                        else:
                            v.wait_ge(s_cm, sum(J[:r]) * T + q * n + b)
                            nc.vector.scalar_tensor_tensor(out=o, in0=pj, scalar=c, in1=o, op0=ALU.mult,
                                                           op1=ALU.add).then_inc(s_cm, 1)
                    if r == 1:
                        v.wait_ge(s_sp, r * T + q + 1)
                        if j == 0:
                            v.wait_ge(s_xr[k], (it + 1) * 16)
                            out_free(it, k, 2, ST["A"][r])
                        nc.vector.scalar_tensor_tensor(
                            out=HB[k][:, j * D:(j + 1) * D], in0=BK[6][:, 0:D], scalar=0.0,
                            in1=XR[k][:, j * D:(j + 1) * D], op0=ALU.max, op1=ALU.add).then_inc(s_he, 1)
                        if j == CT - 1:
                            v.wait_ge(s_he, r * T + q + 1)
                            norm_chunk(z, it * 2 + k + 1, HB[k])

                run(v, IT, SL, 0, 0, a_phase)
                lc.loop((0, 6, 8)[r])

                def b_phase(i, s):
                    if r:
                        lc.start(i, s)
                    it, z, q = at(i, s, SL, T)
                    k, j = z // CT, z % CT
                    v.wait_ge(s_bd, r * T + q + 1)
                    if j == 0:
                        v.wait_ge(s_cl[k], (r * IT + it + 1) * 48)
                        out_free(it, k, 1, ST["B"][r])
                    nc.vector.tensor_tensor(HB[k][:, j * D:(j + 1) * D], BK[2 + z % 2][:, 0:D],
                                            UB[k][:, j * D:(j + 1) * D], ALU.add).then_inc(s_ad, 1)
                    if j == CT - 1 and r == 1:
                        v.wait_ge(s_ad, r * T + q + 1)
                        v.wait_ge(s_xr[k], (IT + it + 1) * 16)
                        lc(nc.vector.scalar_tensor_tensor(out=HB[k], in0=HB[k], scalar=0.0, in1=XR[k],
                                                          op0=ALU.max, op1=ALU.add))
                        norm_chunk(z, CH + it * 2 + k + 1, HB[k])
                    if j == CT - 1 and r == 2:
                        v.wait_ge(s_ad, r * T + q + 1)
                        scores(HB[k], 0, it * 2 + k, k, AD[:, 0:H * T])
                        scores(HB[k], 1, it * 2 + k, k, AD[:, H * T:2 * H * T]).then_inc(s_hb, CT)

                run(v, IT, SL, 0, 0, b_phase)

            lc.loop(4)

            def s_phase(i, k):
                if k == 0:
                    lc.start(i, 0)
                for j in range(k * CT, (k + 1) * CT):
                    v.wait_ge(s_ga[j], (6 * IT + i + 1) * 16)
                scores(G[:, k * CW:(k + 1) * CW], 0, i * 2 + k, k, AS[:, :]).then_inc(s_sg, 1)

            with v.Fori(0, IT) as i:
                for k in range(2):
                    s_phase(i, k)

            hT3 = lambda a: a.rearrange("p (h t) -> p h t", t=T)
            v.wait_ge(s_sg, CH)
            link(nc.vector.tensor_tensor(ES[:, :], AD[:, 0:H * T], AD[:, H * T:2 * H * T], ALU.add))
            link(nc.vector.scalar_tensor_tensor(out=ES[:, :], in0=ES[:, :], scalar=SLOPE, in1=ES[:, :],
                                                op0=ALU.mult, op1=ALU.max))
            link(nc.vector.tensor_tensor(AS[:, :], AS[:, :], AD[:, H * T:2 * H * T], ALU.add))
            nc.vector.tensor_tensor(wq[:, :], col(0), col(1), ALU.is_equal)
            link(nc.vector.scalar_tensor_tensor(out=AS[:, :], in0=AS[:, :], scalar=SLOPE, in1=AS[:, :],
                                                op0=ALU.mult, op1=ALU.max))
            nc.vector.scalar_tensor_tensor(out=hT3(AS[:, :]), in0=bc_mid(wq[:, :], H), scalar=NEG, in1=hT3(AS[:, :]),
                                           op0=ALU.mult, op1=ALU.add).then_inc(s_gv, 1)
            v.wait_ge(s_aa, 1)
            v.wait_ge(s_st[0], (ST["S"] + 1) * IT * 16)
            v.wait_ge(s_st[1], (ST["S"] + 1) * IT * 16)
            m3, f3, b3 = (a.rearrange("t (h e) -> t h e", e=P) for a in (SMX, TF, TB))
            d = 1
            while d < P:
                w = P - d
                link(nc.vector.tensor_tensor(pen[:, 0:w], ef[:, d:P], ef[:, 0:w], ALU.not_equal))
                link(nc.vector.tensor_scalar(pen[:, 0:w], pen[:, 0:w], NEG, None, ALU.mult))
                nc.vector.tensor_tensor(f3[:, :, 0:w], m3[:, :, 0:w], bc_mid(pen[:, 0:w], H), ALU.add)
                link(nc.vector.tensor_tensor(b3[:, :, 0:w], m3[:, :, d:P], bc_mid(pen[:, 0:w], H), ALU.add))
                link(nc.vector.tensor_tensor(m3[:, :, d:P], m3[:, :, d:P], f3[:, :, 0:w], ALU.max))
                link(nc.vector.tensor_tensor(m3[:, :, 0:w], m3[:, :, 0:w], b3[:, :, 0:w], ALU.max))
                d *= 2
            for k, e in enumerate((P - 1, 0)):
                nc.vector.tensor_scalar(PN[k], BK[7][0:T, k * T:(k + 1) * T], 1.0, -NEG, ALU.subtract, ALU.mult)
                nc.vector.tensor_scalar(PF[k], fle[:, k * P:(k + 1) * P], 1.0, -NEG, ALU.subtract, ALU.mult)
                last = nc.vector.tensor_tensor(hT3(DG[k]), bc_mid(ident[0:T, 0:T], H), bc_in(m3[:, :, e], T), ALU.mult)
            last.then_inc(s_gv, 1)
            v.wait_ge(s_g1, 2)
            for k in range(2):
                link(nc.vector.tensor_tensor(hT3(CX[k]), hT3(BK[5 + k][0:T, 0:H * T]), bc_mid(PN[k], H), ALU.add))
                link(nc.vector.tensor_reduce(CI[k], hT3(CX[k]), AX.X, ALU.max))
                link(nc.vector.tensor_tensor(f3, bc_in(CI[k], P), bc_mid(PF[k], H), ALU.add))
                last = nc.vector.tensor_tensor(m3, m3, f3, ALU.max)
                if k == 0:
                    link(last)
            last.then_inc(s_gv, 1)
            v.wait_ge(s_g1, 3)
            link(nc.vector.tensor_tensor(MX[:, :], BK[3][:, 0:H * T], ES[:, :], ALU.max))
            nc.vector.tensor_tensor(EA[:, :], AS[:, :], MX[:, :], ALU.subtract)
            nc.vector.tensor_tensor(ES[:, :], ES[:, :], MX[:, :], ALU.subtract).then_inc(s_gv, 1)
            v.wait_ge(s_aa, 2)

            def w_phase(i, s):
                a = at(i, s, SL, T)
                it, z, q = a
                k, j = z // CT, z % CT
                equal(4, a, lambda q: (s_u, 3 * T + q - 1))
                if j == 0:
                    v.wait_ge(s_gb[k], (LD["W"] * IT + it + 1) * 16)
                e = hT3(EA[:, :])[:, :, ds(q, 1)]
                nc.vector.tensor_tensor(MS[z % 2][:, 0:D].rearrange("p (h d) -> p h d", d=HD),
                                        G[:, z * D:(z + 1) * D].rearrange("p (h d) -> p h d", d=HD),
                                        e.broadcast_to([P, H, HD]), ALU.mult)
                nc.vector.tensor_scalar(MS[z % 2][:, D:UW].unsqueeze(2), e, 1.0, None, ALU.mult).then_inc(s_mt, 1)

            run(v, IT, SL, 0, 0, w_phase)
            lc.loop(14)

            def o_phase(i, s):
                lc.start(i, s)
                it, z, q = at(i, s, SL, T)
                k, j = z // CT, z % CT
                v.wait_ge(s_bd, 3 * T + q + 1)
                if j == 0:
                    v.wait_ge(s_cl[k], (3 * IT + it + 1) * 48)
                u = UB[k][:, j * UW:(j + 1) * UW]
                nc.vector.tensor_tensor(u, BK[2 + z % 2][:, 0:UW], u, ALU.add).then_inc(s_ad, 1)
                if j < CT - 1:
                    return
                c = it * 2 + k
                v.wait_ge(s_gb[k], (LD["B"][3] * IT + it + 1) * 16)
                v.wait_ge(s_xr[k], (2 * IT + it + 1) * 16)
                if not isinstance(it, int) or it >= 1:
                    for t in range(k * CT, (k + 1) * CT):
                        v.wait_ge(s_sc[t], it * 16)
                u3 = UB[k].rearrange("p (t f) -> p t f", f=UW)
                h3 = HB[k].rearrange("p (a d) -> p a d", d=HD)
                es = ES[:, :].rearrange("p (h t) -> p t h", t=T)[:, ds(c * CT, CT), :]
                rd = red[k][:, 0:CT * H]
                v.wait_ge(s_ad, 3 * T + q + 1)
                nc.vector.tensor_tensor(rd.rearrange("p (t h) -> p t h", h=H), u3[:, :, D:UW], es, ALU.add)
                lc(nc.vector.tensor_tensor(
                    HB[k].rearrange("p (t h d) -> p t h d", h=H, d=HD),
                    G[:, k * CW:(k + 1) * CW].rearrange("p (t h d) -> p t h d", h=H, d=HD),
                    es.unsqueeze(3).broadcast_to([P, CT, H, HD]), ALU.mult))
                nc.vector.reciprocal(rd, rd)
                lc(nc.vector.tensor_tensor(three(HB[k]), three(HB[k]), u3[:, :, 0:D], ALU.add))
                lc(nc.vector.tensor_tensor(h3, h3, bc_in(rd, HD), ALU.mult))
                lc(nc.vector.tensor_tensor(three(HB[k]), three(HB[k]), bc_mid(gbb[:, :], CT), ALU.add))
                lc(nc.vector.tensor_tensor(HB[k], HB[k], XR[k], ALU.add))
                norm_chunk(z, 2 * CH + it * 2 + k + 1, HB[k])

            run(v, IT, SL, 0, 0, o_phase)
            assert lc.n == 14

        LE = T * P - P

        @block.sync
        def _(sp):
            sp.wait_ge(s_ms, 1)
            for k, a in enumerate((dst, src, etype)):
                sp.dma_start(ei[0:T - 1, k * P:(k + 1) * P],
                             a[0:LE].rearrange("(t e) -> t e", e=P)).then_inc(s_le, 16)
                sp.dma_start(ei[T - 1:T, k * P:k * P + TAIL], a[LE:E].unsqueeze(0)).then_inc(s_le, 16)
            sp.dma_start(ei[0:1, 3 * P + 1:4 * P], dst[0:P - 1].unsqueeze(0)).then_inc(s_le, 16)
            sp.dma_start(ei[1:T - 1, 3 * P:4 * P],
                         dst[P - 1:LE - 1].rearrange("(t e) -> t e", e=P)).then_inc(s_le, 16)
            sp.dma_start(ei[T - 1:T, 3 * P:3 * P + TAIL + 1], dst[LE - 1:E].unsqueeze(0)).then_inc(s_le, 16)
            sp.wait_ge(s_wv, 4)
            for k in range(3):
                sp.dma_start(B3[k:k + 1, :], B3h[0:1, k * BRW:(k + 1) * BRW]).then_inc(s_b3, 16)
            sp.wait_ge(s_ep, 1)
            sp.dma_start(dstf_d.rearrange("(t e) -> t e", e=P), ef[:, 0:P]).then_inc(s_fs, 16)
            for k in range(3):
                sp.dma_start(fl_d[k].rearrange("(t e) -> t e", e=P), fle[:, k * P:(k + 1) * P]).then_inc(s_fs, 16)

            xv = x[0:NT * P, :].rearrange("(p j) d -> p (j d)", p=P)
            ov = out[0:NT * P, :].rearrange("(p j) d -> p (j d)", p=P)
            for k in range(2):
                sp.dma_start(XB[k][:, :], xv[:, k * XW:(k + 1) * XW]).then_inc(s_xl[k], 16)

            def dense_io(i, k):
                sp.wait_ge(s_pre, (i * 2 + k) * CS + CS)
                if not isinstance(i, int) or i < DI - 1:
                    sp.dma_start(XB[k][:, :], xv[:, ds((i * 2 + k + 2) * XW, XW)]).then_inc(s_xl[k], 16)
                elif k == 0:
                    sp.dma_start(XB[0][:, 0:D], x[N - P:N, :]).then_inc(s_xl[0], 16)
                sp.wait_ge(s_o, (i * 2 + k) * CS + CS)
                sp.dma_start(ov[:, ds((i * 2 + k) * XW, XW)], OB[k][:, :]).then_inc(s_os[k], 16)

            with sp.Fori(0, DI - 1) as i:
                for k in range(2):
                    dense_io(i, k)
            for k in range(2):
                dense_io(DI - 1, k)
            sp.wait_ge(s_o, NSUB + 1)
            sp.dma_start(out[NT * P:N, :], OB[0][P - REST:P, 0:D]).then_inc(s_os[0], 16)
            sp.wait_ge(s_os[0], 16 * (DI + 1))
            sp.wait_ge(s_os[1], 16 * DI)
            EDGE_SP(sp)

        @block.gpsimd
        def _(g):
            g.memset(ei[:, P:3 * P], 0)
            g.memset(ei[:, 0:P], int(SENT))
            g.memset(ei[:, 3 * P:4 * P], int(SENT)).then_inc(s_tick, 1)
            g.wait_ge(s_tick, 1)
            g.memset(ei[0:1, 3 * P:3 * P + 1], -1).then_inc(s_ms, 1)
            g.memset(ident[:, :], 0.0)
            g.memset(eps[:, :], LN_EPS)
            g.memset(ones[:, :], 1.0)
            g.memset(ones3[:, :], 1.0).then_inc(s_tick, 1)
            g.wait_ge(s_tick, 2)
            g.affine_select(out=ident[:, :], in_=ident[:, :], compare_op=ALU.not_equal, fill=1.0, base=0,
                            pattern=[[-1, P]], channel_multiplier=1).then_inc(s_id, 1)
            g.iota(iota_i[:, :], pattern=[[P, T]], base=0, channel_multiplier=1)
            g.memset(big_i[:, :], BIG).then_inc(s_cn, 1)
            g.wait_ge(s_cn, 1)
            g.dma_start(sm_d[0:NT * P, :].rearrange("(p j) o -> p (j o)", p=P), big_i[:, 0:NT]).then_inc(s_smf, 16)
            g.dma_start(sm_d[NT * P:N, :].rearrange("(p j) o -> p (j o)", p=REST),
                        big_i[0:REST, 0:1]).then_inc(s_smf, 16)
            g.wait_ge(s_ep, 2)
            g.affine_select(out=mk_in[:, :], in_=mk_in[:, :], compare_op=ALU.is_gt, fill=0.0, base=0,
                            pattern=[[1, T]], channel_multiplier=-1)
            g.affine_select(out=mk_out[:, :], in_=mk_out[:, :], compare_op=ALU.is_gt, fill=0.0, base=0,
                            pattern=[[-1, T]], channel_multiplier=1).then_inc(s_mk, 1)
            node_bound = g.to_reg(N - 1)
            slot_bound = g.to_reg(EP - 1)
            g.wait_ge(s_ix, 1)

            def gate(sem_, value):
                g.wait_ge(sem_, value)
                g.sem_inc(s_tick, 1)

            for n, (idx, rows_d) in enumerate(((src_i, xs_d), (dst_i, xd_d))):
                def half(i, k):
                    a = k * CT
                    if n or not isinstance(i, int):
                        gate(s_pst[k], (n * IT + i) * 16)
                    g.tensor_copy(idx_s[:, a:a + CT], idx[:, ds(i * SL + a, CT)]).then_inc(s_ik, 1)
                    gate(s_ik, (n * IT + i) * 2 + k + 1)
                    for j in range(a, a + CT):
                        g.indirect_dma_start(
                            out=G[:, j * D:(j + 1) * D], out_offset=None, in_=x,
                            in_offset=bass.IndirectOffsetOnAxis(ap=idx_s[:, j:j + 1], axis=0),
                            bounds_check=node_bound, oob_is_err=False).then_inc(s_ga[j], 16)
                    for j in range(a, a + CT):
                        gate(s_ga[j], (n * IT + i) * 16 + 16)
                    g.dma_start(chunk(rows_d, i * 2 + k), three(G[:, a * D:(a + CT) * D])).then_inc(s_pst[k], 16)

                for k in range(2):
                    half(0, k)
                with g.Fori(1, IT) as i:
                    for k in range(2):
                        half(i, k)
            for k in range(2):
                g.wait_ge(s_pst[k], 2 * IT * 16)
            g.wait_ge(s_smf, 32)
            with g.Fori(0, IT) as i:
                for j in range(SL):
                    gate(s_ga[j], (2 * IT + i) * 16)
                g.tensor_copy(idx_s[:, :], lead_i[:, ds(i * SL, SL)])
                g.tensor_copy(val_s[:, :], iota_i[:, ds(i * SL, SL)]).then_inc(s_ik, 1)
                gate(s_ik, 4 * IT + i + 1)
                for j in range(SL):
                    g.indirect_dma_start(
                        out=sm_d, out_offset=bass.IndirectOffsetOnAxis(ap=idx_s[:, j:j + 1], axis=0),
                        in_=val_s[:, j:j + 1], in_offset=None,
                        bounds_check=node_bound, oob_is_err=False).then_inc(s_ga[j], 16)
            for j in range(SL):
                g.wait_ge(s_ga[j], 3 * IT * 16)
            with g.Fori(0, IT) as i:
                g.tensor_copy(idx_s[:, :], src_i[:, ds(i * SL, SL)]).then_inc(s_ik, 1)
                gate(s_ik, 5 * IT + 2 * i + 1)
                for j in range(SL):
                    g.indirect_dma_start(
                        out=val_s[:, j:j + 1], out_offset=None, in_=sm_d,
                        in_offset=bass.IndirectOffsetOnAxis(ap=idx_s[:, j:j + 1], axis=0),
                        bounds_check=node_bound, oob_is_err=False).then_inc(s_ga[j], 16)
                for j in range(SL):
                    gate(s_ga[j], (3 * IT + i) * 16 + 16)
                g.tensor_copy(slot_i[:, ds(i * SL, SL)], val_s[:, :]).then_inc(s_ik, 1)
                gate(s_ik, 5 * IT + 2 * i + 2)
            EDGE_POOL(g, node_bound, slot_bound, gate)

        @block.tensor
        def _(pe):
            pe.wait_ge(s_lw, LOADS * 16)
            pe.wait_ge(s_id, 1)
            nc.tensor.transpose(BK[0][:, 0:D], Wemb[:, :], ident[:, :])
            nc.tensor.transpose(BK[0][:, D:2 * D], rt[:, :], ident[:, :]).then_inc(s_w1, 1)
            pe.wait_ge(s_wa, 2)
            nc.tensor.matmul(BK[1][:, :], wT[:, 0:D], bs[:, 0:B * D], start=True, stop=True)
            nc.tensor.matmul(BK[2][:, 0:D], wT[:, 0:D], slf[:, 0:D], start=True, stop=True)
            nc.tensor.matmul(BK[2][:, 2 * D:3 * D], wT[:, D:2 * D], gw[:, :], start=True, stop=True)
            pe.wait_ge(s_wv, 1)
            nc.tensor.matmul(BK[2][:, D:2 * D], wbc[:, 0:P], slf[:, 0:D], start=True, stop=True)
            nc.tensor.matmul(BK[3][:, :], wbc[:, 0:P], bs[:, 0:B * D], start=True, stop=True)
            nc.tensor.matmul(BK[2][:, 3 * D:4 * D], wbc[:, P:2 * P], gw[:, :], start=True, stop=True).then_inc(s_w1, 1)
            pe.wait_ge(s_wv, 3)
            nc.tensor.transpose(BK[4][:, 0:D], BR[:, OFF_B:OFF_B + D], ident[:, :]).then_inc(s_w1, 1)
            pe.wait_ge(s_ep, 1)
            nc.tensor.matmul(BK[5][:, 0:2 * T], ones[0:T, :], fld[:, :], start=True, stop=True)
            for k, a in enumerate((ef[:, 0:P], ef[:, P:2 * P], ef[:, 2 * P:3 * P], lead[:, :])):
                last = nc.tensor.transpose(BK[6][:, k * T:(k + 1) * T], a, ident[0:T, 0:T])
            last.then_inc(s_fb, 1)

            def dense(i, s):
                if (a := at(i, s + 2, CS * 2, NSUB + 1)):
                    it, z, q = a
                    pe.wait_ge(s_xl[z // CS], it * 16 + 16)
                    if not isinstance(q, int) or q >= 2:
                        pe.wait_ge(s_xt, q - 1)
                    for t in range(tiles(q)):
                        o = (z % CS) * SW + t * D
                        last = nc.tensor.transpose(BK[z % 2][:, t * D:(t + 1) * D],
                                                   XB[z // CS][:, o:o + D], ident[:, :])
                    last.then_inc(s_tx, 1)
                if (a := at(i, s + 1, CS * 2, NSUB + 1)):
                    it, z, q = a
                    w = tiles(q) * D
                    pe.wait_ge(s_xt, q + 1)
                    pe.wait_ge(s_ht, q)
                    nc.tensor.matmul(BK[2][:, 0:w], M[0][:, :], xT[z % 2][:, 0:w], start=True, stop=True).then_inc(s_hp, 1)
                if (a := at(i, s, CS * 2, NSUB + 1)):
                    it, z, q = a
                    pe.wait_ge(s_ht, q + 1)
                    if not isinstance(q, int) or q >= 2:
                        pe.wait_ge(s_pre, q - 1)
                    last = rows(BK[3 + z % 2], tiles(q), OFF_B + D, hT[z % 2], M[1])
                    last.then_inc(s_yp, 1)
                if (a := at(i, s - 1, CS * 2, NSUB + 1)):
                    it, z, q = a
                    pe.wait_ge(s_y, q + 1)
                    pe.wait_ge(s_yt, q)
                    for t in range(tiles(q)):
                        last = nc.tensor.transpose(BK[5][:, t * D:(t + 1) * D],
                                                   Y[z % 5][:, t * D:(t + 1) * D], ident[:, :])
                    last.then_inc(s_ty, 1)
                if (a := at(i, s - 2, CS * 2, NSUB + 1)):
                    it, z, q = a
                    pe.wait_ge(s_yt, q + 1)
                    if not isinstance(q, int) or q >= 2:
                        pe.wait_ge(s_z, q - 1)
                    last = rows(BK[6 + z % 2], tiles(q), OFF_DX, yT[z % 2], M[2])
                    last.then_inc(s_zp, 1)

            def tiles(q):
                return 1 if isinstance(q, int) and q == NSUB else SUB

            def rows(bank, n, off, lhs, w):
                b = B3[:, off:off + D]
                nc.tensor.matmul(bank[:, 0:n * D], ones3[:, :], b if n == 1 else bc_mid(b, n),
                                 start=True, stop=False)
                for t in range(n):
                    last = nc.tensor.matmul(bank[:, t * D:(t + 1) * D], lhs[:, t * D:(t + 1) * D], w[:, :],
                                            start=False, stop=(t == n - 1))
                return last

            pe.wait_ge(s_b3, 48)
            pe.wait_ge(s_wv, 5)
            run(pe, DI, CS * 2, 2, 3, dense)
            EDGE_PE(pe)

        @block.scalar
        def _(act):
            for dst_ap, src_ap in LOAD_LIST:
                act.dma_start(dst_ap, src_ap).then_inc(s_lw, 16)
            act.wait_ge(s_w1, 1)
            nc.scalar.copy(wT[:, :], BK[0][:, 0:2 * D]).then_inc(s_wa, 1)
            act.wait_ge(s_wv, 1)
            nc.scalar.activation(vt[:, :], vt[:, :], ACT.Sqrt).then_inc(s_wa, 1)

            def dense(i, s):
                if (a := at(i, s + 2, CS * 2, NSUB + 1)):
                    it, z, q = a
                    w = tiles(q) * D
                    act.wait_ge(s_tx, q + 1)
                    if not isinstance(q, int) or q >= 2:
                        act.wait_ge(s_hp, q - 1)
                    nc.scalar.copy(xT[z % 2][:, 0:w], BK[z % 2][:, 0:w]).then_inc(s_xt, 1)
                if (a := at(i, s + 1, CS * 2, NSUB + 1)):
                    it, z, q = a
                    w = tiles(q) * D
                    act.wait_ge(s_hp, q + 1)
                    if not isinstance(q, int) or q >= 2:
                        act.wait_ge(s_yp, q - 1)
                    nc.scalar.activation(hT[z % 2][:, 0:w], BK[2][:, 0:w], ACT.Relu, bias=b0c[:, 0:1]).then_inc(s_ht, 1)
                if (a := at(i, s, CS * 2, NSUB + 1)):
                    it, z, q = a
                    n = tiles(q)
                    act.wait_ge(s_ag1, q + 1)
                    if not isinstance(q, int) or q >= 2:
                        act.wait_ge(s_y, q - 1)
                    nc.scalar.activation(dsd1[z % 2][:, 0:n], dmv1[z % 2][:, 1:2 * n:2], ACT.Sqrt,
                                         bias=eps[:, 0:1]).then_inc(s_sq1, 1)
                if (a := at(i, s - 2, CS * 2, NSUB + 1)):
                    it, z, q = a
                    n = tiles(q)
                    act.wait_ge(s_ag2, q + 1)
                    if not isinstance(q, int) or q >= 2:
                        act.wait_ge(s_nb2, q - 1)
                    nc.scalar.activation(dsd2[z % 2][:, 0:n], dmv2[z % 2][:, 1:2 * n:2], ACT.Sqrt,
                                         bias=eps[:, 0:1]).then_inc(s_sq2, 1)
                if (a := at(i, s - 1, CS * 2, NSUB + 1)):
                    it, z, q = a
                    w = tiles(q) * D
                    act.wait_ge(s_ty, q + 1)
                    if not isinstance(q, int) or q >= 2:
                        act.wait_ge(s_zp, q - 1)
                    nc.scalar.copy(yT[z % 2][:, 0:w], BK[5][:, 0:w]).then_inc(s_yt, 1)
                if (a := at(i, s - 2, CS * 2, NSUB + 1)):
                    it, z, q = a
                    act.wait_ge(s_nb2, q + 1)
                    if z % CS == 0 and (not isinstance(it, int) or it >= 1):
                        act.wait_ge(s_os[z // CS], it * 16)
                    for t in range(tiles(q)):
                        o = (z % CS) * SW + t * D
                        last = nc.scalar.activation(OB[z // CS][:, o:o + D], Z[z % 5][:, t * D:(t + 1) * D],
                                                    ACT.Identity, bias=dnb2[z % 2][:, t:t + 1],
                                                    scale=drs2[z % 2][:, t:t + 1])
                    last.then_inc(s_o, 1)

            def tiles(q):
                return 1 if isinstance(q, int) and q == NSUB else SUB

            act.wait_ge(s_wv, 5)
            run(act, DI, CS * 2, 2, 3, dense)
            EDGE_ACT(act)

        @block.vector
        def _(v):
            chain = [0]

            def link(ins):
                chain[0] += 1
                ins.then_inc(s_dv, 1)
                v.wait_ge(s_dv, chain[0])

            v.wait_ge(s_lw, LOADS * 16)
            nc.vector.tensor_copy(wbc[:, 0:P], bemb[:, 0:1].broadcast_to([P, P]))
            nc.vector.tensor_copy(wbc[:, P:2 * P], b1c[:, 0:1].broadcast_to([P, P]))
            nc.vector.tensor_scalar_add(vt[:, :], bnv[:, :], BN_EPS).then_inc(s_wv, 1)
            v.wait_ge(s_wa, 2)
            link(nc.vector.reciprocal(vt[:, :], vt[:, :]))
            link(nc.vector.tensor_tensor(sc[:, :], bng[:, :], vt[:, :], ALU.mult))
            nc.vector.tensor_tensor(four(V[1]), four(bs[:, B * D:2 * B * D]), bc_mid(sc[:, D:2 * D], B), ALU.mult)
            nc.vector.tensor_tensor(M[1][:, :], slf[:, D:2 * D], sc[:, D:2 * D], ALU.mult)
            link(nc.vector.tensor_tensor(vt[:, :], bnm[:, :], sc[:, :], ALU.mult))
            link(nc.vector.tensor_tensor(vt[:, :], bnb[:, :], vt[:, :], ALU.subtract))
            v.wait_ge(s_w1, 2)
            nc.vector.tensor_tensor(four(V[0]), four(BK[1][:, :]), bc_mid(sc[:, 0:D], B), ALU.mult)
            nc.vector.tensor_tensor(four(BR[:, 0:B * D]), four(BK[3][:, :]), bc_mid(sc[:, 0:D], B), ALU.mult)
            nc.vector.tensor_tensor(M[0][:, :], BK[2][:, 0:D], sc[:, 0:D], ALU.mult)
            nc.vector.tensor_copy(M[2][:, :], BK[2][:, 2 * D:3 * D])
            nc.vector.tensor_tensor(BR[:, OFF_B:OFF_B + D], BK[2][:, D:2 * D], sc[:, 0:D], ALU.mult)
            nc.vector.tensor_copy(BR[:, OFF_B + D:OFF_B + 2 * D], vt[:, D:2 * D])
            nc.vector.tensor_copy(BR[:, OFF_B + 2 * D:OFF_B + 3 * D], BK[2][:, 3 * D:4 * D])
            link(nc.vector.tensor_tensor(BR[:, OFF_DX:OFF_DX + D], BK[2][:, 3 * D:4 * D], gbb[:, :], ALU.add))
            link(nc.vector.tensor_tensor(BR[:, OFF_B:OFF_B + D], BR[:, OFF_B:OFF_B + D], vt[:, 0:D], ALU.add))
            link(nc.vector.tensor_copy(B3h[0:1, 0:BRW], BR[0:1, :]))
            nc.vector.tensor_tensor(bsp[0:1, 0:BRW], BR[0:1, :], B3h[0:1, 0:BRW], ALU.subtract).then_inc(s_wv, 2)
            v.wait_ge(s_wv, 3)
            link(nc.vector.tensor_copy(B3h[0:1, BRW:2 * BRW], bsp[0:1, 0:BRW]))
            link(nc.vector.tensor_tensor(bsp[0:1, BRW:2 * BRW], bsp[0:1, 0:BRW], B3h[0:1, BRW:2 * BRW], ALU.subtract))
            nc.vector.tensor_copy(B3h[0:1, 2 * BRW:3 * BRW], bsp[0:1, BRW:2 * BRW]).then_inc(s_wv, 1)
            v.wait_ge(s_w1, 3)
            nc.vector.tensor_copy(b0c[:, :], BK[4][:, 0:1]).then_inc(s_wv, 1)

            v.wait_ge(s_le, 9 * 16)
            link(nc.vector.tensor_copy(ef[:, :], ei[:, :]))
            v.wait_ge(s_id, 1)
            for k, c in enumerate((0, P - 1)):
                nc.vector.tensor_scalar(fle[:, k * P:(k + 1) * P], ef[:, 0:P], ef[:, c:c + 1], None, ALU.is_equal)
                nc.vector.tensor_scalar(fld[:, k * T:(k + 1) * T], ident[0:T, 0:T], ef[:, c:c + 1], None, ALU.mult)
            nc.vector.memset(fle[:, 2 * P:3 * P], 1.0)
            link(nc.vector.tensor_tensor(lead[:, :], ef[:, 0:P], ef[:, 3 * P:4 * P], ALU.is_equal))
            nc.vector.scalar_tensor_tensor(out=lead[:, :], in0=lead[:, :], scalar=float(BIG), in1=ef[:, 0:P],
                                           op0=ALU.mult, op1=ALU.add).then_inc(s_ep, 1)
            v.wait_ge(s_fb, 1)
            nc.vector.tensor_copy(FBC[:, :], BK[5][:, 0:2 * T])
            link(nc.vector.tensor_copy(EC[:, :], BK[6][:, 0:4 * T]))
            nc.vector.tensor_copy(src_i[:, :], col(1))
            nc.vector.tensor_scalar(dst_i[:, :], col(0), float(N - 1), None, ALU.min)
            nc.vector.tensor_copy(lead_i[:, :], col(3)).then_inc(s_ix, 1)
            nc.vector.tensor_scalar(mk_in[:, :], FBC[0:T, 0:T], ef[:, P - 1:P], None, ALU.is_equal)
            nc.vector.tensor_scalar(mk_out[:, :], FBC[0:T, T:2 * T], ef[:, 0:1], None, ALU.is_equal).then_inc(s_ep, 1)
            nc.vector.tensor_tensor(eqc[:, 0:T], col(0), FBC[:, 0:T], ALU.is_equal)
            nc.vector.tensor_tensor(eqc[:, T:2 * T], col(0), FBC[:, T:2 * T], ALU.is_equal)
            for r in range(R):
                last = nc.vector.tensor_scalar(OH[:, :].rearrange("p (t r) -> p t r", r=R)[:, :, r], col(2), float(r), None, ALU.is_equal)
            link(last)

            def dense(i, s):
                if (a := at(i, s, CS * 2, NSUB + 1)):
                    it, z, q = a
                    n = tiles(q)
                    w = n * D
                    k = z % 2
                    v.wait_ge(s_yp, q + 1)
                    if not isinstance(q, int) or q >= 5:
                        v.wait_ge(s_z, q - 4)
                    nc.vector.scalar_tensor_tensor(
                        out=Y[z % 5][:, 0:w], in0=BK[3 + k][:, 0:w], scalar=0.0,
                        in1=XB[z // CS][:, (z % CS) * SW:(z % CS) * SW + w], op0=ALU.max, op1=ALU.add).then_inc(s_pre, 1)
                    v.wait_ge(s_pre, q + 1)
                    stats(n, Y[z % 5], dst1[k], dmv1[k], s_bs1, s_ag1, q)
                if (a := at(i, s - 2, CS * 2, NSUB + 1)):
                    it, z, q = a
                    n = tiles(q)
                    w = n * D
                    k = z % 2
                    v.wait_ge(s_zp, q + 1)
                    if not isinstance(q, int) or q >= 5:
                        v.wait_ge(s_o, q - 4)
                    nc.vector.tensor_tensor(Z[z % 5][:, 0:w], BK[6 + k][:, 0:w], Y[z % 5][:, 0:w], ALU.add).then_inc(s_z, 1)
                    v.wait_ge(s_z, q + 1)
                    stats(n, Z[z % 5], dst2[k], dmv2[k], s_bs2, s_ag2, q)
                if (a := at(i, s, CS * 2, NSUB + 1)):
                    it, z, q = a
                    n = tiles(q)
                    k = z % 2
                    v.wait_ge(s_sq1, q + 1)
                    nc.vector.reciprocal(drs1[k][:, 0:n], dsd1[k][:, 0:n]).then_inc(s_rc1, 1)
                    v.wait_ge(s_rc1, q + 1)
                    for t in range(n):
                        o = Y[z % 5][:, t * D:(t + 1) * D]
                        last = nc.vector.tensor_scalar(o, o, dmv1[k][:, 2 * t:2 * t + 1], drs1[k][:, t:t + 1],
                                                       ALU.subtract, ALU.mult)
                    last.then_inc(s_y, 1)
                if (a := at(i, s - 2, CS * 2, NSUB + 1)):
                    it, z, q = a
                    n = tiles(q)
                    k = z % 2
                    v.wait_ge(s_sq2, q + 1)
                    nc.vector.reciprocal(drs2[k][:, 0:n], dsd2[k][:, 0:n]).then_inc(s_rc2, 1)
                    v.wait_ge(s_rc2, q + 1)
                    nc.vector.scalar_tensor_tensor(out=dnb2[k][:, 0:n], in0=dmv2[k][:, 0:2 * n:2], scalar=-1.0,
                                                   in1=drs2[k][:, 0:n], op0=ALU.mult, op1=ALU.mult).then_inc(s_nb2, 1)

            def stats(n, rows_, bn, mv_, s_bs, s_ag_, q):
                for t in range(n):
                    last = nc.vector.bn_stats(bn[:, 6 * t:6 * t + 6], rows_[:, t * D:(t + 1) * D])
                last.then_inc(s_bs, 1)
                v.wait_ge(s_bs, q + 1)
                v.sem_inc(s_vtick, 1)
                for t in range(n):
                    last = nc.vector.bn_aggr(mv_[:, 2 * t:2 * t + 2], bn[:, 6 * t:6 * t + 6])
                last.then_inc(s_ag_, 1)

            def tiles(q):
                return 1 if isinstance(q, int) and q == NSUB else SUB

            run(v, DI, CS * 2, 2, 3, dense)
            EDGE_DVE(v, link)


_INS = ["x", "src", "dst", "edge_type_8", "L0_gnn_W_emb", "L0_gnn_b_emb", "L0_gnn_bases", "L0_gnn_w_coe",
        "L0_gnn_self_loop", "L0_gnn_bn_gamma", "L0_gnn_bn_beta", "L0_gnn_bn_mean", "L0_gnn_bn_var",
        "L1_gnn_comp", "L1_gnn_basis", "L1_gnn_root", "L1_gnn_bias1", "L1_gnn_gat_w", "L1_gnn_att_src",
        "L1_gnn_att_dst", "L1_gnn_gat_bias"]


def kernel(**inputs):
    import numpy as np
    import concourse.bacc as bacc
    from concourse.bass_utils import run_bass_kernel_spmd

    nc = bacc.Bacc("TRN2", target_bir_lowering=False, num_devices=1)
    arrays, args = {}, []
    for name in _INS:
        a = np.ascontiguousarray(inputs[name])
        arrays[f"in_{name}"] = a
        args.append(nc.dram_tensor(f"in_{name}", a.shape, mybir.dt.from_np(a.dtype), kind="ExternalInput").ap())
    out = nc.dram_tensor("out", arrays["in_x"].shape, mybir.dt.float32, kind="ExternalOutput").ap()
    gnn_program(nc, *args, out)
    r = run_bass_kernel_spmd(nc, [arrays], core_ids=[0])
    return r.results[0]["out"]
```

```python
import concourse.bass as bass
from concourse import mybir
from contextlib import ExitStack


def gnn_program(nc, x, src, dst, etype, W_emb, b_emb, bases, w_coe, self_loop, bn_gamma, bn_beta,
                bn_mean, bn_var, comp, basis, root, bias1, gat_w, att_src, att_dst, gat_bias, out):
    f32, bf16, i32 = mybir.dt.float32, mybir.dt.bfloat16, mybir.dt.int32
    ALU, ACT, AX = mybir.AluOpType, mybir.ActivationFunctionType, mybir.AxisListType
    ds = bass.ds

    P = 128
    N, D = x.shape
    E = src.shape[0]
    R = comp.shape[0]
    NB = comp.shape[1]
    B = bases.shape[1]
    H = att_src.shape[0]
    HD = D // H
    T = -(-E // P)
    CT = 7
    IT = T // (2 * CT)
    SL = 2 * CT
    GT = (0, 4, CT)
    GS = 4
    NG = IT * GS
    assert T == IT * SL
    EP = T * P
    TAIL = E - (T - 1) * P
    CW = CT * D
    UW = D + H
    BIG = 1 << 20
    NEG = -1.0e30
    SENT = 60000.0
    assert N - 1 < SENT
    LN_EPS, BN_EPS, SLOPE = 1e-5, 1e-3, 0.2

    NT = N // P
    SUB = 3
    NSUB = NT // SUB
    assert NSUB * SUB == NT
    SW = SUB * D
    REST = N - NT * P
    RING = 4
    UNITS = NSUB // RING
    DU = dict(B=[UNITS - (4 - r) * IT for r in range(3)], S=UNITS - IT)
    PRE_UNITS = DU["B"][0]
    assert PRE_UNITS >= 3

    ctx = ExitStack()
    with ctx:
        def sb(name, shape, dt=f32):
            return ctx.enter_context(nc.sbuf_tensor(name, shape, dt))

        def sem(name):
            return ctx.enter_context(nc.semaphore(name))

        def dram(name, shape, dt=f32):
            return nc.dram_tensor(name, shape, dt, kind="Internal").ap()

        dstf_d = dram("dstf_d", (EP,))
        fl_d = dram("fl_d", (3, EP))
        xs_d = dram("xs_d", (EP, D))
        xd_d = dram("xd_d", (EP, D))
        hs_d = dram("hs_d", (EP, D))
        ys_d = dram("ys_d", (EP, D))
        ls_d = dram("ls_d", (EP, D))
        lm_d = dram("lm_d", (EP, D))
        h_d = dram("h_d", (EP, D))
        y_d = dram("y_d", (EP, D))
        l_d = dram("l_d", (EP, D))
        u_d = [dram(f"u{r}_d", (EP, D)) for r in range(3)]
        ua_d = dram("ua_d", (EP, UW))
        cr_d = [dram(f"cr{r}_d", (3, T, D)) for r in range(3)]
        cra_d = dram("cra_d", (2, T, UW))
        cc_d = dram("cc_d", (2, T, R))
        ce_d = dram("ce_d", (2, T, R))
        sm_d = dram("sm_d", (N, 1), i32)

        def chunk(a, c, w=D):
            return a[ds(c * CT * P, CT * P), :].rearrange("(t p) f -> p t f", p=P)

        ident = sb("ident", [P, P])
        ones = sb("ones", [P, P])
        ones3 = sb("ones3", [3, P], bf16)
        Wemb = sb("Wemb", [P, D])
        bemb = sb("bemb", [P, 1])
        bs = sb("bs", [P, 2 * B * D])
        slf = sb("slf", [P, 2 * D])
        bng = sb("bng", [P, 2 * D])
        bnb = sb("bnb", [P, 2 * D])
        bnm = sb("bnm", [P, 2 * D])
        bnv = sb("bnv", [P, 2 * D])
        rt = sb("rt", [P, D])
        b1c = sb("b1c", [P, 1])
        gw = sb("gw_sb", [P, D])
        bass_ = sb("basis_sb", [P, NB * D])
        gbb = sb("gbb", [P, D])
        attb = sb("attb", [P, 2 * D])
        cmpb = sb("cmpb", [P, R * NB])
        wcb = sb("wcb", [P, 2 * R * B])
        V = [sb("V0", [P, B * D]), sb("V1", [P, B * D]), sb("V2", [P, R * D])]
        M = [sb(f"M{l}", [P, D]) for l in range(3)]
        BR = sb("BR", [P, B * D + 4 * D])
        B3h = sb("B3h", [1, 3 * (B * D + 4 * D)], bf16)
        B3 = sb("B3", [3, B * D + 4 * D], bf16)
        b0c = sb("b0c", [P, 1])
        sc = sb("sc", [P, 2 * D])
        vt = sb("vt", [P, 2 * D])
        WW = sb("WW", [P, 2 * R * D])
        Wr, WrT = WW[:, 0:R * D], WW[:, R * D:2 * R * D]
        wT = sb("wT", [P, 2 * D])
        wbc = sb("wbc", [P, 2 * P])

        ei = sb("ei", [T, 4 * P], i32)
        ef = sb("ef", [T, 4 * P])
        fle = sb("fle", [T, 3 * P])
        lead = sb("lead", [T, P])
        fld = sb("fld", [T, 2 * T])
        FBC = sb("FBC", [P, 2 * T])
        mk_in = sb("mk_in", [T, T])
        mk_out = sb("mk_out", [T, T])
        EC = sb("EC", [P, 4 * T])
        src_i = sb("src_i", [P, T], i32)
        dst_i = sb("dst_i", [P, T], i32)
        lead_i = sb("lead_i", [P, T], i32)
        slot_i = sb("slot_i", [P, T], i32)
        iota_i = sb("iota_i", [P, T], i32)
        big_i = sb("big_i", [P, NT], i32)
        OH = sb("OH", [P, T * R])
        CNT = sb("CNT", [P, T * R])
        CB = WW[:, 0:2 * T * R]
        ct = sb("ct", [T, 2 * R])
        cti = sb("cti", [T, 2 * R])
        q1 = sb("q1", [P, T * R])
        q2 = sb("q2", [P, T * R])
        eqc = sb("eqc", [P, 2 * T])
        nrm = sb("nrm", [P, T])
        nz = sb("nz", [P, T])
        wq = sb("wq", [P, T])
        C = [sb("C0", [P, T * B]), sb("C1", [P, T * B]), sb("C2", [P, T * R])]
        AS = sb("AS", [P, T * H])
        AD = sb("AD", [P, 2 * T * H])
        MX = sb("MX", [P, T * H])
        EA = sb("EA", [P, T * H])
        ES = sb("ES", [P, T * H])

        G = sb("G", [P, SL * D])
        ZT = [sb(f"ZT{k}", [P, 4 * D]) for k in range(2)]
        EQ = [sb(f"EQ{k}", [P, P]) for k in range(2)]
        MS = [sb(f"MS{k}", [P, UW]) for k in range(2)]
        MT = [sb(f"MT{k}", [P, D]) for k in range(2)]
        UFL = sb("UFL", [T, 2 * UW])
        CIO = sb("CIO", [T, 2 * UW])
        st = sb("st", [P, SL * 6])
        mv = sb("mv", [P, SL * 2])
        sd = sb("sd", [P, SL])
        rs = sb("rs", [P, SL])
        idx_s = sb("idx_s", [P, SL], i32)
        red = [sb(f"red{k}", [P, 2 * CT * H]) for k in range(2)]
        W1 = sb("W1", [P, CT * UW])

        DB2, XR2, HB2 = (sb(n, [P, 2 * CW]) for n in ("DB2", "XR2", "HB2"))
        UB2 = sb("UB2", [P, 2 * CT * UW])
        FL2 = sb("FL2", [3, 2 * CW])
        CR2 = sb("CR2", [3, 2 * CT * UW])
        DB = [DB2[:, k * CW:(k + 1) * CW] for k in range(2)]
        XR = [XR2[:, k * CW:(k + 1) * CW] for k in range(2)]
        HB = [HB2[:, k * CW:(k + 1) * CW] for k in range(2)]
        UB = [UB2[:, k * CT * UW:(k + 1) * CT * UW] for k in range(2)]
        FLc = [FL2[:, k * CW:(k + 1) * CW] for k in range(2)]
        CRc = [CR2[:, k * CT * UW:(k + 1) * CT * UW] for k in range(2)]
        bsp = [a[0:1, 0:B * D + 4 * D] for a in (XR2, HB2)]

        XB = [sb(f"XB{k}", [P, SW]) for k in range(RING)]
        OB = [sb(f"OB{k}", [P, SW]) for k in range(RING)]
        Y = [sb(f"Y{k}", [P, SW]) for k in range(RING)]
        Z = [sb(f"Z{k}", [P, SW]) for k in range(RING)]
        xT = [sb(f"xT{k}", [P, SW]) for k in range(2)]
        hT = [sb(f"hT{k}", [P, SW]) for k in range(2)]
        yT = [sb(f"yT{k}", [P, SW]) for k in range(2)]
        dst1, dst2 = ([sb(f"dst{n}_{k}", [P, SUB * 6]) for k in range(2)] for n in (1, 2))
        dmv1, dmv2 = ([sb(f"dmv{n}_{k}", [P, SUB * 2]) for k in range(2)] for n in (1, 2))
        dsd1, dsd2 = ([sb(f"dsd{n}_{k}", [P, SUB]) for k in range(2)] for n in (1, 2))
        drs1, drs2 = ([sb(f"drs{n}_{k}", [P, SUB]) for k in range(2)] for n in (1, 2))
        dnb2 = [sb(f"dnb2_{k}", [P, SUB]) for k in range(2)]
        eps = sb("eps", [P, 1])

        BK = [ctx.enter_context(nc.psum_tensor(f"BK{k}", [P, 512], f32)) for k in range(8)]

        s_ms = sem("s_ms")
        s_le = sem("s_le")
        s_lw = sem("s_lw")
        s_id = sem("s_id")
        s_ep = sem("s_ep")
        s_fb = sem("s_fb")
        s_fs = sem("s_fs")
        s_mk = sem("s_mk")
        s_ix = sem("s_ix")
        s_cn = sem("s_cn")
        s_smf = sem("s_smf")
        s_smw = sem("s_smw")
        s_pst = [sem(f"s_pst{k}") for k in range(2)]
        s_ga = [sem(f"s_ga{j}") for j in range(SL)]
        s_ik = sem("s_ik")
        s_tick = sem("s_tick")
        s_w1 = sem("s_w1")
        s_wa = sem("s_wa")
        s_wv = sem("s_wv")
        s_b3 = sem("s_b3")
        s_dv = sem("s_dv")
        s_wr = sem("s_wr")
        s_xl = [sem(f"s_xl{k}") for k in range(RING)]
        s_os = [sem(f"s_os{k}") for k in range(RING)]
        s_tx, s_xt, s_hp, s_ht, s_yp = (sem(n) for n in ("s_tx", "s_xt", "s_hp", "s_ht", "s_yp"))
        s_pre, s_ag1, s_sq1, s_y, s_ty = (sem(n) for n in ("s_pre", "s_ag1", "s_sq1", "s_y", "s_ty"))
        s_yt, s_zp, s_z, s_ag2, s_sq2 = (sem(n) for n in ("s_yt", "s_zp", "s_z", "s_ag2", "s_sq2"))
        s_nb2, s_o = sem("s_nb2"), sem("s_o")
        s_ph = sem("s_ph")
        s_gb = [sem(f"s_gb{k}") for k in range(2)]
        s_db = [sem(f"s_db{k}") for k in range(2)]
        s_xr = [sem(f"s_xr{k}") for k in range(2)]
        s_cl = [sem(f"s_cl{k}") for k in range(2)]
        s_st = [sem(f"s_st{k}") for k in range(2)]
        s_tr = sem("s_tr")
        s_zt = sem("s_zt")
        s_pj = sem("s_pj")
        s_sp = sem("s_sp")
        s_hb = sem("s_hb")
        s_he = sem("s_he")
        s_eq = sem("s_eq")
        s_cm = sem("s_cm")
        s_u = sem("s_u")
        s_ue = sem("s_ue")
        s_ad = sem("s_ad")
        s_sq = sem("s_sq")
        s_ag = sem("s_ag")
        s_cf = sem("s_cf")
        s_cp = sem("s_cp")
        s_ca = sem("s_ca")
        s_cs = sem("s_cs")
        s_cq = sem("s_cq")
        s_ce = sem("s_ce")
        s_g1 = sem("s_g1")
        s_aa = sem("s_aa")
        s_gv = sem("s_gv")
        s_sc = [sem(f"s_sc{j}") for j in range(SL)]
        s_sg = sem("s_sg")

        block = ctx.enter_context(nc.Block())

        def run(eng, its, per, lead, tail, body):
            for s in range(-lead, per):
                body(0, s)
            with eng.Fori(1, its - 1) as i:
                for s in range(per):
                    body(i, s)
            for s in range(per + tail):
                body(its - 1, s)

        def at(i, s, per, count):
            q = i * per + s
            if isinstance(i, int) and not 0 <= q < count:
                return None
            return i + s // per, s % per, q

        def sub(u, z, o):
            q = u * RING + z + o
            if isinstance(u, int) and not 0 <= q <= NSUB:
                return None
            return u + (z + o) // RING, (z + o) % RING, q

        def tiles(q):
            return 1 if isinstance(q, int) and q == NSUB else SUB

        def past(q, n):
            return not isinstance(q, int) or q >= n

        def prelude(eng, dense):
            for z in range(-2, RING):
                dense(0, z)
            for z in range(RING):
                dense(1, z)
            with eng.Fori(2, PRE_UNITS) as u:
                for z in range(RING):
                    dense(u, z)

        def rest(dense):
            for z in range(NSUB - UNITS * RING + 4):
                dense(UNITS, z)

        def group_of(s):
            z = s % GS
            k, g = z // 2, z % 2
            n = GT[g + 1] - GT[g]
            return k, g, GT[g], n, k * CT + GT[g]

        def three(a):
            return a.rearrange("p (a f) -> p a f", f=D)

        OFF_BV, OFF_B = 0, B * D
        OFF_DX = OFF_B + 3 * D
        BRW = OFF_DX + D

        def col(k):
            return EC[:, k * T:(k + 1) * T]

        def bc_mid(a, n):
            return a.unsqueeze(1).broadcast_to([a.shape[0], n, a.shape[1]])

        def bc_in(a, n):
            return a.unsqueeze(2).broadcast_to([a.shape[0], a.shape[1], n])

        def four(a):
            return a.rearrange("p (b f) -> p b f", f=D)

        val_s = sb("val_s", [P, SL], i32)
        s_bs1, s_bs2, s_rc1, s_rc2 = (sem(n) for n in ("s_bs1", "s_bs2", "s_rc1", "s_rc2"))
        s_vtick, s_atick = sem("s_vtick"), sem("s_atick")

        def bcast(a):
            return a.partition_broadcast(P)

        LOAD_LIST = [
            (Wemb[:, :], W_emb), (bemb[:, :], b_emb.rearrange("(k o) -> k o", o=1)),
            (four(bs[:, :]), bases.rearrange("l b k f -> k (l b) f")),
            (four(slf[:, :]), self_loop.rearrange("l k f -> k l f")),
            (bng[:, :], bcast(bn_gamma.rearrange("l f -> (l f)"))),
            (bnb[:, :], bcast(bn_beta.rearrange("l f -> (l f)"))),
            (bnm[:, :], bcast(bn_mean.rearrange("l f -> (l f)"))),
            (bnv[:, :], bcast(bn_var.rearrange("l f -> (l f)"))),
            (rt[:, :], root), (b1c[:, :], bias1.rearrange("(k o) -> k o", o=1)), (gw[:, :], gat_w),
            (four(bass_[:, :]), basis.rearrange("b i o -> i b o")),
            (gbb[:, :], bcast(gat_bias)),
            (attb[:, 0:D], bcast(att_src.rearrange("h d -> (h d)"))),
            (attb[:, D:2 * D], bcast(att_dst.rearrange("h d -> (h d)"))),
            (cmpb[:, :], bcast(comp.rearrange("r b -> (r b)"))),
            (wcb[:, :], bcast(w_coe.rearrange("l r b -> (l r b)"))),
        ]
        LOADS = len(LOAD_LIST)

        N_A, N_B = (0, 2, 4), (1, 3, 5)
        HB_N = dict(A1=1, B=(0, 2, 3), O=4)
        LD = dict(A=(0, 2, 4), B=(1, 3, 5, 8), S=6, W=7)
        ST = dict(A=(0, 3, 6), B=(2, 5, 8), S=9, W=10)
        J = (B, B, R)
        src_rows = (xs_d, hs_d, ys_d)
        src_next = (hs_d, ys_d, ls_d)
        table = (None, h_d, y_d, l_d)
        dst_rows = (xd_d, h_d, y_d)
        dst_next = (h_d, y_d, l_d)
        CH = IT * 2

        s_stick = sem("s_stick")
        s_cu = sem("s_cu")
        s_bd = sem("s_bd")
        s_mt = sem("s_mt")
        s_lc = sem("s_lc")

        def places(buf, widths):
            o, a = 0, []
            for w in widths:
                a.append(buf[0:T, o:o + w])
                o += w
            assert o <= buf.shape[1]
            return a

        SMX, TF, TB, pen, *DG = places(bass_, [H * P] * 3 + [P] + [H * T] * 2)
        PN0, PN1, PF0, PF1, CI0, CI1, CX0, CX1 = places(WW, [T] * 2 + [P] * 2 + [H] * 2 + [H * T] * 2)
        PN, PF, CI, CX = (PN0, PN1), (PF0, PF1), (CI0, CI1), (CX0, CX1)

        def counts_sp(sp):
            sp.wait_ge(s_fs, 64)
            phase(sp, load_db, lambda c: sp.wait_ge(s_eq, (c + 1) * CT), lambda c, k: None)
            sp.wait_ge(s_ce, CH)
            for k, p in enumerate((0, P - 1)):
                sp.dma_start(ce_d[k:k + 1].rearrange("o t r -> o (t r)"), CNT[p:p + 1, :]).then_inc(s_cs, 16)
            sp.wait_ge(s_cs, 32)
            for k in range(2):
                sp.dma_start(ct[:, k * R:(k + 1) * R], ce_d[k]).then_inc(s_cf, 16)
            sp.wait_ge(s_ca, 1)
            for k in range(2):
                sp.dma_start(cc_d[k], cti[:, k * R:(k + 1) * R]).then_inc(s_cs, 16)
            sp.wait_ge(s_cs, 64)
            sp.wait_ge(s_w1, 5)
            for k in range(2):
                sp.dma_start(CB[:, k * T * R:(k + 1) * T * R],
                             cc_d[k].rearrange("t r -> (t r)").partition_broadcast(P)).then_inc(s_cf, 16)

        def load_db(c, k):
            nc.sync.dma_start(DB[k], dstf_d[ds(c * CT * P, CT * P)].partition_broadcast(P)).then_inc(s_db[k], 16)

        def phase(sp, load, done, store, dense=None, unit=0, again=None, read=None, early=None):
            for k in range(2):
                if early:
                    early(k, k)
                load(k, k)

            def step(i, k):
                c = i * 2 + k
                more = not isinstance(i, int) or i < IT - 1
                if read and more:
                    read(c)
                    sp.sem_inc(s_stick, 1)
                    early(c + 2, k)
                if dense:
                    dense(unit + i, 2 * k)
                    if not again:
                        dense(unit + i, 2 * k + 1)
                done(c)
                sp.sem_inc(s_stick, 1)
                store(c, k)
                if again:
                    dense(unit + i, 2 * k + 1)
                    if more:
                        again(i, k)
                if more:
                    load(c + 2, k)

            if dense:
                for k in range(2):
                    step(0, k)
            with sp.Fori(1 if dense else 0, IT - 1) as i:
                for k in range(2):
                    step(i, k)
            for k in range(2):
                step(IT - 1, k)

        def edge_sp(sp, dense):
            def load_g(rows_d, c, k):
                a = k * CT * D
                sp.dma_start(three(G[:, a:a + CW]), chunk(rows_d, c)).then_inc(s_gb[k], 16)

            def carries(r, rows_d, w, to_d):
                v3 = rows_d.rearrange("(t e) f -> t e f", e=P)
                for k, e in enumerate((0, P - 1)):
                    sp.dma_start(UFL[:, k * w:(k + 1) * w], v3[:, e, :]).then_inc(s_cf, 16)
                sp.wait_ge(s_ca, r + 2)
                for k in range(2):
                    sp.dma_start(to_d[k], CIO[:, k * w:(k + 1) * w]).then_inc(s_cs, 16)
                if r < 3:
                    sp.dma_start(to_d[2], BR[0:T, OFF_B + r * D:OFF_B + (r + 1) * D]).then_inc(s_cs, 16)
                sp.wait_ge(s_cs, 64 + 48 * min(r + 1, 3) + (32 if r == 3 else 0))

            def stored(upto):
                for k in range(2):
                    sp.wait_ge(s_st[k], upto * IT * 16)

            for k in range(2):
                sp.wait_ge(s_pst[k], 2 * IT * 16)
            for r in range(3):
                def load_a(c, k):
                    load_db(c, k)
                    if r == 1:
                        sp.dma_start(three(XR[k]), chunk(xs_d, c)).then_inc(s_xr[k], 16)

                def done_a(c):
                    sp.wait_ge(s_ue, r * NG + (c + 1) * 2)
                    sp.sem_inc(s_stick, 1)
                    if r == 1:
                        sp.wait_ge(s_hb, HB_N["A1"] * T + (c + 1) * CT)
                    else:
                        sp.wait_ge(s_he, r * NG + (c + 1) * 2)

                def store_a(c, k):
                    sp.dma_start(chunk(u_d[r], c), three(UB[k][:, 0:CW])).then_inc(s_st[k], 16)
                    sp.dma_start(chunk(src_next[r], c), three(HB[k])).then_inc(s_st[k], 16)

                phase(sp, load_a, done_a, store_a, read=lambda c: sp.wait_ge(s_tr, N_A[r] * NG + (c + 1) * 2),
                      early=lambda c, k: load_g(src_rows[r], c, k))
                stored(ST["A"][r] + 2)
                carries(r, u_d[r], D, cr_d[r])

                def load_b(c, k):
                    load_g(dst_rows[r], c, k)
                    sp.dma_start(three(UB[k][:, 0:CW]), chunk(u_d[r], c)).then_inc(s_cl[k], 16)
                    sp.dma_start(FLc[k], fl_d[:, ds(c * CT * P, CT * P)]).then_inc(s_cl[k], 16)
                    sp.dma_start(three(CRc[k][:, 0:CW]), cr_d[r][:, ds(c * CT, CT), :]).then_inc(s_cl[k], 16)
                    if r == 1:
                        sp.dma_start(three(XR[k]), chunk(xd_d, c)).then_inc(s_xr[k], 16)

                phase(sp, load_b, lambda c: sp.wait_ge(s_hb, HB_N["B"][r] * T + (c + 1) * CT),
                      lambda c, k: sp.dma_start(chunk(dst_next[r], c), three(HB[k])).then_inc(s_st[k], 16),
                      dense, DU["B"][r])
                stored(ST["B"][r] + 1)

            def merged_stored(i, k):
                sp.wait_ge(s_st[k], (ST["S"] * IT + i + 1) * 16)
                sp.sem_inc(s_stick, 1)

            phase(sp, lambda c, k: load_g(ls_d, c, k), lambda c: sp.wait_ge(s_sg, c + 1),
                  lambda c, k: sp.dma_start(chunk(lm_d, c), three(G[:, k * CW:(k + 1) * CW])).then_inc(s_st[k], 16),
                  dense, DU["S"], merged_stored)
            rest(dense)
            stored(ST["S"] + 1)

            sp.wait_ge(s_aa, 2)

            def load_w(c, k):
                load_g(lm_d, c, k)
                load_db(c, k)

            phase(sp, load_w, lambda c: sp.wait_ge(s_ue, 3 * NG + (c + 1) * CT),
                  lambda c, k: sp.dma_start(chunk(ua_d, c), UB[k].rearrange("p (t f) -> p t f", f=UW)
                                            ).then_inc(s_st[k], 16))
            stored(ST["W"] + 1)
            carries(3, ua_d, UW, cra_d)

            def load_o(c, k):
                load_g(l_d, c, k)
                sp.dma_start(UB[k].rearrange("p (t f) -> p t f", f=UW), chunk(ua_d, c)).then_inc(s_cl[k], 16)
                sp.dma_start(FLc[k][0:2, :], fl_d[0:2, ds(c * CT * P, CT * P)]).then_inc(s_cl[k], 16)
                sp.dma_start(CRc[k][0:2, :].rearrange("p (t f) -> p t f", f=UW),
                             cra_d[:, ds(c * CT, CT), :]).then_inc(s_cl[k], 16)
                sp.dma_start(three(XR[k]), chunk(y_d, c)).then_inc(s_xr[k], 16)

            for z in range(RING):
                sp.wait_ge(s_os[z], len(range(z, NSUB + 1, RING)) * 16)
            phase(sp, load_o, lambda c: sp.wait_ge(s_hb, HB_N["O"] * T + (c + 1) * CT), lambda c, k: None)

        def edge_pool(g, node_bound, slot_bound, gate):
            for n, (tab, ld) in enumerate(((h_d, LD["A"][1]), (y_d, LD["A"][2]), (l_d, LD["S"]))):
                with g.Fori(0, IT) as i:
                    for k in range(2):
                        a = k * CT
                        gate(s_gb[k], (ld * IT + i + 1) * 16)
                        for j in range(a, a + CT):
                            gate(s_ga[j], ((4 + n) * IT + i) * 16)
                        g.tensor_copy(idx_s[:, a:a + CT], slot_i[:, ds(i * SL + a, CT)]).then_inc(s_ik, 1)
                        gate(s_ik, 7 * IT + n * 2 * IT + i * 2 + k + 1)
                        for j in range(a, a + CT):
                            g.indirect_dma_start(
                                out=G[:, j * D:(j + 1) * D], out_offset=None, in_=tab,
                                in_offset=bass.IndirectOffsetOnAxis(ap=idx_s[:, j:j + 1], axis=0),
                                bounds_check=slot_bound, oob_is_err=False).then_inc(s_ga[j], 16)
            for j in range(SL):
                g.wait_ge(s_ga[j], 7 * IT * 16)
            def scatter(i, k):
                a = k * CT
                if not isinstance(i, int):
                    for j in range(a, a + CT):
                        gate(s_sc[j], i * 16)
                g.tensor_copy(idx_s[:, a:a + CT], lead_i[:, ds(i * SL + a, CT)]).then_inc(s_ik, 1)
                gate(s_ik, 13 * IT + i * 2 + k + 1)
                for j in range(a, a + CT):
                    gate(s_hb, HB_N["O"] * T + i * SL + j + 1)
                    g.indirect_dma_start(
                        out=out, out_offset=bass.IndirectOffsetOnAxis(ap=idx_s[:, j:j + 1], axis=0),
                        in_=HB[k][:, (j - a) * D:(j - a + 1) * D], in_offset=None,
                        bounds_check=node_bound, oob_is_err=False).then_inc(s_sc[j], 16)

            for k in range(2):
                scatter(0, k)
            with g.Fori(1, IT) as i:
                for k in range(2):
                    scatter(i, k)
            for j in range(SL):
                g.wait_ge(s_sc[j], IT * 16)

        def carries_pe(pe, r, ufl, w, bank):
            pe.wait_ge(s_cf, 32 if r < 0 else 96 + 32 * r)
            nc.tensor.matmul(bank[0:T, 0:w], mk_in[:, :], ufl[:, w:2 * w], start=True, stop=True)
            nc.tensor.matmul(bank[0:T, w:2 * w], mk_out[:, :], ufl[:, 0:w], start=True, stop=True).then_inc(s_cp, 1)

        def relation_weights(pe):
            pe.wait_ge(s_wr, NB * R)
            for r in range(R):
                last = nc.tensor.transpose(BK[r // 4][:, (r % 4) * D:(r % 4 + 1) * D],
                                           Wr[:, r * D:(r + 1) * D], ident[:, :])
            last.then_inc(s_w1, 1)
            pe.wait_ge(s_wa, 4)
            for r in range(R):
                last = nc.tensor.matmul(BK[2 + r // 4][:, (r % 4) * D:(r % 4 + 1) * D],
                                        WrT[:, r * D:(r + 1) * D], gw[:, :], start=True, stop=True)
            last.then_inc(s_w1, 1)
            pe.wait_ge(s_wa, 6)

        def edge_counts(pe):

            def count(i, s):
                if (a := at(i, s, SL, T)):
                    it, z, q = a
                    k, j = z // CT, z % CT
                    pe.wait_ge(s_eq, q + 1)
                    if j == 0 and (not isinstance(it, int) or it >= 1):
                        pe.wait_ge(s_ce, it * 2 + k - 1)
                    m = nc.tensor.matmul(BK[2 + k][:, j * R:(j + 1) * R], EQ[z % 2][:, :], OH[:, ds(q * R, R)],
                                         start=True, stop=True).then_inc(s_cu, 1)

            run(pe, IT, SL, 0, 0, count)

            pe.wait_ge(s_mk, 1)
            carries_pe(pe, -1, ct, R, BK[6])

        def edge_pe(pe, dense, rows):
            def dense_read(u):
                pe.wait_ge(s_yt, u * RING - 1)
                pe.wait_ge(s_ht, u * RING + 1)
                pe.wait_ge(s_pre, u * RING)
                pe.wait_ge(s_z, u * RING - 2)

            def transpose(n, i, s, loaded):
                if not (a := at(i, s, GS, NG)):
                    return
                it, z, q = a
                k, g, j0, w, z0 = group_of(z)
                loaded(it, k, g, z0, w)
                if past(q, 2):
                    pe.wait_ge(s_zt, n * NG + q - 1)
                for t in range(w):
                    last = nc.tensor.transpose(BK[g][:, t * D:(t + 1) * D], G[:, (z0 + t) * D:(z0 + t + 1) * D], ident[:, :])
                last.then_inc(s_tr, 1)

            for r in range(3):
                dense_read(DU["B"][r])

                def loaded_a(it, k, g, z0, w):
                    if r > 0:
                        for t in range(z0, z0 + w):
                            pe.wait_ge(s_ga[t], ((3 + r) * IT + it + 1) * 16)
                    elif g == 0:
                        pe.wait_ge(s_gb[k], (LD["A"][0] * IT + it + 1) * 16)

                def a_phase(i, s):
                    if s == -1:
                        return transpose(N_A[r], i, 0, loaded_a)
                    if (a := at(i, s, SL, T)):
                        it, z, q = a
                        k, j = z // CT, z % CT
                        gs = 2 * k + (j >= GT[1])
                        _, g, j0, w, _ = group_of(gs)
                        qg = it * GS + gs
                        zt = ZT[g][:, (j - j0) * D:(j - j0 + 1) * D]
                        if j == j0:
                            transpose(N_A[r], i, gs + 1, loaded_a)
                            pe.wait_ge(s_zt, N_A[r] * NG + qg + 1)
                        nb = J[r] // 4
                        if past(q, 2):
                            pe.wait_ge(s_cm, sum(J[:r]) * T + (q - 1) * J[r])
                        for h in range(nb):
                            bank = BK[2 + z % 2] if nb == 1 else BK[2 + 2 * (z % 2) + h]
                            last = nc.tensor.matmul(bank[:, :], zt, V[r][:, h * 4 * D:(h + 1) * 4 * D],
                                                    start=True, stop=r > 0)
                            if r == 0:
                                last = nc.tensor.matmul(bank[:, :], ones3[:, :], B3[:, OFF_BV:OFF_BV + B * D],
                                                        start=False, stop=True)
                        last.then_inc(s_pj, 1)
                        if j == j0:
                            pe.wait_ge(s_he, r * NG + qg)
                            rows(BK[6], w, OFF_B + r * D, ZT[g], M[r]).then_inc(s_sp, 1)
                    if (a := at(i, s - 1, SL, T)):
                        it, z, q = a
                        k, j = z // CT, z % CT
                        gs = 2 * k + (j >= GT[1])
                        _, g, j0, w, _ = group_of(gs)
                        pe.wait_ge(s_cm, sum(J[:r]) * T + (q + 1) * J[r])
                        if j == j0:
                            pe.wait_ge(s_ue, r * NG + it * GS + gs)
                        u = BK[7][:, (j - j0) * D:(j - j0 + 1) * D]
                        nc.tensor.matmul(u, EQ[z % 2][:, :], MS[z % 2][:, 0:D], start=True, stop=False)
                        nc.tensor.matmul(u, EQ[z % 2][:, :], MT[z % 2][:, :], start=False, stop=True).then_inc(s_u, 1)

                run(pe, IT, SL, 1, 1, a_phase)
                carries_pe(pe, r, UFL, D, BK[4])

                def loaded_b(it, k, g, z0, w):
                    if g == 0:
                        pe.wait_ge(s_gb[k], (LD["B"][r] * IT + it + 1) * 16)

                def b_phase(i, s):
                    transpose(N_B[r], i, s + 1, loaded_b)
                    if (a := at(i, s, GS, NG)):
                        it, z, q = a
                        k, g, j0, w, _ = group_of(z)
                        pe.wait_ge(s_zt, N_B[r] * NG + q + 1)
                        if g == 0:
                            pe.wait_ge(s_cl[k], (r * IT + it + 1) * 48)
                        if past(q, 2):
                            pe.wait_ge(s_ad, r * NG + q - 1)
                        for t in range(w):
                            j, o = j0 + t, BK[2 + g][:, t * D:(t + 1) * D]
                            nc.tensor.matmul(o, ZT[g][:, t * D:(t + 1) * D], M[r][:, :], start=True, stop=False)
                            last = nc.tensor.matmul(o, FLc[k][:, j * P:(j + 1) * P], CRc[k][:, j * D:(j + 1) * D],
                                                    start=False, stop=True)
                        last.then_inc(s_bd, 1)
                        dense(DU["B"][r] + it, z)

                run(pe, IT, GS, 1, 0, b_phase)

            dense_alone(pe, dense)
            rest(dense)
            for done in (s_yt, s_ht, s_pre, s_z):
                pe.wait_ge(done, NSUB + 1)

            pe.wait_ge(s_gv, 1)
            for h in range(H):
                last = nc.tensor.transpose(BK[4][0:T, h * P:(h + 1) * P], AS[:, h * T:(h + 1) * T], ident[:, :])
            nc.tensor.transpose(BK[7][0:T, 0:T], mk_in[:, :], ident[0:T, 0:T])
            nc.tensor.transpose(BK[7][0:T, T:2 * T], mk_out[:, :], ident[0:T, 0:T]).then_inc(s_g1, 1)
            pe.wait_ge(s_gv, 2)
            for k in range(2):
                last = nc.tensor.matmul(BK[5 + k][0:T, 0:H * T], ones[0:T, 0:T], DG[k], start=True, stop=True)
            last.then_inc(s_g1, 1)
            pe.wait_ge(s_gv, 3)
            for h in range(H):
                last = nc.tensor.transpose(BK[3][:, h * T:(h + 1) * T], SMX[:, h * P:(h + 1) * P], ident[0:T, 0:T])
            last.then_inc(s_g1, 1)

            def w_phase(i, s):
                if (a := at(i, s, SL, T)):
                    it, z, q = a
                    pe.wait_ge(s_mt, q + 1)
                    if not isinstance(q, int) or q >= 2:
                        pe.wait_ge(s_ue, 3 * NG + q - 1)
                    nc.tensor.matmul(BK[6 + z % 2][:, 0:UW], EQ[z % 2][:, :], MS[z % 2][:, :],
                                     start=True, stop=True).then_inc(s_u, 1)

            run(pe, IT, SL, 0, 0, w_phase)
            carries_pe(pe, 3, UFL, UW, BK[4])

            def o_phase(i, s):
                if (a := at(i, s, SL, T)):
                    it, z, q = a
                    k, j = z // CT, z % CT
                    if j == 0:
                        pe.wait_ge(s_cl[k], (3 * IT + it + 1) * 48)
                    if not isinstance(q, int) or q >= 2:
                        pe.wait_ge(s_ad, 3 * NG + q - 1)
                    nc.tensor.matmul(BK[2 + z % 2][:, 0:UW], FLc[k][0:2, j * P:(j + 1) * P],
                                     CRc[k][0:2, j * UW:(j + 1) * UW], start=True, stop=True).then_inc(s_bd, 1)

            run(pe, IT, SL, 0, 0, o_phase)

        def carries_act(act, r, bank, w, to):
            act.wait_ge(s_cp, r + 2)
            nc.scalar.copy(to[:, 0:2 * w], bank[0:T, 0:2 * w]).then_inc(s_ca, 1)

        def edge_counts_act(act):
            act.wait_ge(s_w1, 4)
            for k in range(2):
                nc.scalar.copy(WrT[:, k * 4 * D:(k + 1) * 4 * D], BK[k][:, :]).then_inc(s_wa, 1)
            act.wait_ge(s_w1, 5)
            for k in range(2):
                nc.scalar.copy(V[2][:, k * 4 * D:(k + 1) * 4 * D], BK[2 + k][:, :]).then_inc(s_wa, 1)

            with act.Fori(0, IT) as i:
                for k in range(2):
                    act.wait_ge(s_cu, (i * 2 + k + 1) * CT)
                    act.sem_inc(s_atick, 1)
                    nc.scalar.copy(CNT[:, ds((i * 2 + k) * CT * R, CT * R)], BK[2 + k][:, 0:CT * R]).then_inc(s_ce, 1)

            carries_act(act, -1, BK[6], R, cti)

        def edge_act(act, dense):

            def transposed(n, i, s):
                if (a := at(i, s, GS, NG)):
                    _, z, q = a
                    _, g, _, w, _ = group_of(z)
                    act.wait_ge(s_tr, n * NG + q + 1)
                    nc.scalar.copy(ZT[g][:, 0:w * D], BK[g][:, 0:w * D]).then_inc(s_zt, 1)

            def deviation(n, z):
                k = z // CT
                act.wait_ge(s_ag, n)
                nc.scalar.activation(sd[:, k * CT:(k + 1) * CT], mv[:, 2 * k * CT + 1:2 * (k + 1) * CT:2],
                                     ACT.Sqrt, bias=eps[:, 0:1]).then_inc(s_sq, 1)

            def out_free(it, k, count, before):
                if not isinstance(it, int) or it >= 1:
                    act.wait_ge(s_st[k], (before * IT + count * it) * 16)

            for r in range(3):
                def a_phase(i, s):
                    if s == -1:
                        return transposed(N_A[r], i, 0)
                    if (a := at(i, s, SL, T)):
                        it, z, q = a
                        k, j = z // CT, z % CT
                        if j in GT:
                            gs = 2 * k + (j >= GT[1])
                            _, g, j0, w, _ = group_of(gs)
                            transposed(N_A[r], i, gs + 1)
                            if r != 1:
                                act.wait_ge(s_sp, r * NG + it * GS + gs + 1)
                                if j == 0:
                                    out_free(it, k, 2, ST["A"][r])
                                nc.scalar.activation(HB[k][:, j * D:(j + w) * D], BK[6][:, 0:w * D],
                                                     ACT.Relu if r == 0 else ACT.Copy).then_inc(s_he, 1)
                    if (a := at(i, s - 1, SL, T)) and a[1] % CT + 1 in GT:
                        it, z, q = a
                        k, j = z // CT, z % CT
                        _, g, j0, w, _ = group_of(2 * k + (j >= GT[1]))
                        act.wait_ge(s_u, r * T + q + 1)
                        if g == 0:
                            out_free(it, k, 2, ST["A"][r])
                        nc.scalar.copy(UB[k][:, j0 * D:(j0 + w) * D], BK[7][:, 0:w * D]).then_inc(s_ue, 1)
                    if r == 1 and (a := at(i, s, SL, T)) and a[1] % CT == CT - 1:
                        deviation(a[0] * 2 + a[1] // CT + 1, a[1])

                run(act, IT, SL, 1, 1, a_phase)
                carries_act(act, r, BK[4], D, CIO)

                def b_phase(i, s):
                    if r == 0 and (a := at(i, s - 1, GS, NG)):
                        it, z, q = a
                        k, g, j0, w, _ = group_of(z)
                        act.wait_ge(s_ad, q + 1)
                        h = HB[k][:, j0 * D:(j0 + w) * D]
                        nc.scalar.activation(h, h, ACT.Relu).then_inc(s_hb, w)
                    transposed(N_B[r], i, s + 1)
                    if (a := at(i, s, GS, NG)):
                        it, z, q = a
                        if r == 1 and z % 2 == 1:
                            deviation(CH + it * 2 + z // 2 + 1, (z // 2) * CT)
                        dense(DU["B"][r] + it, z)

                run(act, IT, GS, 1, 1, b_phase)

            dense_alone(act, dense)
            rest(dense)

            act.wait_ge(s_g1, 1)
            nc.scalar.copy(SMX, BK[4][0:T, :]).then_inc(s_aa, 1)
            act.wait_ge(s_gv, 4)
            nc.scalar.activation(EA[:, :], EA[:, :], ACT.Exp)
            nc.scalar.activation(ES[:, :], ES[:, :], ACT.Exp).then_inc(s_aa, 1)

            def w_phase(i, s):
                if (a := at(i, s, SL, T)):
                    it, z, q = a
                    k, j = z // CT, z % CT
                    act.wait_ge(s_u, 3 * T + q + 1)
                    if j == 0:
                        out_free(it, k, 1, ST["W"])
                    nc.scalar.copy(UB[k][:, j * UW:(j + 1) * UW], BK[6 + z % 2][:, 0:UW]).then_inc(s_ue, 1)

            run(act, IT, SL, 0, 0, w_phase)
            carries_act(act, 3, BK[4], UW, CIO)

            def o_phase(i, s):
                if (a := at(i, s, SL, T)) and a[1] % CT == CT - 1:
                    deviation(2 * CH + a[0] * 2 + a[1] // CT + 1, a[1])

            run(act, IT, SL, 0, 0, o_phase)

        class LoopChain:

            def __init__(self, v):
                self.v, self.base, self.n, self.per = v, 0, 0, 0

            def loop(self, per):
                self.base += self.per * IT
                self.per = per

            def start(self, i, s):
                if s == 0:
                    self.i, self.n = i, 0

            def __call__(self, ins):
                self.n += 1
                assert self.n <= self.per
                ins.then_inc(s_lc, 1)
                self.v.wait_ge(s_lc, self.i * self.per + self.base + self.n)

        def dense_alone(eng, dense):
            with eng.Fori(0, IT - 1) as i:
                for z in range(RING):
                    dense(DU["S"] + i, z)
            for z in range(RING):
                dense(UNITS - 1, z)

        def equal(v, n, a, done):
            it, z, q = a
            k, j = z // CT, z % CT
            if j == 0:
                v.wait_ge(s_db[k], (n * IT + it + 1) * 16)
            if not isinstance(q, int) or q >= 2:
                v.wait_ge(*done(q))
            nc.vector.tensor_scalar(EQ[z % 2][:, :], DB[k][:, j * P:(j + 1) * P], EC[:, ds(q, 1)], None,
                                    ALU.is_equal).then_inc(s_eq, 1)

        def counts_dve(v, link):
            for b in range(NB):
                for r in range(R):
                    o = Wr[:, r * D:(r + 1) * D]
                    if b:
                        v.wait_ge(s_wr, (b - 1) * R + r + 1)
                        nc.vector.scalar_tensor_tensor(
                            out=o, in0=bass_[:, b * D:(b + 1) * D], scalar=cmpb[:, r * NB + b:r * NB + b + 1],
                            in1=o, op0=ALU.mult, op1=ALU.add).then_inc(s_wr, 1)
                    else:
                        nc.vector.tensor_scalar(o, bass_[:, 0:D], cmpb[:, r * NB:r * NB + 1], None,
                                                ALU.mult).then_inc(s_wr, 1)

            run(v, IT, SL, 0, 0, lambda i, s: equal(v, 0, at(i, s, SL, T), lambda q: (s_cu, q - 1)))

            v.wait_ge(s_cf, 64)
            q13, cnt3, oh3 = (a[:, :].rearrange("p (t r) -> p t r", r=R) for a in (q1, CNT, OH))
            q23 = q2[:, :].rearrange("p (t r) -> p t r", r=R)
            for k in range(2):
                link(nc.vector.tensor_tensor(q13, CB[:, k * T * R:(k + 1) * T * R].rearrange("p (t r) -> p t r", r=R),
                                             bc_in(eqc[:, k * T:(k + 1) * T], R), ALU.mult))
                link(nc.vector.tensor_tensor(CNT[:, :], CNT[:, :], q1[:, :], ALU.add))
            link(nc.vector.tensor_scalar(q1[:, :], CNT[:, :], 1.0, None, ALU.max))
            link(nc.vector.reciprocal(q1[:, :], q1[:, :]))
            nc.vector.memset(nz[:, :], 1.0)
            link(nc.vector.memset(nrm[:, :], 0.0))
            for r in reversed(range(R)):
                link(nc.vector.scalar_tensor_tensor(out=wq[:, :], in0=cnt3[:, :, r], scalar=0.0, in1=nz[:, :],
                                                    op0=ALU.is_gt, op1=ALU.mult))
                nc.vector.tensor_tensor(nz[:, :], nz[:, :], wq[:, :], ALU.subtract)
                link(nc.vector.tensor_tensor(q2[:, 0:T], wq[:, :], q13[:, :, r], ALU.mult))
                link(nc.vector.tensor_tensor(nrm[:, :], nrm[:, :], q2[:, 0:T], ALU.add))
            for l in range(2):
                for b in range(B):
                    w = wcb[:, l * R * B:(l + 1) * R * B].rearrange("p (r b) -> p r b", b=B)[:, :, b]
                    link(nc.vector.tensor_tensor(q23, oh3, bc_mid(w, T), ALU.mult))
                    link(nc.vector.tensor_reduce(wq[:, :], q23, AX.X, ALU.add))
                    link(nc.vector.tensor_tensor(C[l][:, :].rearrange("p (t b) -> p t b", b=B)[:, :, b],
                                                 wq[:, :], nrm[:, :], ALU.mult))
            link(nc.vector.tensor_tensor(C[2][:, :], OH[:, :], q1[:, :], ALU.mult))

        def edge_dve(v, link, dense):
            lc = LoopChain(v)

            def norm_chunk(z, n, rows_):
                k = z // CT
                for t in range(CT):
                    o = k * CT + t
                    last = nc.vector.bn_stats(st[:, 6 * o:6 * o + 6], rows_[:, t * D:(t + 1) * D])
                lc(last)
                v.sem_inc(s_vtick, 1)
                for t in range(CT):
                    o = k * CT + t
                    last = nc.vector.bn_aggr(mv[:, 2 * o:2 * o + 2], st[:, 6 * o:6 * o + 6])
                last.then_inc(s_ag, 1)
                v.wait_ge(s_sq, n)
                lc(nc.vector.reciprocal(rs[:, k * CT:(k + 1) * CT], sd[:, k * CT:(k + 1) * CT]))
                for t in range(CT):
                    o = k * CT + t
                    w = rows_[:, t * D:(t + 1) * D]
                    nc.vector.tensor_scalar(w, w, mv[:, 2 * o:2 * o + 1], rs[:, o:o + 1], ALU.subtract,
                                            ALU.mult).then_inc(s_hb, 1)

            def scores(rows_, m, c, k, to):
                lc(nc.vector.tensor_tensor(three(W1[:, 0:CW]), three(rows_), bc_mid(attb[:, m * D:(m + 1) * D], CT),
                                           ALU.mult))
                rd = red[k][:, m * CT * H:(m + 1) * CT * H]
                lc(nc.vector.tensor_reduce(rd, W1[:, 0:CW].rearrange("p (a d) -> p a d", d=HD), AX.X, ALU.add))
                return nc.vector.tensor_scalar(to.rearrange("p (h t) -> p t h", t=T)[:, ds(c * CT, CT), :],
                                               rd.rearrange("p (t h) -> p t h", h=H), 1.0, None, ALU.mult)

            def out_free(it, k, count, before):
                if not isinstance(it, int) or it >= 1:
                    v.wait_ge(s_st[k], (before * IT + count * it) * 16)

            for r in range(3):
                lc.loop(4 if r == 1 else 0)

                def a_phase(i, s):
                    if r == 1:
                        lc.start(i, s)
                    a = at(i, s, SL, T)
                    it, z, q = a
                    k, j = z // CT, z % CT
                    equal(v, 1 + r, a, lambda q: (s_u, r * T + q - 1))
                    v.wait_ge(s_pj, r * T + q + 1)
                    n = J[r]
                    for m in range(n):
                        b = m % 2 * (n // 2) + m // 2
                        o = (MS, MT)[m % 2][z % 2][:, 0:D]
                        bank = BK[2 + z % 2] if n == 4 else BK[2 + 2 * (z % 2) + b // 4]
                        pj = bank[:, (b % 4) * D:(b % 4 + 1) * D]
                        c = C[r][:, ds(q * n + b, 1)]
                        if m < 2:
                            nc.vector.tensor_scalar(o, pj, c, None, ALU.mult).then_inc(s_cm, 1)
                        else:
                            v.wait_ge(s_cm, sum(J[:r]) * T + q * n + m - 1)
                            nc.vector.scalar_tensor_tensor(out=o, in0=pj, scalar=c, in1=o, op0=ALU.mult,
                                                           op1=ALU.add).then_inc(s_cm, 1)
                    if r == 1:
                        if j in GT:
                            gs = 2 * k + (j >= GT[1])
                            _, g, _, w, _ = group_of(gs)
                            v.wait_ge(s_sp, r * NG + it * GS + gs + 1)
                            if j == 0:
                                v.wait_ge(s_xr[k], (it + 1) * 16)
                                out_free(it, k, 2, ST["A"][r])
                            nc.vector.scalar_tensor_tensor(
                                out=HB[k][:, j * D:(j + w) * D], in0=BK[6][:, 0:w * D], scalar=0.0,
                                in1=XR[k][:, j * D:(j + w) * D], op0=ALU.max, op1=ALU.add).then_inc(s_he, 1)
                        if j == CT - 1:
                            v.wait_ge(s_he, r * NG + it * GS + 2 * k + 2)
                            norm_chunk(z, it * 2 + k + 1, HB[k])

                run(v, IT, SL, 0, 0, a_phase)
                lc.loop((0, 6, 8)[r])

                def b_phase(i, s):
                    if r:
                        lc.start(i, s)
                    it, z, q = at(i, s, GS, NG)
                    k, g, j0, w, _ = group_of(z)
                    v.wait_ge(s_bd, r * NG + q + 1)
                    if g == 0:
                        v.wait_ge(s_cl[k], (r * IT + it + 1) * 48)
                        out_free(it, k, 1, ST["B"][r])
                    nc.vector.tensor_tensor(HB[k][:, j0 * D:(j0 + w) * D], BK[2 + g][:, 0:w * D],
                                            UB[k][:, j0 * D:(j0 + w) * D], ALU.add).then_inc(s_ad, 1)
                    if g == 1 and r == 1:
                        v.wait_ge(s_ad, r * NG + q + 1)
                        v.wait_ge(s_xr[k], (IT + it + 1) * 16)
                        lc(nc.vector.scalar_tensor_tensor(out=HB[k], in0=HB[k], scalar=0.0, in1=XR[k],
                                                          op0=ALU.max, op1=ALU.add))
                        norm_chunk(k * CT, CH + it * 2 + k + 1, HB[k])
                    if g == 1 and r == 2:
                        v.wait_ge(s_ad, r * NG + q + 1)
                        scores(HB[k], 0, it * 2 + k, k, AD[:, 0:H * T])
                        scores(HB[k], 1, it * 2 + k, k, AD[:, H * T:2 * H * T]).then_inc(s_hb, CT)
                    dense(DU["B"][r] + it, z)

                run(v, IT, GS, 0, 0, b_phase)

            lc.loop(4)

            def s_phase(i, k):
                if k == 0:
                    lc.start(i, 0)
                dense(DU["S"] + i, 2 * k)
                for j in range(k * CT, (k + 1) * CT):
                    v.wait_ge(s_ga[j], (6 * IT + i + 1) * 16)
                scores(G[:, k * CW:(k + 1) * CW], 0, i * 2 + k, k, AS[:, :]).then_inc(s_sg, 1)
                dense(DU["S"] + i, 2 * k + 1)

            with v.Fori(0, IT - 1) as i:
                for k in range(2):
                    s_phase(i, k)
            for k in range(2):
                s_phase(IT - 1, k)
            rest(dense)

            hT3 = lambda a: a.rearrange("p (h t) -> p h t", t=T)
            v.wait_ge(s_sg, CH)
            link(nc.vector.tensor_tensor(ES[:, :], AD[:, 0:H * T], AD[:, H * T:2 * H * T], ALU.add))
            link(nc.vector.scalar_tensor_tensor(out=ES[:, :], in0=ES[:, :], scalar=SLOPE, in1=ES[:, :],
                                                op0=ALU.mult, op1=ALU.max))
            link(nc.vector.tensor_tensor(AS[:, :], AS[:, :], AD[:, H * T:2 * H * T], ALU.add))
            nc.vector.tensor_tensor(wq[:, :], col(0), col(1), ALU.is_equal)
            link(nc.vector.scalar_tensor_tensor(out=AS[:, :], in0=AS[:, :], scalar=SLOPE, in1=AS[:, :],
                                                op0=ALU.mult, op1=ALU.max))
            nc.vector.scalar_tensor_tensor(out=hT3(AS[:, :]), in0=bc_mid(wq[:, :], H), scalar=NEG, in1=hT3(AS[:, :]),
                                           op0=ALU.mult, op1=ALU.add).then_inc(s_gv, 1)
            v.wait_ge(s_aa, 1)
            v.wait_ge(s_st[0], (ST["S"] + 1) * IT * 16)
            v.wait_ge(s_st[1], (ST["S"] + 1) * IT * 16)
            m3, f3, b3 = (a.rearrange("t (h e) -> t h e", e=P) for a in (SMX, TF, TB))
            d = 1
            while d < P:
                w = P - d
                link(nc.vector.tensor_tensor(pen[:, 0:w], ef[:, d:P], ef[:, 0:w], ALU.not_equal))
                link(nc.vector.tensor_scalar(pen[:, 0:w], pen[:, 0:w], NEG, None, ALU.mult))
                nc.vector.tensor_tensor(f3[:, :, 0:w], m3[:, :, 0:w], bc_mid(pen[:, 0:w], H), ALU.add)
                link(nc.vector.tensor_tensor(b3[:, :, 0:w], m3[:, :, d:P], bc_mid(pen[:, 0:w], H), ALU.add))
                link(nc.vector.tensor_tensor(m3[:, :, d:P], m3[:, :, d:P], f3[:, :, 0:w], ALU.max))
                link(nc.vector.tensor_tensor(m3[:, :, 0:w], m3[:, :, 0:w], b3[:, :, 0:w], ALU.max))
                d *= 2
            for k, e in enumerate((P - 1, 0)):
                nc.vector.tensor_scalar(PN[k], BK[7][0:T, k * T:(k + 1) * T], 1.0, -NEG, ALU.subtract, ALU.mult)
                nc.vector.tensor_scalar(PF[k], fle[:, k * P:(k + 1) * P], 1.0, -NEG, ALU.subtract, ALU.mult)
                last = nc.vector.tensor_tensor(hT3(DG[k]), bc_mid(ident[0:T, 0:T], H), bc_in(m3[:, :, e], T), ALU.mult)
            last.then_inc(s_gv, 1)
            v.wait_ge(s_g1, 2)
            for k in range(2):
                link(nc.vector.tensor_tensor(hT3(CX[k]), hT3(BK[5 + k][0:T, 0:H * T]), bc_mid(PN[k], H), ALU.add))
                link(nc.vector.tensor_reduce(CI[k], hT3(CX[k]), AX.X, ALU.max))
                link(nc.vector.tensor_tensor(f3, bc_in(CI[k], P), bc_mid(PF[k], H), ALU.add))
                last = nc.vector.tensor_tensor(m3, m3, f3, ALU.max)
                if k == 0:
                    link(last)
            last.then_inc(s_gv, 1)
            v.wait_ge(s_g1, 3)
            link(nc.vector.tensor_tensor(MX[:, :], BK[3][:, 0:H * T], ES[:, :], ALU.max))
            nc.vector.tensor_tensor(EA[:, :], AS[:, :], MX[:, :], ALU.subtract)
            nc.vector.tensor_tensor(ES[:, :], ES[:, :], MX[:, :], ALU.subtract).then_inc(s_gv, 1)
            v.wait_ge(s_aa, 2)

            def w_phase(i, s):
                a = at(i, s, SL, T)
                it, z, q = a
                k, j = z // CT, z % CT
                equal(v, 4, a, lambda q: (s_u, 3 * T + q - 1))
                if j == 0:
                    v.wait_ge(s_gb[k], (LD["W"] * IT + it + 1) * 16)
                e = hT3(EA[:, :])[:, :, ds(q, 1)]
                nc.vector.tensor_tensor(MS[z % 2][:, 0:D].rearrange("p (h d) -> p h d", d=HD),
                                        G[:, z * D:(z + 1) * D].rearrange("p (h d) -> p h d", d=HD),
                                        e.broadcast_to([P, H, HD]), ALU.mult)
                nc.vector.tensor_scalar(MS[z % 2][:, D:UW].unsqueeze(2), e, 1.0, None, ALU.mult).then_inc(s_mt, 1)

            run(v, IT, SL, 0, 0, w_phase)
            lc.loop(14)

            def o_phase(i, s):
                lc.start(i, s)
                it, z, q = at(i, s, SL, T)
                k, j = z // CT, z % CT
                v.wait_ge(s_bd, 3 * NG + q + 1)
                if j == 0:
                    v.wait_ge(s_cl[k], (3 * IT + it + 1) * 48)
                u = UB[k][:, j * UW:(j + 1) * UW]
                nc.vector.tensor_tensor(u, BK[2 + z % 2][:, 0:UW], u, ALU.add).then_inc(s_ad, 1)
                if j < CT - 1:
                    return
                c = it * 2 + k
                v.wait_ge(s_gb[k], (LD["B"][3] * IT + it + 1) * 16)
                v.wait_ge(s_xr[k], (2 * IT + it + 1) * 16)
                if not isinstance(it, int) or it >= 1:
                    for t in range(k * CT, (k + 1) * CT):
                        v.wait_ge(s_sc[t], it * 16)
                u3 = UB[k].rearrange("p (t f) -> p t f", f=UW)
                h3 = HB[k].rearrange("p (a d) -> p a d", d=HD)
                es = ES[:, :].rearrange("p (h t) -> p t h", t=T)[:, ds(c * CT, CT), :]
                rd = red[k][:, 0:CT * H]
                v.wait_ge(s_ad, 3 * NG + q + 1)
                nc.vector.tensor_tensor(rd.rearrange("p (t h) -> p t h", h=H), u3[:, :, D:UW], es, ALU.add)
                lc(nc.vector.tensor_tensor(
                    HB[k].rearrange("p (t h d) -> p t h d", h=H, d=HD),
                    G[:, k * CW:(k + 1) * CW].rearrange("p (t h d) -> p t h d", h=H, d=HD),
                    es.unsqueeze(3).broadcast_to([P, CT, H, HD]), ALU.mult))
                nc.vector.reciprocal(rd, rd)
                lc(nc.vector.tensor_tensor(three(HB[k]), three(HB[k]), u3[:, :, 0:D], ALU.add))
                lc(nc.vector.tensor_tensor(h3, h3, bc_in(rd, HD), ALU.mult))
                lc(nc.vector.tensor_tensor(three(HB[k]), three(HB[k]), bc_mid(gbb[:, :], CT), ALU.add))
                lc(nc.vector.tensor_tensor(HB[k], HB[k], XR[k], ALU.add))
                norm_chunk(z, 2 * CH + it * 2 + k + 1, HB[k])

            run(v, IT, SL, 0, 0, o_phase)
            assert lc.n == 14

        LE = T * P - P

        @block.sync
        def _(sp):
            sp.wait_ge(s_ms, 1)
            for k, a in enumerate((dst, src, etype)):
                sp.dma_start(ei[0:T - 1, k * P:(k + 1) * P],
                             a[0:LE].rearrange("(t e) -> t e", e=P)).then_inc(s_le, 16)
                sp.dma_start(ei[T - 1:T, k * P:k * P + TAIL], a[LE:E].unsqueeze(0)).then_inc(s_le, 16)
            sp.dma_start(ei[0:1, 3 * P + 1:4 * P], dst[0:P - 1].unsqueeze(0)).then_inc(s_le, 16)
            sp.dma_start(ei[1:T - 1, 3 * P:4 * P],
                         dst[P - 1:LE - 1].rearrange("(t e) -> t e", e=P)).then_inc(s_le, 16)
            sp.dma_start(ei[T - 1:T, 3 * P:3 * P + TAIL + 1], dst[LE - 1:E].unsqueeze(0)).then_inc(s_le, 16)
            sp.wait_ge(s_wv, 4)
            for k in range(3):
                sp.dma_start(B3[k:k + 1, :], B3h[0:1, k * BRW:(k + 1) * BRW]).then_inc(s_b3, 16)
            sp.wait_ge(s_ep, 1)
            sp.dma_start(dstf_d.rearrange("(t e) -> t e", e=P), ef[:, 0:P]).then_inc(s_fs, 16)
            for k in range(3):
                sp.dma_start(fl_d[k].rearrange("(t e) -> t e", e=P), fle[:, k * P:(k + 1) * P]).then_inc(s_fs, 16)

            xv = x[0:NT * P, :].rearrange("(p j) d -> p (j d)", p=P)
            ov = out[0:NT * P, :].rearrange("(p j) d -> p (j d)", p=P)

            def dense(u, z):
                if (a := sub(u, z, 0)) and not (isinstance(u, int) and a[2] + RING > NSUB):
                    q = a[2]
                    sp.wait_ge(s_pre, q + 1)
                    sp.sem_inc(s_stick, 1)
                    if isinstance(u, int) and q + RING == NSUB:
                        sp.dma_start(XB[z][:, 0:D], x[N - P:N, :]).then_inc(s_xl[z], 16)
                    else:
                        sp.dma_start(XB[z][:, :], xv[:, ds((q + RING) * SW, SW)]).then_inc(s_xl[z], 16)
                if (a := sub(u, z, -3)):
                    _, y, q = a
                    sp.wait_ge(s_o, q + 1)
                    sp.sem_inc(s_stick, 1)
                    if isinstance(u, int) and q == NSUB:
                        sp.dma_start(out[NT * P:N, :], OB[y][P - REST:P, 0:D]).then_inc(s_os[y], 16)
                    else:
                        sp.dma_start(ov[:, ds(q * SW, SW)], OB[y][:, :]).then_inc(s_os[y], 16)

            for z in range(RING):
                sp.dma_start(XB[z][:, :], xv[:, z * SW:(z + 1) * SW]).then_inc(s_xl[z], 16)
            counts_sp(sp)
            prelude(sp, dense)
            edge_sp(sp, dense)

        @block.gpsimd
        def _(g):
            g.memset(ei[:, P:3 * P], 0)
            g.memset(ei[:, 0:P], int(SENT))
            g.memset(ei[:, 3 * P:4 * P], int(SENT)).then_inc(s_tick, 1)
            g.wait_ge(s_tick, 1)
            g.memset(ei[0:1, 3 * P:3 * P + 1], -1).then_inc(s_ms, 1)
            g.memset(ident[:, :], 0.0)
            g.memset(eps[:, :], LN_EPS)
            g.memset(ones[:, :], 1.0)
            g.memset(ones3[:, :], 1.0).then_inc(s_tick, 1)
            g.wait_ge(s_tick, 2)
            g.affine_select(out=ident[:, :], in_=ident[:, :], compare_op=ALU.not_equal, fill=1.0, base=0,
                            pattern=[[-1, P]], channel_multiplier=1).then_inc(s_id, 1)
            g.iota(iota_i[:, :], pattern=[[P, T]], base=0, channel_multiplier=1)
            g.memset(big_i[:, :], BIG).then_inc(s_cn, 1)
            g.wait_ge(s_cn, 1)
            g.dma_start(sm_d[0:NT * P, :].rearrange("(p j) o -> p (j o)", p=P), big_i[:, 0:NT]).then_inc(s_smf, 16)
            g.dma_start(sm_d[NT * P:N, :].rearrange("(p j) o -> p (j o)", p=REST),
                        big_i[0:REST, 0:1]).then_inc(s_smf, 16)
            g.wait_ge(s_ep, 2)
            g.affine_select(out=mk_in[:, :], in_=mk_in[:, :], compare_op=ALU.is_gt, fill=0.0, base=0,
                            pattern=[[1, T]], channel_multiplier=-1)
            g.affine_select(out=mk_out[:, :], in_=mk_out[:, :], compare_op=ALU.is_gt, fill=0.0, base=0,
                            pattern=[[-1, T]], channel_multiplier=1).then_inc(s_mk, 1)
            node_bound = g.to_reg(N - 1)
            slot_bound = g.to_reg(EP - 1)
            g.wait_ge(s_ix, 1)

            def gate(sem_, value):
                g.wait_ge(sem_, value)
                g.sem_inc(s_tick, 1)

            for n, (idx, rows_d) in enumerate(((src_i, xs_d), (dst_i, xd_d))):
                def half(i, k):
                    a = k * CT
                    if n or not isinstance(i, int):
                        gate(s_pst[k], (n * IT + i) * 16)
                    g.tensor_copy(idx_s[:, a:a + CT], idx[:, ds(i * SL + a, CT)]).then_inc(s_ik, 1)
                    gate(s_ik, (n * IT + i) * 2 + k + 1)
                    for j in range(a, a + CT):
                        g.indirect_dma_start(
                            out=G[:, j * D:(j + 1) * D], out_offset=None, in_=x,
                            in_offset=bass.IndirectOffsetOnAxis(ap=idx_s[:, j:j + 1], axis=0),
                            bounds_check=node_bound, oob_is_err=False).then_inc(s_ga[j], 16)
                    for j in range(a, a + CT):
                        gate(s_ga[j], (n * IT + i) * 16 + 16)
                    g.dma_start(chunk(rows_d, i * 2 + k), three(G[:, a * D:(a + CT) * D])).then_inc(s_pst[k], 16)

                for k in range(2):
                    half(0, k)
                with g.Fori(1, IT) as i:
                    for k in range(2):
                        half(i, k)
            for k in range(2):
                g.wait_ge(s_pst[k], 2 * IT * 16)
            g.wait_ge(s_smf, 32)
            with g.Fori(0, IT) as i:
                for j in range(SL):
                    gate(s_ga[j], (2 * IT + i) * 16)
                g.tensor_copy(idx_s[:, :], lead_i[:, ds(i * SL, SL)])
                g.tensor_copy(val_s[:, :], iota_i[:, ds(i * SL, SL)]).then_inc(s_ik, 1)
                gate(s_ik, 4 * IT + i + 1)
                for j in range(SL):
                    g.indirect_dma_start(
                        out=sm_d, out_offset=bass.IndirectOffsetOnAxis(ap=idx_s[:, j:j + 1], axis=0),
                        in_=val_s[:, j:j + 1], in_offset=None,
                        bounds_check=node_bound, oob_is_err=False).then_inc(s_ga[j], 16)
            for j in range(SL):
                g.wait_ge(s_ga[j], 3 * IT * 16)
            with g.Fori(0, IT) as i:
                g.tensor_copy(idx_s[:, :], src_i[:, ds(i * SL, SL)]).then_inc(s_ik, 1)
                gate(s_ik, 5 * IT + 2 * i + 1)
                for j in range(SL):
                    g.indirect_dma_start(
                        out=val_s[:, j:j + 1], out_offset=None, in_=sm_d,
                        in_offset=bass.IndirectOffsetOnAxis(ap=idx_s[:, j:j + 1], axis=0),
                        bounds_check=node_bound, oob_is_err=False).then_inc(s_ga[j], 16)
                for j in range(SL):
                    gate(s_ga[j], (3 * IT + i) * 16 + 16)
                g.tensor_copy(slot_i[:, ds(i * SL, SL)], val_s[:, :]).then_inc(s_ik, 1)
                gate(s_ik, 5 * IT + 2 * i + 2)
            edge_pool(g, node_bound, slot_bound, gate)

        @block.tensor
        def _(pe):
            pe.wait_ge(s_lw, LOADS * 16)
            pe.wait_ge(s_id, 1)
            nc.tensor.transpose(BK[0][:, 0:D], Wemb[:, :], ident[:, :])
            nc.tensor.transpose(BK[0][:, D:2 * D], rt[:, :], ident[:, :]).then_inc(s_w1, 1)
            pe.wait_ge(s_wa, 2)
            nc.tensor.matmul(BK[1][:, :], wT[:, 0:D], bs[:, 0:B * D], start=True, stop=True)
            nc.tensor.matmul(BK[2][:, 0:D], wT[:, 0:D], slf[:, 0:D], start=True, stop=True)
            nc.tensor.matmul(BK[2][:, 2 * D:3 * D], wT[:, D:2 * D], gw[:, :], start=True, stop=True)
            pe.wait_ge(s_wv, 1)
            nc.tensor.matmul(BK[2][:, D:2 * D], wbc[:, 0:P], slf[:, 0:D], start=True, stop=True)
            nc.tensor.matmul(BK[3][:, :], wbc[:, 0:P], bs[:, 0:B * D], start=True, stop=True)
            nc.tensor.matmul(BK[2][:, 3 * D:4 * D], wbc[:, P:2 * P], gw[:, :], start=True, stop=True).then_inc(s_w1, 1)
            pe.wait_ge(s_wv, 3)
            nc.tensor.transpose(BK[4][:, 0:D], BR[:, OFF_B:OFF_B + D], ident[:, :]).then_inc(s_w1, 1)
            pe.wait_ge(s_ep, 1)
            nc.tensor.matmul(BK[5][:, 0:2 * T], ones[0:T, :], fld[:, :], start=True, stop=True)
            for k, a in enumerate((ef[:, 0:P], ef[:, P:2 * P], ef[:, 2 * P:3 * P], lead[:, :])):
                last = nc.tensor.transpose(BK[6][:, k * T:(k + 1) * T], a, ident[0:T, 0:T])
            last.then_inc(s_fb, 1)

            def dense(u, z):
                if (a := sub(u, z, 2)):
                    it, y, q = a
                    pe.wait_ge(s_xl[y], it * 16 + 16)
                    if past(q, 1):
                        pe.wait_ge(s_xt, q)
                    if past(q, 4):
                        pe.wait_ge(s_yt, q - 3)
                    for t in range(tiles(q)):
                        last = nc.tensor.transpose(BK[4][:, t * D:(t + 1) * D], XB[y][:, t * D:(t + 1) * D], ident[:, :])
                    last.then_inc(s_tx, 1)
                if (a := sub(u, z, 1)):
                    _, y, q = a
                    w = tiles(q) * D
                    pe.wait_ge(s_xt, q + 1)
                    if past(q, 1):
                        pe.wait_ge(s_ht, q)
                    nc.tensor.matmul(BK[5][:, 0:w], M[0][:, :], xT[y % 2][:, 0:w], start=True, stop=True).then_inc(s_hp, 1)
                if (a := sub(u, z, 0)):
                    _, y, q = a
                    pe.wait_ge(s_ht, q + 1)
                    if past(q, 1):
                        pe.wait_ge(s_pre, q)
                    rows(BK[6], tiles(q), OFF_B + D, hT[y % 2], M[1]).then_inc(s_yp, 1)
                if (a := sub(u, z, -2)):
                    _, y, q = a
                    pe.wait_ge(s_yt, q + 1)
                    if past(q, 1):
                        pe.wait_ge(s_z, q)
                    rows(BK[7], tiles(q), OFF_DX, yT[y % 2], M[2]).then_inc(s_zp, 1)
                if (a := sub(u, z, -1)):
                    _, y, q = a
                    pe.wait_ge(s_y, q + 1)
                    pe.wait_ge(s_xt, min(q + 4, NSUB + 1) if isinstance(q, int) else q + 4)
                    if past(q, 1):
                        pe.wait_ge(s_yt, q)
                    for t in range(tiles(q)):
                        last = nc.tensor.transpose(BK[4][:, t * D:(t + 1) * D], Y[y][:, t * D:(t + 1) * D], ident[:, :])
                    last.then_inc(s_ty, 1)

            def rows(bank, n, off, lhs, w):
                b = B3[:, off:off + D]
                nc.tensor.matmul(bank[:, 0:n * D], ones3[:, :], b if n == 1 else bc_mid(b, n),
                                 start=True, stop=False)
                for t in range(n):
                    last = nc.tensor.matmul(bank[:, t * D:(t + 1) * D], lhs[:, t * D:(t + 1) * D], w[:, :],
                                            start=False, stop=(t == n - 1))
                return last

            pe.wait_ge(s_b3, 48)
            pe.wait_ge(s_wv, 5)
            relation_weights(pe)
            edge_counts(pe)
            prelude(pe, dense)
            edge_pe(pe, dense, rows)

        @block.scalar
        def _(act):
            for dst_ap, src_ap in LOAD_LIST:
                act.dma_start(dst_ap, src_ap).then_inc(s_lw, 16)
            act.wait_ge(s_w1, 1)
            nc.scalar.copy(wT[:, :], BK[0][:, 0:2 * D]).then_inc(s_wa, 1)
            act.wait_ge(s_wv, 1)
            nc.scalar.activation(vt[:, :], vt[:, :], ACT.Sqrt).then_inc(s_wa, 1)

            def dense(u, z):
                if (a := sub(u, z, -3)):
                    it, y, q = a
                    n = tiles(q)
                    act.wait_ge(s_nb2, q + 1)
                    if past(q, RING):
                        act.wait_ge(s_os[y], it * 16)
                    for t in range(n):
                        last = nc.scalar.activation(OB[y][:, t * D:(t + 1) * D], Z[y][:, t * D:(t + 1) * D],
                                                    ACT.Identity, bias=dnb2[y % 2][:, t:t + 1],
                                                    scale=drs2[y % 2][:, t:t + 1])
                    last.then_inc(s_o, 1)
                if (a := sub(u, z, 2)):
                    _, y, q = a
                    w = tiles(q) * D
                    act.wait_ge(s_tx, q + 1)
                    if past(q, 2):
                        act.wait_ge(s_hp, q - 1)
                    nc.scalar.copy(xT[y % 2][:, 0:w], BK[4][:, 0:w]).then_inc(s_xt, 1)
                if (a := sub(u, z, 1)):
                    _, y, q = a
                    w = tiles(q) * D
                    act.wait_ge(s_hp, q + 1)
                    if past(q, 2):
                        act.wait_ge(s_yp, q - 1)
                    nc.scalar.activation(hT[y % 2][:, 0:w], BK[5][:, 0:w], ACT.Relu, bias=b0c[:, 0:1]).then_inc(s_ht, 1)
                if (a := sub(u, z, -1)):
                    _, y, q = a
                    w = tiles(q) * D
                    act.wait_ge(s_ty, q + 1)
                    if past(q, 2):
                        act.wait_ge(s_zp, q - 1)
                    nc.scalar.copy(yT[y % 2][:, 0:w], BK[4][:, 0:w]).then_inc(s_yt, 1)
                if (a := sub(u, z, 0)):
                    _, y, q = a
                    n = tiles(q)
                    act.wait_ge(s_ag1, q + 1)
                    if past(q, 2):
                        act.wait_ge(s_y, q - 1)
                    nc.scalar.activation(dsd1[y % 2][:, 0:n], dmv1[y % 2][:, 1:2 * n:2], ACT.Sqrt,
                                         bias=eps[:, 0:1]).then_inc(s_sq1, 1)
                if (a := sub(u, z, -2)):
                    it, y, q = a
                    n = tiles(q)
                    act.wait_ge(s_ag2, q + 1)
                    if past(q, 2):
                        act.wait_ge(s_nb2, q - 1)
                    nc.scalar.activation(dsd2[y % 2][:, 0:n], dmv2[y % 2][:, 1:2 * n:2], ACT.Sqrt,
                                         bias=eps[:, 0:1]).then_inc(s_sq2, 1)

            act.wait_ge(s_wv, 5)
            edge_counts_act(act)
            prelude(act, dense)
            edge_act(act, dense)

        @block.vector
        def _(v):
            chain = [0]

            def link(ins):
                chain[0] += 1
                ins.then_inc(s_dv, 1)
                v.wait_ge(s_dv, chain[0])

            v.wait_ge(s_lw, LOADS * 16)
            nc.vector.tensor_copy(wbc[:, 0:P], bemb[:, 0:1].broadcast_to([P, P]))
            nc.vector.tensor_copy(wbc[:, P:2 * P], b1c[:, 0:1].broadcast_to([P, P]))
            nc.vector.tensor_scalar_add(vt[:, :], bnv[:, :], BN_EPS).then_inc(s_wv, 1)
            v.wait_ge(s_wa, 2)
            link(nc.vector.reciprocal(vt[:, :], vt[:, :]))
            link(nc.vector.tensor_tensor(sc[:, :], bng[:, :], vt[:, :], ALU.mult))
            nc.vector.tensor_tensor(four(V[1]), four(bs[:, B * D:2 * B * D]), bc_mid(sc[:, D:2 * D], B), ALU.mult)
            nc.vector.tensor_tensor(M[1][:, :], slf[:, D:2 * D], sc[:, D:2 * D], ALU.mult)
            link(nc.vector.tensor_tensor(vt[:, :], bnm[:, :], sc[:, :], ALU.mult))
            link(nc.vector.tensor_tensor(vt[:, :], bnb[:, :], vt[:, :], ALU.subtract))
            v.wait_ge(s_w1, 2)
            nc.vector.tensor_tensor(four(V[0]), four(BK[1][:, :]), bc_mid(sc[:, 0:D], B), ALU.mult)
            nc.vector.tensor_tensor(four(BR[:, 0:B * D]), four(BK[3][:, :]), bc_mid(sc[:, 0:D], B), ALU.mult)
            nc.vector.tensor_tensor(M[0][:, :], BK[2][:, 0:D], sc[:, 0:D], ALU.mult)
            nc.vector.tensor_copy(M[2][:, :], BK[2][:, 2 * D:3 * D])
            nc.vector.tensor_tensor(BR[:, OFF_B:OFF_B + D], BK[2][:, D:2 * D], sc[:, 0:D], ALU.mult)
            nc.vector.tensor_copy(BR[:, OFF_B + D:OFF_B + 2 * D], vt[:, D:2 * D])
            nc.vector.tensor_copy(BR[:, OFF_B + 2 * D:OFF_B + 3 * D], BK[2][:, 3 * D:4 * D])
            link(nc.vector.tensor_tensor(BR[:, OFF_DX:OFF_DX + D], BK[2][:, 3 * D:4 * D], gbb[:, :], ALU.add))
            link(nc.vector.tensor_tensor(BR[:, OFF_B:OFF_B + D], BR[:, OFF_B:OFF_B + D], vt[:, 0:D], ALU.add))
            link(nc.vector.tensor_copy(B3h[0:1, 0:BRW], BR[0:1, :]))
            nc.vector.tensor_tensor(bsp[0], BR[0:1, :], B3h[0:1, 0:BRW], ALU.subtract).then_inc(s_wv, 2)
            v.wait_ge(s_wv, 3)
            link(nc.vector.tensor_copy(B3h[0:1, BRW:2 * BRW], bsp[0]))
            link(nc.vector.tensor_tensor(bsp[1], bsp[0], B3h[0:1, BRW:2 * BRW], ALU.subtract))
            nc.vector.tensor_copy(B3h[0:1, 2 * BRW:3 * BRW], bsp[1]).then_inc(s_wv, 1)
            v.wait_ge(s_w1, 3)
            nc.vector.tensor_copy(b0c[:, :], BK[4][:, 0:1]).then_inc(s_wv, 1)

            v.wait_ge(s_le, 9 * 16)
            link(nc.vector.tensor_copy(ef[:, :], ei[:, :]))
            v.wait_ge(s_id, 1)
            for k, c in enumerate((0, P - 1)):
                nc.vector.tensor_scalar(fle[:, k * P:(k + 1) * P], ef[:, 0:P], ef[:, c:c + 1], None, ALU.is_equal)
                nc.vector.tensor_scalar(fld[:, k * T:(k + 1) * T], ident[0:T, 0:T], ef[:, c:c + 1], None, ALU.mult)
            nc.vector.memset(fle[:, 2 * P:3 * P], 1.0)
            link(nc.vector.tensor_tensor(lead[:, :], ef[:, 0:P], ef[:, 3 * P:4 * P], ALU.is_equal))
            nc.vector.scalar_tensor_tensor(out=lead[:, :], in0=lead[:, :], scalar=float(BIG), in1=ef[:, 0:P],
                                           op0=ALU.mult, op1=ALU.add).then_inc(s_ep, 1)
            v.wait_ge(s_fb, 1)
            nc.vector.tensor_copy(FBC[:, :], BK[5][:, 0:2 * T])
            link(nc.vector.tensor_copy(EC[:, :], BK[6][:, 0:4 * T]))
            nc.vector.tensor_copy(src_i[:, :], col(1))
            nc.vector.tensor_scalar(dst_i[:, :], col(0), float(N - 1), None, ALU.min)
            nc.vector.tensor_copy(lead_i[:, :], col(3)).then_inc(s_ix, 1)
            nc.vector.tensor_scalar(mk_in[:, :], FBC[0:T, 0:T], ef[:, P - 1:P], None, ALU.is_equal)
            nc.vector.tensor_scalar(mk_out[:, :], FBC[0:T, T:2 * T], ef[:, 0:1], None, ALU.is_equal).then_inc(s_ep, 1)
            nc.vector.tensor_tensor(eqc[:, 0:T], col(0), FBC[:, 0:T], ALU.is_equal)
            nc.vector.tensor_tensor(eqc[:, T:2 * T], col(0), FBC[:, T:2 * T], ALU.is_equal)
            for r in range(R):
                last = nc.vector.tensor_scalar(OH[:, :].rearrange("p (t r) -> p t r", r=R)[:, :, r], col(2), float(r), None, ALU.is_equal)
            link(last)

            def dense(u, z):
                a, b = sub(u, z, 0), sub(u, z, -2)
                if a:
                    _, y, q = a
                    w = tiles(q) * D
                    v.wait_ge(s_yp, q + 1)
                    if past(q, RING):
                        v.wait_ge(s_z, q - 3)
                    nc.vector.scalar_tensor_tensor(out=Y[y][:, 0:w], in0=BK[6][:, 0:w], scalar=0.0, in1=XB[y][:, 0:w],
                                                   op0=ALU.max, op1=ALU.add).then_inc(s_pre, 1)
                if b:
                    _, y, q = b
                    w = tiles(q) * D
                    v.wait_ge(s_zp, q + 1)
                    if past(q, RING):
                        v.wait_ge(s_o, q - 3)
                    nc.vector.tensor_tensor(Z[y][:, 0:w], BK[7][:, 0:w], Y[y][:, 0:w], ALU.add).then_inc(s_z, 1)
                both = [(a, s_pre, Y, dst1, dmv1, s_bs1, s_ag1), (b, s_z, Z, dst2, dmv2, s_bs2, s_ag2)]
                for c, ready, rows_, bn, _, s_bs, _ in both:
                    if c:
                        _, y, q = c
                        v.wait_ge(ready, q + 1)
                        for t in range(tiles(q)):
                            last = nc.vector.bn_stats(bn[y % 2][:, 6 * t:6 * t + 6], rows_[y][:, t * D:(t + 1) * D])
                        last.then_inc(s_bs, 1)
                for c, _, _, bn, mv_, s_bs, s_agg in both:
                    if c:
                        _, y, q = c
                        v.wait_ge(s_bs, q + 1)
                        v.sem_inc(s_vtick, 1)
                        for t in range(tiles(q)):
                            last = nc.vector.bn_aggr(mv_[y % 2][:, 2 * t:2 * t + 2], bn[y % 2][:, 6 * t:6 * t + 6])
                        last.then_inc(s_agg, 1)
                for c, s_sqr, rs_, sd_, s_rc in ((a, s_sq1, drs1, dsd1, s_rc1), (b, s_sq2, drs2, dsd2, s_rc2)):
                    if c:
                        _, y, q = c
                        n = tiles(q)
                        v.wait_ge(s_sqr, q + 1)
                        nc.vector.reciprocal(rs_[y % 2][:, 0:n], sd_[y % 2][:, 0:n]).then_inc(s_rc, 1)
                if a:
                    _, y, q = a
                    v.wait_ge(s_rc1, q + 1)
                    for t in range(tiles(q)):
                        o = Y[y][:, t * D:(t + 1) * D]
                        last = nc.vector.tensor_scalar(o, o, dmv1[y % 2][:, 2 * t:2 * t + 1], drs1[y % 2][:, t:t + 1],
                                                       ALU.subtract, ALU.mult)
                    last.then_inc(s_y, 1)
                if b:
                    _, y, q = b
                    n = tiles(q)
                    v.wait_ge(s_rc2, q + 1)
                    nc.vector.scalar_tensor_tensor(out=dnb2[y % 2][:, 0:n], in0=dmv2[y % 2][:, 0:2 * n:2], scalar=-1.0,
                                                   in1=drs2[y % 2][:, 0:n], op0=ALU.mult, op1=ALU.mult).then_inc(s_nb2, 1)

            counts_dve(v, link)
            prelude(v, dense)
            edge_dve(v, link, dense)

_INS = ["x", "src", "dst", "edge_type_8", "L0_gnn_W_emb", "L0_gnn_b_emb", "L0_gnn_bases", "L0_gnn_w_coe",
        "L0_gnn_self_loop", "L0_gnn_bn_gamma", "L0_gnn_bn_beta", "L0_gnn_bn_mean", "L0_gnn_bn_var",
        "L1_gnn_comp", "L1_gnn_basis", "L1_gnn_root", "L1_gnn_bias1", "L1_gnn_gat_w", "L1_gnn_att_src",
        "L1_gnn_att_dst", "L1_gnn_gat_bias"]


def kernel(**inputs):
    import numpy as np
    import concourse.bacc as bacc
    from concourse.bass_utils import run_bass_kernel_spmd

    nc = bacc.Bacc("TRN2", target_bir_lowering=False, num_devices=1)
    arrays, args = {}, []
    for name in _INS:
        a = np.ascontiguousarray(inputs[name])
        arrays[f"in_{name}"] = a
        args.append(nc.dram_tensor(f"in_{name}", a.shape, mybir.dt.from_np(a.dtype), kind="ExternalInput").ap())
    out = nc.dram_tensor("out", arrays["in_x"].shape, mybir.dt.float32, kind="ExternalOutput").ap()
    gnn_program(nc, *args, out)
    r = run_bass_kernel_spmd(nc, [arrays], core_ids=[0])
    return r.results[0]["out"]
```

```python
import concourse.bass as bass
from concourse import mybir
from contextlib import ExitStack


def gnn_program(nc, x, src, dst, etype, W_emb, b_emb, bases, w_coe, self_loop, bn_gamma, bn_beta,
                bn_mean, bn_var, comp, basis, root, bias1, gat_w, att_src, att_dst, gat_bias, out):
    f32, bf16, i32 = mybir.dt.float32, mybir.dt.bfloat16, mybir.dt.int32
    ALU, ACT, AX = mybir.AluOpType, mybir.ActivationFunctionType, mybir.AxisListType
    ds = bass.ds

    P = 128
    N, D = x.shape
    E = src.shape[0]
    R = comp.shape[0]
    NB = comp.shape[1]
    B = bases.shape[1]
    H = att_src.shape[0]
    HD = D // H
    T = -(-E // P)
    CT = 7
    IT = T // (2 * CT)
    SL = 2 * CT
    GT = (0, 4, CT)
    GS = 4
    NG = IT * GS
    assert T == IT * SL
    EP = T * P
    TAIL = E - (T - 1) * P
    CW = CT * D
    UW = D + H
    BIG = 1 << 20
    NEG = -1.0e30
    SENT = 60000.0
    assert N - 1 < SENT
    LN_EPS, BN_EPS, SLOPE = 1e-5, 1e-3, 0.2

    NT = N // P
    SUB = 3
    NSUB = NT // SUB
    assert NSUB * SUB == NT
    SW = SUB * D
    REST = N - NT * P
    RING = 4
    UNITS = NSUB // RING
    DU = dict(C=[1 + r * (IT + 1) for r in range(3)], B=[2 + r * (IT + 1) for r in range(3)], S=UNITS - IT)
    assert DU["S"] == DU["B"][2] + IT

    OFF_BV, OFF_B = 0, B * D
    OFF_DX = OFF_B + 3 * D
    OFF_GB = OFF_DX + D
    BRW = OFF_GB + D

    ctx = ExitStack()
    with ctx:
        def sb(name, shape, dt=f32):
            return ctx.enter_context(nc.sbuf_tensor(name, shape, dt))

        def sem(name):
            return ctx.enter_context(nc.semaphore(name))

        def dram(name, shape, dt=f32):
            return nc.dram_tensor(name, shape, dt, kind="Internal").ap()

        dstf_d = dram("dstf_d", (EP,))
        fl_d = dram("fl_d", (3, EP))
        xs_d = dram("xs_d", (EP, D))
        xd_d = dram("xd_d", (EP, D))
        hs_d = dram("hs_d", (EP, D))
        ys_d = dram("ys_d", (EP, D))
        ls_d = dram("ls_d", (EP, D))
        lm_d = dram("lm_d", (EP, D))
        h_d = dram("h_d", (EP, D))
        y_d = dram("y_d", (EP, D))
        l_d = dram("l_d", (EP, D))
        u_d = [dram(f"u{r}_d", (EP, D)) for r in range(3)]
        ua_d = dram("ua_d", (EP, UW))
        cr_d = [dram(f"cr{r}_d", (3, T, D)) for r in range(3)]
        cra_d = dram("cra_d", (2, T, UW))
        cc_d = dram("cc_d", (2, T, R))
        ce_d = dram("ce_d", (2, T, R))
        sm_d = dram("sm_d", (N, 1), i32)

        def chunk(a, c, w=D):
            return a[ds(c * CT * P, CT * P), :].rearrange("(t p) f -> p t f", p=P)

        ident = sb("ident", [P, P])
        ones = sb("ones", [P, P])
        ones3 = sb("ones3", [3, P], bf16)
        Wemb = sb("Wemb", [P, D])
        bemb = sb("bemb", [P, 1])
        bs = sb("bs", [P, 2 * B * D])
        slf = sb("slf", [P, 2 * D])
        bng = sb("bng", [P, 2 * D])
        bnb = sb("bnb", [P, 2 * D])
        bnm = sb("bnm", [P, 2 * D])
        bnv = sb("bnv", [P, 2 * D])
        rt = sb("rt", [P, D])
        b1c = sb("b1c", [P, 1])
        gw = sb("gw_sb", [P, D])
        bass_ = sb("basis_sb", [P, NB * D])
        gbb = sb("gbb", [P, D])
        attb = sb("attb", [P, 2 * D])
        cmpb = sb("cmpb", [P, R * NB])
        wcb = sb("wcb", [P, 2 * R * B])
        V = [sb("V0", [P, B * D]), sb("V1", [P, B * D]), sb("V2", [P, R * D])]
        M = [sb(f"M{l}", [P, D]) for l in range(3)]
        BR = sb("BR", [P, BRW])
        B3h = sb("B3h", [1, 3 * BRW], bf16)
        B3 = sb("B3", [3, BRW], bf16)
        b0c = sb("b0c", [P, 1])
        sc = sb("sc", [P, 2 * D])
        vt = sb("vt", [P, 2 * D])
        WW = sb("WW", [P, 2 * R * D])
        Wr, WrT = WW[:, 0:R * D], WW[:, R * D:2 * R * D]
        wT = sb("wT", [P, 2 * D])
        wbc = sb("wbc", [P, 2 * P])

        ei = sb("ei", [T, 4 * P], i32)
        ef = sb("ef", [T, 4 * P])
        fle = sb("fle", [T, 3 * P])
        lead = sb("lead", [T, P])
        fld = sb("fld", [T, 2 * T])
        FBC = sb("FBC", [P, 2 * T])
        mk_in = sb("mk_in", [T, T])
        mk_out = sb("mk_out", [T, T])
        EC = sb("EC", [P, 4 * T])
        src_i = sb("src_i", [P, T], i32)
        dst_i = sb("dst_i", [P, T], i32)
        lead_i = sb("lead_i", [P, T], i32)
        slot_i = sb("slot_i", [P, T], i32)
        iota_i = sb("iota_i", [P, T], i32)
        big_i = sb("big_i", [P, NT], i32)
        OH = sb("OH", [P, T * R])
        CNT = sb("CNT", [P, T * R])
        CB = WW[:, 0:2 * T * R]
        ct = sb("ct", [T, 2 * R])
        cti = sb("cti", [T, 2 * R])
        q1 = sb("q1", [P, T * R])
        q2 = sb("q2", [P, T * R])
        eqc = sb("eqc", [P, 2 * T])
        nrm = sb("nrm", [P, T])
        nz = sb("nz", [P, T])
        wq = sb("wq", [P, T])
        C = [sb("C0", [P, T * B]), sb("C1", [P, T * B]), sb("C2", [P, T * R])]
        AS = sb("AS", [P, T * H])
        AD = sb("AD", [P, 2 * T * H])
        MX = sb("MX", [P, T * H])
        EA = sb("EA", [P, T * H])
        ES = sb("ES", [P, T * H])

        G = sb("G", [P, SL * D])
        ZT = [sb(f"ZT{k}", [P, 4 * D]) for k in range(2)]
        EQ = [sb(f"EQ{k}", [P, P]) for k in range(4)]
        MS = [sb(f"MS{k}", [P, D]) for k in range(4)]
        MT = [sb(f"MT{k}", [P, D]) for k in range(4)]
        UFL = sb("UFL", [T, 2 * UW])
        CIO = sb("CIO", [T, 2 * UW])
        st = sb("st", [P, SL * 6])
        mv = sb("mv", [P, SL * 2])
        sd = sb("sd", [P, SL])
        rs = sb("rs", [P, SL])
        nb = sb("nb", [P, SL])
        idx_s = sb("idx_s", [P, SL], i32)
        red = [sb(f"red{k}", [P, 2 * CT * H]) for k in range(2)]
        W1 = sb("W1", [P, CT * UW])

        DB2, XR2, HB2 = (sb(n, [P, 2 * CW]) for n in ("DB2", "XR2", "HB2"))
        UB2 = sb("UB2", [P, 2 * CT * UW])
        FL2 = sb("FL2", [3, 2 * CW])
        CR2 = sb("CR2", [3, 2 * CT * UW])
        DB = [DB2[:, k * CW:(k + 1) * CW] for k in range(2)]
        XR = [XR2[:, k * CW:(k + 1) * CW] for k in range(2)]
        HB = [HB2[:, k * CW:(k + 1) * CW] for k in range(2)]
        UB = [UB2[:, k * CT * UW:(k + 1) * CT * UW] for k in range(2)]
        FLc = [FL2[:, k * CW:(k + 1) * CW] for k in range(2)]
        CRc = [CR2[:, k * CT * UW:(k + 1) * CT * UW] for k in range(2)]
        bsp = [a[0:1, 0:BRW] for a in (UB2, HB2)]

        XB = [sb(f"XB{k}", [P, SW]) for k in range(RING)]
        OB = [sb(f"OB{k}", [P, SW]) for k in range(RING)]
        Y = [sb(f"Y{k}", [P, SW]) for k in range(RING)]
        Z = [sb(f"Z{k}", [P, SW]) for k in range(RING)]
        xT = [sb(f"xT{k}", [P, SW]) for k in range(2)]
        hT = [sb(f"hT{k}", [P, SW]) for k in range(2)]
        yT = [sb(f"yT{k}", [P, SW]) for k in range(2)]
        dst1, dst2 = ([sb(f"dst{n}_{k}", [P, SUB * 6]) for k in range(2)] for n in (1, 2))
        dmv1, dmv2 = ([sb(f"dmv{n}_{k}", [P, SUB * 2]) for k in range(2)] for n in (1, 2))
        dsd1, dsd2 = ([sb(f"dsd{n}_{k}", [P, SUB]) for k in range(2)] for n in (1, 2))
        drs1, drs2 = ([sb(f"drs{n}_{k}", [P, SUB]) for k in range(2)] for n in (1, 2))
        dnb2 = [sb(f"dnb2_{k}", [P, SUB]) for k in range(2)]
        eps = sb("eps", [P, 1])

        BK = [ctx.enter_context(nc.psum_tensor(f"BK{k}", [P, 512], f32)) for k in range(8)]

        edge_tiles_set = sem("edge_tiles_set")
        edges_loaded = sem("edges_loaded")
        weights_loaded = sem("weights_loaded")
        ident_ready = sem("ident_ready")
        edge_prep = sem("edge_prep")
        edge_columns = sem("edge_columns")
        masks_stored = sem("masks_stored")
        carry_masks = sem("carry_masks")
        indices_ready = sem("indices_ready")
        index_consts = sem("index_consts")
        table_filled = sem("table_filled")
        rows_stored = [sem(f"rows_stored{k}") for k in range(2)]
        gathered = [sem(f"gathered{j}") for j in range(SL)]
        index_staged = sem("index_staged")
        pool_tick = sem("pool_tick")
        weight_products = sem("weight_products")
        act_weights = sem("act_weights")
        dve_weights = sem("dve_weights")
        bias_ready = sem("bias_ready")
        dve_order = sem("dve_order")
        relation_terms = sem("relation_terms")
        x_loaded = [sem(f"x_loaded{k}") for k in range(RING)]
        out_stored = [sem(f"out_stored{k}") for k in range(RING)]
        x_transposed, xT_copied, h1_made, hT_ready, h2_made = (sem(n) for n in ("x_transposed", "xT_copied", "h1_made", "hT_ready", "h2_made"))
        pre_y_ready, y_stats, y_deviation, y_ready, y_transposed = (sem(n) for n in ("pre_y_ready", "y_stats", "y_deviation", "y_ready", "y_transposed"))
        yT_copied, xl_made, z_ready, z_stats, z_deviation = (sem(n) for n in ("yT_copied", "xl_made", "z_ready", "z_stats", "z_deviation"))
        z_shift, out_ready = sem("z_shift"), sem("out_ready")
        base_loaded = [sem(f"base_loaded{k}") for k in range(2)]
        dst_loaded = [sem(f"dst_loaded{k}") for k in range(2)]
        residual_loaded = [sem(f"residual_loaded{k}") for k in range(2)]
        sums_loaded = [sem(f"sums_loaded{k}") for k in range(2)]
        results_stored = [sem(f"results_stored{k}") for k in range(2)]
        rows_transposed = sem("rows_transposed")
        rowsT_copied = sem("rowsT_copied")
        products_made = sem("products_made")
        self_made = sem("self_made")
        rows_ready = sem("rows_ready")
        self_taken = sem("self_taken")
        equality_ready = sem("equality_ready")
        terms_added = sem("terms_added")
        segments_made = sem("segments_made")
        segments_copied = sem("segments_copied")
        slots_added = sem("slots_added")
        deviations_ready = sem("deviations_ready")
        stats_ready = sem("stats_ready")
        first_bank = sem("first_bank")
        first_terms = sem("first_terms")
        shift_ready = sem("shift_ready")
        counts_taken = sem("counts_taken")
        self_loops_ready = sem("self_loops_ready")
        residual_made = sem("residual_made")
        residual_taken = sem("residual_taken")
        carry_in_loaded = sem("carry_in_loaded")
        carries_made = sem("carries_made")
        carries_copied = sem("carries_copied")
        carries_stored = sem("carries_stored")
        counts_copied = sem("counts_copied")
        attention_pe = sem("attention_pe")
        attention_act = sem("attention_act")
        attention_dve = sem("attention_dve")
        scatter_done = [sem(f"scatter_done{j}") for j in range(SL)]
        scores_ready = sem("scores_ready")

        block = ctx.enter_context(nc.Block())

        def run(eng, its, per, lead, tail, body):
            for s in range(-lead, per):
                body(0, s)
            with eng.Fori(1, its - 1) as i:
                for s in range(per):
                    body(i, s)
            for s in range(per + tail):
                body(its - 1, s)

        def at(i, s, per, count):
            q = i * per + s
            if isinstance(i, int) and not 0 <= q < count:
                return None
            return i + s // per, s % per, q

        def sub(u, z, o):
            q = u * RING + z + o
            if isinstance(u, int) and not 0 <= q <= NSUB:
                return None
            return u + (z + o) // RING, (z + o) % RING, q

        def tiles(q):
            return 1 if isinstance(q, int) and q == NSUB else SUB

        def past(q, n):
            return not isinstance(q, int) or q >= n

        def prelude(dense):
            for z in range(-2, RING):
                dense(0, z)

        def rest(dense):
            for z in range(NSUB - UNITS * RING + 4):
                dense(UNITS, z)

        def group_of(s):
            z = s % GS
            k, g = z // 2, z % 2
            n = GT[g + 1] - GT[g]
            return k, g, GT[g], n, k * CT + GT[g]

        def three(a):
            return a.rearrange("p (a f) -> p a f", f=D)

        def col(k):
            return EC[:, k * T:(k + 1) * T]

        def bc_mid(a, n):
            return a.unsqueeze(1).broadcast_to([a.shape[0], n, a.shape[1]])

        def bc_in(a, n):
            return a.unsqueeze(2).broadcast_to([a.shape[0], a.shape[1], n])

        def four(a):
            return a.rearrange("p (b f) -> p b f", f=D)

        val_s = sb("val_s", [P, SL], i32)
        y_moments, z_moments, y_scale, z_scale = (sem(n) for n in ("y_moments", "z_moments", "y_scale", "z_scale"))
        dve_tick, act_tick = sem("dve_tick"), sem("act_tick")

        def bcast(a):
            return a.partition_broadcast(P)

        LOAD_LIST = [
            (Wemb[:, :], W_emb), (bemb[:, :], b_emb.rearrange("(k o) -> k o", o=1)),
            (four(bs[:, :]), bases.rearrange("l b k f -> k (l b) f")),
            (four(slf[:, :]), self_loop.rearrange("l k f -> k l f")),
            (bng[:, :], bcast(bn_gamma.rearrange("l f -> (l f)"))),
            (bnb[:, :], bcast(bn_beta.rearrange("l f -> (l f)"))),
            (bnm[:, :], bcast(bn_mean.rearrange("l f -> (l f)"))),
            (bnv[:, :], bcast(bn_var.rearrange("l f -> (l f)"))),
            (rt[:, :], root), (b1c[:, :], bias1.rearrange("(k o) -> k o", o=1)), (gw[:, :], gat_w),
            (four(bass_[:, :]), basis.rearrange("b i o -> i b o")),
            (gbb[:, :], bcast(gat_bias)),
            (attb[:, 0:D], bcast(att_src.rearrange("h d -> (h d)"))),
            (attb[:, D:2 * D], bcast(att_dst.rearrange("h d -> (h d)"))),
            (cmpb[:, :], bcast(comp.rearrange("r b -> (r b)"))),
            (wcb[:, :], bcast(w_coe.rearrange("l r b -> (l r b)"))),
        ]
        LOADS = len(LOAD_LIST)

        N_A, N_B = (0, 2, 4), (1, 3, 5)
        HB_N = dict(A1=1, B=(0, 2, 3), O=4)
        LD = dict(A=(0, 2, 4), B=(1, 3, 5, 8), S=6, W=7)
        ST = dict(A=(0, 3, 6), B=(2, 5, 8), S=9, W=10)
        J = (B, B, R)
        CM = tuple(j - 1 for j in J)
        src_rows = (xs_d, hs_d, ys_d)
        src_next = (hs_d, ys_d, ls_d)
        table = (None, h_d, y_d, l_d)
        dst_rows = (xd_d, h_d, y_d)
        dst_next = (h_d, y_d, l_d)
        CH = IT * 2
        MG = [a[:, 0:CT * UW] for a in (XR2, HB2)]
        GO = (0, 3, 6, CT)

        sp_tick = sem("sp_tick")
        counts_made = sem("counts_made")
        slots_made = sem("slots_made")
        weighted_ready = sem("weighted_ready")
        loop_order = sem("loop_order")

        def places(buf, widths):
            o, a = 0, []
            for w in widths:
                a.append(buf[0:T, o:o + w])
                o += w
            assert o <= buf.shape[1]
            return a

        SMX, TF, TB, pen, *DG = places(bass_, [H * P] * 3 + [P] + [H * T] * 2)
        PN0, PN1, PF0, PF1, CI0, CI1, CX0, CX1 = places(WW, [T] * 2 + [P] * 2 + [H] * 2 + [H * T] * 2)
        PN, PF, CI, CX = (PN0, PN1), (PF0, PF1), (CI0, CI1), (CX0, CX1)

        def product(r, z, m):
            b = m % 2 * (J[r] // 2) + m // 2
            bank = BK[2 + z % CT % 4] if J[r] == 4 else BK[2 + 2 * (z % 2) + b // 4]
            return bank[:, (b % 4) * D:(b % 4 + 1) * D], b

        def counts_sp(sp):
            sp.wait_ge(masks_stored, 64)
            phase(sp, load_db, lambda c: sp.wait_ge(equality_ready, (c + 1) * CT), lambda c, k: None)
            sp.wait_ge(counts_copied, CH)
            for k, p in enumerate((0, P - 1)):
                sp.dma_start(ce_d[k:k + 1].rearrange("o t r -> o (t r)"), CNT[p:p + 1, :]).then_inc(carries_stored, 16)
            sp.wait_ge(carries_stored, 32)
            for k in range(2):
                sp.dma_start(ct[:, k * R:(k + 1) * R], ce_d[k]).then_inc(carry_in_loaded, 16)
            sp.wait_ge(carries_copied, 1)
            for k in range(2):
                sp.dma_start(cc_d[k], cti[:, k * R:(k + 1) * R]).then_inc(carries_stored, 16)
            sp.wait_ge(carries_stored, 64)
            for k in range(2):
                sp.dma_start(CB[:, k * T * R:(k + 1) * T * R],
                             cc_d[k].rearrange("t r -> (t r)").partition_broadcast(P)).then_inc(carry_in_loaded, 16)

        def load_db(c, k):
            nc.sync.dma_start(DB[k], dstf_d[ds(c * CT * P, CT * P)].partition_broadcast(P)).then_inc(dst_loaded[k], 16)

        def phase(sp, load, done, store, dense=None, unit=0, again=None, read=None, early=None, late=False, then=None):
            for k in range(2):
                if early:
                    early(k, k)
                load(k, k)
            if then:
                then()

            def ahead(i, k):
                if not isinstance(i, int) or i < IT - 1:
                    read(i * 2 + k)
                    sp.sem_inc(sp_tick, 1)
                    early(i * 2 + k + 2, k)

            def step(i, k):
                c = i * 2 + k
                more = not isinstance(i, int) or i < IT - 1
                if read and not late:
                    ahead(i, k)
                if dense:
                    dense(unit + i, 2 * k)
                    if not again:
                        dense(unit + i, 2 * k + 1)
                done(c)
                sp.sem_inc(sp_tick, 1)
                store(c, k)
                if again:
                    dense(unit + i, 2 * k + 1)
                    if more:
                        again(i, k)
                if more:
                    load(c + 2, k)

            if late:
                ahead(0, 0)
                ahead(0, 1)
                step(0, 0)
                with sp.Fori(1, IT - 1) as i:
                    ahead(i, 0)
                    step(i - 1, 1)
                    ahead(i, 1)
                    step(i, 0)
                step(IT - 2, 1)
                step(IT - 1, 0)
                step(IT - 1, 1)
                return
            if dense:
                for k in range(2):
                    step(0, k)
            with sp.Fori(1 if dense else 0, IT - 1) as i:
                for k in range(2):
                    step(i, k)
            for k in range(2):
                step(IT - 1, k)

        def edge_sp(sp, dense):
            def load_g(rows_d, c, k):
                a = k * CT * D
                sp.dma_start(three(G[:, a:a + CW]), chunk(rows_d, c)).then_inc(base_loaded[k], 16)

            def carries(r, rows_d, w, to_d):
                v3 = rows_d.rearrange("(t e) f -> t e f", e=P)
                for k, e in enumerate((0, P - 1)):
                    sp.dma_start(UFL[:, k * w:(k + 1) * w], v3[:, e, :]).then_inc(carry_in_loaded, 16)
                if r < 3:
                    dense(DU["C"][r], 0)
                sp.wait_ge(carries_copied, r + 2)
                for k in range(2):
                    sp.dma_start(to_d[k], CIO[:, k * w:(k + 1) * w]).then_inc(carries_stored, 16)
                if r < 3:
                    sp.dma_start(to_d[2], BR[0:T, OFF_B + r * D:OFF_B + (r + 1) * D]).then_inc(carries_stored, 16)
                    dense(DU["C"][r], 1)
                sp.wait_ge(carries_stored, 64 + 48 * min(r + 1, 3) + (32 if r == 3 else 0))

            def stored(upto):
                for k in range(2):
                    sp.wait_ge(results_stored[k], upto * IT * 16)

            for r in range(3):
                def load_src(c, k):
                    if r == 0:
                        sp.wait_ge(rows_stored[k], (c - k) * 8 + 16)
                        sp.sem_inc(sp_tick, 1)
                    load_g(src_rows[r], c, k)

                def load_a(c, k):
                    load_db(c, k)
                    if r == 1:
                        sp.dma_start(three(XR[k]), chunk(xs_d, c)).then_inc(residual_loaded[k], 16)

                def done_a(c):
                    sp.wait_ge(segments_copied, r * NG + (c + 1) * 2)
                    sp.sem_inc(sp_tick, 1)
                    if r == 1:
                        sp.wait_ge(rows_ready, HB_N["A1"] * T + (c + 1) * CT)
                    else:
                        sp.wait_ge(self_taken, r * NG + (c + 1) * 2)

                def store_a(c, k):
                    sp.dma_start(chunk(u_d[r], c), three(UB[k][:, 0:CW])).then_inc(results_stored[k], 16)
                    sp.dma_start(chunk(src_next[r], c), three(HB[k])).then_inc(results_stored[k], 16)

                phase(sp, load_a, done_a, store_a, read=lambda c: sp.wait_ge(rows_transposed, N_A[r] * NG + (c + 1) * 2),
                      early=load_src, late=True,
                      then=(lambda: prelude(dense)) if r == 0 else None)
                stored(ST["A"][r] + 2)
                carries(r, u_d[r], D, cr_d[r])

                if r == 0:
                    for k in range(2):
                        sp.wait_ge(rows_stored[k], 2 * IT * 16)

                def rest_of_unit():
                    for z in range(2, RING):
                        dense(DU["C"][r], z)

                def load_b(c, k):
                    load_g(dst_rows[r], c, k)
                    sp.dma_start(three(UB[k][:, 0:CW]), chunk(u_d[r], c)).then_inc(sums_loaded[k], 16)
                    sp.dma_start(FLc[k], fl_d[:, ds(c * CT * P, CT * P)]).then_inc(sums_loaded[k], 16)
                    sp.dma_start(three(CRc[k][:, 0:CW]), cr_d[r][:, ds(c * CT, CT), :]).then_inc(sums_loaded[k], 16)
                    if r == 1:
                        sp.dma_start(three(XR[k]), chunk(xd_d, c)).then_inc(residual_loaded[k], 16)

                phase(sp, load_b, lambda c: sp.wait_ge(rows_ready, HB_N["B"][r] * T + (c + 1) * CT),
                      lambda c, k: sp.dma_start(chunk(dst_next[r], c), three(HB[k])).then_inc(results_stored[k], 16),
                      dense, DU["B"][r], then=rest_of_unit)
                stored(ST["B"][r] + 1)

            def merged_stored(i, k):
                sp.wait_ge(results_stored[k], (ST["S"] * IT + i + 1) * 16)
                sp.sem_inc(sp_tick, 1)

            phase(sp, lambda c, k: load_g(ls_d, c, k), lambda c: sp.wait_ge(scores_ready, c + 1),
                  lambda c, k: sp.dma_start(chunk(lm_d, c), three(G[:, k * CW:(k + 1) * CW])).then_inc(results_stored[k], 16),
                  dense, DU["S"], merged_stored)
            rest(dense)
            stored(ST["S"] + 1)

            phase(sp, load_db, lambda c: sp.wait_ge(segments_copied, 3 * NG + (c + 1) * 3),
                  lambda c, k: sp.dma_start(chunk(ua_d, c), UB[k].rearrange("p (t f) -> p t f", f=UW)
                                            ).then_inc(results_stored[k], 16),
                  read=lambda c: sp.wait_ge(weighted_ready, c + 1), early=lambda c, k: load_g(lm_d, c, k))
            stored(ST["W"] + 1)
            carries(3, ua_d, UW, cra_d)

            def load_o(c, k):
                load_g(l_d, c, k)
                sp.dma_start(UB[k].rearrange("p (t f) -> p t f", f=UW), chunk(ua_d, c)).then_inc(sums_loaded[k], 16)
                sp.dma_start(FLc[k][0:2, :], fl_d[0:2, ds(c * CT * P, CT * P)]).then_inc(sums_loaded[k], 16)
                sp.dma_start(CRc[k][0:2, :].rearrange("p (t f) -> p t f", f=UW),
                             cra_d[:, ds(c * CT, CT), :]).then_inc(sums_loaded[k], 16)
                sp.dma_start(three(XR[k]), chunk(y_d, c)).then_inc(residual_loaded[k], 16)

            for z in range(RING):
                sp.wait_ge(out_stored[z], len(range(z, NSUB + 1, RING)) * 16)
            phase(sp, load_o, lambda c: sp.wait_ge(rows_ready, HB_N["O"] * T + (c + 1) * CT), lambda c, k: None)

        def relation_sums(g):
            g.wait_ge(counts_taken, 1)
            g.wait_ge(weights_loaded, LOADS * 16)
            cmp3 = cmpb[:, :].rearrange("p (r b) -> p r b", b=NB)
            for b in range(NB):
                term = four(Wr if b == 0 else WrT)
                if b > 1:
                    g.wait_ge(relation_terms, 2 * b - 1)
                g.tensor_tensor(term, bc_mid(bass_[:, b * D:(b + 1) * D], R), bc_in(cmp3[:, :, b], D),
                                ALU.mult).then_inc(relation_terms, 1)
                if b:
                    g.wait_ge(relation_terms, 2 * b)
                    g.tensor_tensor(four(Wr), four(Wr), four(WrT), ALU.add).then_inc(relation_terms, 1)

        def edge_pool(g, node_bound, slot_bound, gate):
            for n, (tab, ld) in enumerate(((h_d, LD["A"][1]), (y_d, LD["A"][2]), (l_d, LD["S"]))):
                if n == 1:
                    relation_sums(g)
                with g.Fori(0, IT) as i:
                    for k in range(2):
                        a = k * CT
                        gate(base_loaded[k], (ld * IT + i + 1) * 16)
                        for j in range(a, a + CT):
                            gate(gathered[j], ((4 + n) * IT + i) * 16)
                        g.tensor_copy(idx_s[:, a:a + CT], slot_i[:, ds(i * SL + a, CT)]).then_inc(index_staged, 1)
                        gate(index_staged, 10 * IT + n * 2 * IT + i * 2 + k + 1)
                        for j in range(a, a + CT):
                            g.indirect_dma_start(
                                out=G[:, j * D:(j + 1) * D], out_offset=None, in_=tab,
                                in_offset=bass.IndirectOffsetOnAxis(ap=idx_s[:, j:j + 1], axis=0),
                                bounds_check=slot_bound, oob_is_err=False).then_inc(gathered[j], 16)
            for j in range(SL):
                g.wait_ge(gathered[j], 7 * IT * 16)
            def self_loops(i, k):
                gate(base_loaded[k], (LD["B"][3] * IT + i + 1) * 16)
                g4 = G[:, k * CW:(k + 1) * CW].rearrange("p (t h d) -> p t h d", h=H, d=HD)
                es = ES[:, :].rearrange("p (h t) -> p t h", t=T)[:, ds((i * 2 + k) * CT, CT), :]
                g.tensor_tensor(g4, g4, es.unsqueeze(3).broadcast_to([P, CT, H, HD]), ALU.mult).then_inc(self_loops_ready, 1)

            def scatter(i, k):
                a = k * CT
                if not isinstance(i, int) or i > 0:
                    for j in range(a, a + CT):
                        gate(scatter_done[j], i * 16)
                g.tensor_copy(idx_s[:, a:a + CT], lead_i[:, ds(i * SL + a, CT)]).then_inc(index_staged, 1)
                gate(index_staged, 16 * IT + i * 2 + k + 1)
                for j in range(a, a + CT):
                    gate(rows_ready, HB_N["O"] * T + i * SL + j + 1)
                    g.indirect_dma_start(
                        out=out, out_offset=bass.IndirectOffsetOnAxis(ap=idx_s[:, j:j + 1], axis=0),
                        in_=HB[k][:, (j - a) * D:(j - a + 1) * D], in_offset=None,
                        bounds_check=node_bound, oob_is_err=False).then_inc(scatter_done[j], 16)

            g.wait_ge(attention_act, 2)
            self_loops(0, 0)
            self_loops(0, 1)
            scatter(0, 0)
            with g.Fori(1, IT) as i:
                self_loops(i, 0)
                scatter(i - 1, 1)
                self_loops(i, 1)
                scatter(i, 0)
            scatter(IT - 1, 1)
            for j in range(SL):
                g.wait_ge(scatter_done[j], IT * 16)

        def carries_pe(pe, r, ufl, w, bank):
            pe.wait_ge(carry_in_loaded, 32 if r < 0 else 96 + 32 * r)
            nc.tensor.matmul(bank[0:T, 0:w], mk_in[:, :], ufl[:, w:2 * w], start=True, stop=True)
            nc.tensor.matmul(bank[0:T, w:2 * w], mk_out[:, :], ufl[:, 0:w], start=True, stop=True).then_inc(carries_made, 1)

        def relation_weights(pe):
            pe.wait_ge(relation_terms, 2 * NB - 1)
            for r in range(R):
                last = nc.tensor.transpose(BK[r // 4][:, (r % 4) * D:(r % 4 + 1) * D],
                                           Wr[:, r * D:(r + 1) * D], ident[:, :])
            last.then_inc(weight_products, 1)
            pe.wait_ge(act_weights, 4)
            for r in range(R):
                last = nc.tensor.matmul(BK[2 + r // 4][:, (r % 4) * D:(r % 4 + 1) * D],
                                        WrT[:, r * D:(r + 1) * D], gw[:, :], start=True, stop=True)
            last.then_inc(weight_products, 1)
            pe.wait_ge(act_weights, 6)

        def edge_counts(pe):

            def count(i, s):
                if (a := at(i, s, SL, T)):
                    it, z, q = a
                    k, j = z // CT, z % CT
                    pe.wait_ge(equality_ready, q + 1)
                    if j == 0 and (not isinstance(it, int) or it >= 1):
                        pe.wait_ge(counts_copied, it * 2 + k - 1)
                    m = nc.tensor.matmul(BK[2 + k][:, j * R:(j + 1) * R], EQ[z % CT % 4][:, :], OH[:, ds(q * R, R)],
                                         start=True, stop=True).then_inc(counts_made, 1)

            run(pe, IT, SL, 0, 0, count)

        def count_carries(pe):
            pe.wait_ge(carry_masks, 1)
            carries_pe(pe, -1, ct, R, BK[6])

        def edge_pe(pe, dense, rows):
            def dense_read(u):
                pe.wait_ge(yT_copied, u * RING - 1)
                pe.wait_ge(hT_ready, u * RING + 1)
                pe.wait_ge(pre_y_ready, u * RING)
                pe.wait_ge(z_ready, u * RING - 2)

            def transpose(n, i, s, loaded):
                if not (a := at(i, s, GS, NG)):
                    return
                it, z, q = a
                k, g, j0, w, z0 = group_of(z)
                loaded(it, k, g, z0, w)
                if past(q, 2):
                    pe.wait_ge(rowsT_copied, n * NG + q - 1)
                for t in range(w):
                    last = nc.tensor.transpose(BK[g][:, t * D:(t + 1) * D], G[:, (z0 + t) * D:(z0 + t + 1) * D], ident[:, :])
                last.then_inc(rows_transposed, 1)

            for r in range(3):
                if r == 2:
                    pe.wait_ge(rowsT_copied, 4 * NG)
                    pe.wait_ge(slots_added, 2 * NG)
                    relation_weights(pe)
                dense_read(DU["C"][r])

                def loaded_a(it, k, g, z0, w):
                    if r > 0:
                        for t in range(z0, z0 + w):
                            pe.wait_ge(gathered[t], ((3 + r) * IT + it + 1) * 16)
                    elif g == 0:
                        pe.wait_ge(base_loaded[k], (LD["A"][0] * IT + it + 1) * 16)

                def a_phase(i, s):
                    if s == -1:
                        return transpose(N_A[r], i, 0, loaded_a)
                    if (a := at(i, s, SL, T)):
                        it, z, q = a
                        k, j = z // CT, z % CT
                        gs = 2 * k + (j >= GT[1])
                        _, g, j0, w, _ = group_of(gs)
                        qg = it * GS + gs
                        zt = ZT[g][:, (j - j0) * D:(j - j0 + 1) * D]
                        if j == j0:
                            transpose(N_A[r], i, gs + 1, loaded_a)
                            pe.wait_ge(rowsT_copied, N_A[r] * NG + qg + 1)
                        nb = J[r] // 4
                        back = 3 if nb == 1 else 2
                        if past(q, back):
                            pe.wait_ge(terms_added, sum(CM[:r]) * T + (q - back + 1) * CM[r])
                        for h in range(nb):
                            bank = BK[2 + j % 4] if nb == 1 else BK[2 + 2 * (z % 2) + h]
                            last = nc.tensor.matmul(bank[:, :], zt, V[r][:, h * 4 * D:(h + 1) * 4 * D],
                                                    start=True, stop=r > 0)
                            if r == 0:
                                last = nc.tensor.matmul(bank[:, :], ones3[:, :], B3[:, OFF_BV:OFF_BV + B * D],
                                                        start=False, stop=True)
                            if h < nb - 1:
                                last.then_inc(first_bank, 1)
                        last.then_inc(products_made, 1)
                        if j == j0:
                            pe.wait_ge(self_taken, r * NG + qg)
                            rows(BK[6], w, OFF_B + r * D, ZT[g], M[r]).then_inc(self_made, 1)
                    if (a := at(i, s - 2, SL, T)):
                        it, z, q = a
                        k, j = z // CT, z % CT
                        gs = 2 * k + (j >= GT[1])
                        _, g, j0, w, _ = group_of(gs)
                        pe.wait_ge(terms_added, sum(CM[:r]) * T + (q + 1) * CM[r])
                        if j == j0:
                            pe.wait_ge(segments_copied, r * NG + it * GS + gs)
                        u = BK[7][:, (j - j0) * D:(j - j0 + 1) * D]
                        nc.tensor.matmul(u, EQ[z % CT % 4][:, :], MS[z % CT % 4][:, 0:D], start=True, stop=True).then_inc(segments_made, 1)

                run(pe, IT, SL, 1, 2, a_phase)
                pe.wait_ge(segments_copied, (r + 1) * NG)
                pe.wait_ge(self_taken, (r + 1) * NG)
                pe.wait_ge(terms_added, sum(CM[:r + 1]) * T)
                dense(DU["C"][r], 0)
                carries_pe(pe, r, UFL, D, BK[0])
                for z in range(1, RING):
                    dense(DU["C"][r], z)
                pe.wait_ge(carries_copied, r + 2)

                def loaded_b(it, k, g, z0, w):
                    if g == 0:
                        pe.wait_ge(base_loaded[k], (LD["B"][r] * IT + it + 1) * 16)

                def b_phase(i, s):
                    transpose(N_B[r], i, s + 1, loaded_b)
                    if (a := at(i, s, GS, NG)):
                        it, z, q = a
                        k, g, j0, w, _ = group_of(z)
                        pe.wait_ge(rowsT_copied, N_B[r] * NG + q + 1)
                        if g == 0:
                            pe.wait_ge(sums_loaded[k], (r * IT + it + 1) * 48)
                        if past(q, 2):
                            pe.wait_ge(slots_added, r * NG + q - 1)
                        for t in range(w):
                            j, o = j0 + t, BK[2 + g][:, t * D:(t + 1) * D]
                            nc.tensor.matmul(o, ZT[g][:, t * D:(t + 1) * D], M[r][:, :], start=True, stop=False)
                            last = nc.tensor.matmul(o, FLc[k][:, j * P:(j + 1) * P], CRc[k][:, j * D:(j + 1) * D],
                                                    start=False, stop=True)
                        last.then_inc(slots_made, 1)
                        dense(DU["B"][r] + it, z)

                run(pe, IT, GS, 1, 0, b_phase)

            dense_alone(pe, dense)
            rest(dense)
            for done in (yT_copied, hT_ready, pre_y_ready, z_ready):
                pe.wait_ge(done, NSUB + 1)

            pe.wait_ge(attention_dve, 1)
            for h in range(H):
                last = nc.tensor.transpose(BK[4][0:T, h * P:(h + 1) * P], AS[:, h * T:(h + 1) * T], ident[:, :])
            nc.tensor.transpose(BK[7][0:T, 0:T], mk_in[:, :], ident[0:T, 0:T])
            nc.tensor.transpose(BK[7][0:T, T:2 * T], mk_out[:, :], ident[0:T, 0:T]).then_inc(attention_pe, 1)
            pe.wait_ge(attention_dve, 2)
            for k in range(2):
                last = nc.tensor.matmul(BK[5 + k][0:T, 0:H * T], ones[0:T, 0:T], DG[k], start=True, stop=True)
            last.then_inc(attention_pe, 1)
            pe.wait_ge(attention_dve, 3)
            for h in range(H):
                last = nc.tensor.transpose(BK[3][:, h * T:(h + 1) * T], SMX[:, h * P:(h + 1) * P], ident[0:T, 0:T])
            last.then_inc(attention_pe, 1)

            def w_phase(i, k):
                c = i * 2 + k
                pe.wait_ge(weighted_ready, c + 1)
                if not isinstance(i, int) or i >= 1:
                    pe.wait_ge(segments_copied, 3 * NG + (c - 1) * 3)
                for g in range(3):
                    for j in range(GO[g], GO[g + 1]):
                        o = (j - GO[g]) * UW
                        last = nc.tensor.matmul(BK[1 + 4 * k + g][:, o:o + UW], DB[k][:, j * P:(j + 1) * P],
                                                MG[k][:, j * UW:(j + 1) * UW], start=True, stop=True)
                    last.then_inc(segments_made, 1)

            run(pe, IT, 2, 0, 0, w_phase)
            carries_pe(pe, 3, UFL, UW, BK[0])

            def o_phase(i, k):
                c = i * 2 + k
                first = isinstance(i, int) and i == 0
                pe.wait_ge(sums_loaded[k], (3 * IT + i + 1) * 48)
                for g in range(3):
                    if not first or k:
                        pe.wait_ge(slots_added, 3 * NG + (c - 1) * 3 + g + 1)
                    for j in range(GO[g], GO[g + 1]):
                        o = (j - GO[g]) * UW
                        last = nc.tensor.matmul(BK[1 + g][:, o:o + UW], FLc[k][0:2, j * P:(j + 1) * P],
                                                CRc[k][0:2, j * UW:(j + 1) * UW], start=True, stop=True)
                    last.then_inc(slots_made, 1)
                pe.wait_ge(residual_loaded[k], (2 * IT + i + 1) * 16)
                if not first:
                    pe.wait_ge(residual_taken, c - 1)
                for n in range(2):
                    a0, w = GT[n] * D, (GT[n + 1] - GT[n]) * D
                    bank = BK[4 + 2 * k + n][:, 0:w]
                    nc.tensor.matmul(bank, ident[:, :], XR[k][:, a0:a0 + w], start=True, stop=False)
                    last = nc.tensor.matmul(bank, ones3[:, :], bc_mid(B3[:, OFF_GB:OFF_GB + D], w // D),
                                            start=False, stop=True)
                last.then_inc(residual_made, 1)

            pe.wait_ge(carries_copied, 5)
            pe.wait_ge(segments_copied, 3 * NG + CH * 3)
            run(pe, IT, 2, 0, 0, o_phase)

        def carries_act(act, r, bank, w, to):
            act.wait_ge(carries_made, r + 2)
            nc.scalar.copy(to[:, 0:2 * w], bank[0:T, 0:2 * w]).then_inc(carries_copied, 1)

        def edge_counts_act(act):
            with act.Fori(0, IT) as i:
                for k in range(2):
                    act.wait_ge(counts_made, (i * 2 + k + 1) * CT)
                    act.sem_inc(act_tick, 1)
                    nc.scalar.copy(CNT[:, ds((i * 2 + k) * CT * R, CT * R)], BK[2 + k][:, 0:CT * R]).then_inc(counts_copied, 1)


        def edge_act(act, dense):

            def transposed(n, i, s):
                if (a := at(i, s, GS, NG)):
                    _, z, q = a
                    _, g, _, w, _ = group_of(z)
                    act.wait_ge(rows_transposed, n * NG + q + 1)
                    nc.scalar.copy(ZT[g][:, 0:w * D], BK[g][:, 0:w * D]).then_inc(rowsT_copied, 1)

            def deviation(n, z):
                k = z // CT
                act.wait_ge(stats_ready, n)
                nc.scalar.activation(sd[:, k * CT:(k + 1) * CT], mv[:, 2 * k * CT + 1:2 * (k + 1) * CT:2],
                                     ACT.Sqrt, bias=eps[:, 0:1]).then_inc(deviations_ready, 1)

            def normalize(n, k, t0=0, t1=CT):
                act.wait_ge(shift_ready, n)
                for t in range(t0, t1):
                    o, w = k * CT + t, HB[k][:, t * D:(t + 1) * D]
                    nc.scalar.activation(w, w, ACT.Identity, bias=nb[:, o:o + 1],
                                         scale=rs[:, o:o + 1]).then_inc(rows_ready, 1)

            def out_free(it, k, count, before):
                if not isinstance(it, int) or it >= 1:
                    act.wait_ge(results_stored[k], (before * IT + count * it) * 16)

            for r in range(3):
                if r == 2:
                    act.wait_ge(weight_products, 4)
                    for k in range(2):
                        nc.scalar.copy(WrT[:, k * 4 * D:(k + 1) * 4 * D], BK[k][:, :]).then_inc(act_weights, 1)
                    act.wait_ge(weight_products, 5)
                    for k in range(2):
                        nc.scalar.copy(V[2][:, k * 4 * D:(k + 1) * 4 * D], BK[2 + k][:, :]).then_inc(act_weights, 1)

                def a_phase(i, s):
                    if s == -1:
                        return transposed(N_A[r], i, 0)
                    if (a := at(i, s, SL, T)):
                        it, z, q = a
                        k, j = z // CT, z % CT
                        if r < 2:
                            act.wait_ge(products_made, r * T + q + 1)
                        else:
                            act.wait_ge(first_bank, q + 1)
                        act.sem_inc(act_tick, 1)
                        if past(q, 3):
                            act.wait_ge(segments_made, r * T + q - 2)
                            act.sem_inc(act_tick, 1)
                        for m in range(2):
                            if r == 2 and m == 1:
                                act.wait_ge(products_made, r * T + q + 1)
                                act.sem_inc(act_tick, 1)
                            pj, b = product(r, z, m)
                            last = nc.scalar.activation((MS, MT)[m][z % CT % 4][:, 0:D], pj, ACT.Copy,
                                                        scale=C[r][:, ds(q * J[r] + b, 1)])
                        last.then_inc(first_terms, 1)
                        if j in GT:
                            gs = 2 * k + (j >= GT[1])
                            _, g, j0, w, _ = group_of(gs)
                            transposed(N_A[r], i, gs + 1)
                            if r != 1:
                                act.wait_ge(self_made, r * NG + it * GS + gs + 1)
                                if j == 0:
                                    out_free(it, k, 2, ST["A"][r])
                                nc.scalar.activation(HB[k][:, j * D:(j + w) * D], BK[6][:, 0:w * D],
                                                     ACT.Relu if r == 0 else ACT.Copy).then_inc(self_taken, 1)
                    if (a := at(i, s - 2, SL, T)) and a[1] % CT + 1 in GT:
                        it, z, q = a
                        k, j = z // CT, z % CT
                        _, g, j0, w, _ = group_of(2 * k + (j >= GT[1]))
                        act.wait_ge(segments_made, r * T + q + 1)
                        if g == 0:
                            out_free(it, k, 2, ST["A"][r])
                        nc.scalar.copy(UB[k][:, j0 * D:(j0 + w) * D], BK[7][:, 0:w * D]).then_inc(segments_copied, 1)
                    if r == 1 and (a := at(i, s, SL, T)) and a[1] % CT == CT - 1:
                        deviation(a[0] * 2 + a[1] // CT + 1, a[1])
                    if r == 1 and s % CT < 4 and (a := at(i, s - CT, SL, T)):
                        j = a[1] % CT
                        normalize(a[0] * 2 + a[1] // CT + 1, a[1] // CT, 2 * j, min(2 * j + 2, CT))

                run(act, IT, SL, 1, 4 if r == 1 else 2, a_phase)
                dense(DU["C"][r], 0)
                carries_act(act, r, BK[0], D, CIO)
                for z in range(1, RING):
                    dense(DU["C"][r], z)

                def b_phase(i, s):
                    if r == 0 and (a := at(i, s - 1, GS, NG)):
                        it, z, q = a
                        k, g, j0, w, _ = group_of(z)
                        act.wait_ge(slots_added, q + 1)
                        h = HB[k][:, j0 * D:(j0 + w) * D]
                        nc.scalar.activation(h, h, ACT.Relu).then_inc(rows_ready, w)
                    transposed(N_B[r], i, s + 1)
                    if (a := at(i, s, GS, NG)):
                        it, z, q = a
                        n = CH + it * 2 + z // 2 + 1
                        if r == 1 and z % 2 == 1:
                            dense(DU["B"][r] + it, z, lambda: deviation(n, z // 2 * CT))
                        else:
                            dense(DU["B"][r] + it, z)

                run(act, IT, GS, 1, 1, b_phase)

            dense_alone(act, dense)
            rest(dense)

            act.wait_ge(attention_pe, 1)
            nc.scalar.copy(SMX, BK[4][0:T, :]).then_inc(attention_act, 1)
            act.wait_ge(attention_dve, 4)
            nc.scalar.activation(EA[:, :], EA[:, :], ACT.Exp)
            nc.scalar.activation(ES[:, :], ES[:, :], ACT.Exp).then_inc(attention_act, 1)

            def w_phase(i, k):
                for g in range(3):
                    act.wait_ge(segments_made, 3 * T + (i * 2 + k) * 3 + g + 1)
                    if g == 0:
                        out_free(i, k, 1, ST["W"])
                    w = slice(GO[g] * UW, GO[g + 1] * UW)
                    nc.scalar.copy(UB[k][:, w], BK[1 + 4 * k + g][:, 0:w.stop - w.start]).then_inc(segments_copied, 1)

            run(act, IT, 2, 0, 0, w_phase)
            carries_act(act, 3, BK[0], UW, CIO)

            def o_phase(i, k):
                deviation(2 * CH + i * 2 + k + 1, k * CT)
                normalize(CH + i * 2 + k + 1, k)

            run(act, IT, 2, 0, 0, o_phase)

        class LoopChain:

            def __init__(self, v):
                self.v, self.base, self.n, self.per = v, 0, 0, 0

            def loop(self, per):
                self.base += self.per * IT
                self.per = per

            def start(self, i, s):
                if s == 0:
                    self.i, self.n = i, 0

            def __call__(self, ins):
                self.n += 1
                assert self.n <= self.per
                ins.then_inc(loop_order, 1)
                self.v.wait_ge(loop_order, self.i * self.per + self.base + self.n)

        def dense_alone(eng, dense):
            with eng.Fori(0, IT - 1) as i:
                for z in range(RING):
                    dense(DU["S"] + i, z)
            for z in range(RING):
                dense(UNITS - 1, z)

        def equal(v, n, a, done):
            it, z, q = a
            k, j = z // CT, z % CT
            if j == 0:
                v.wait_ge(dst_loaded[k], (n * IT + it + 1) * 16)
            if past(q, 3):
                v.wait_ge(*done(q - 2))
            nc.vector.tensor_scalar(EQ[z % CT % 4][:, :], DB[k][:, j * P:(j + 1) * P], EC[:, ds(q, 1)], None,
                                    ALU.is_equal).then_inc(equality_ready, 1)

        def count_tiles(v):
            run(v, IT, SL, 0, 0, lambda i, s: equal(v, 0, at(i, s, SL, T), lambda n: (counts_made, n)))

        def coefficients(v, link):
            v.wait_ge(carry_in_loaded, 64)
            q13, cnt3 = (a[:, :].rearrange("p (t r) -> p t r", r=R) for a in (q1, CNT))
            for k in range(2):
                link(nc.vector.tensor_tensor(q13, CB[:, k * T * R:(k + 1) * T * R].rearrange("p (t r) -> p t r", r=R),
                                             bc_in(eqc[:, k * T:(k + 1) * T], R), ALU.mult))
                link(nc.vector.tensor_tensor(CNT[:, :], CNT[:, :], q1[:, :], ALU.add))
            v.sem_inc(counts_taken, 1)
            link(nc.vector.tensor_scalar(q1[:, :], CNT[:, :], 1.0, None, ALU.max))
            link(nc.vector.reciprocal(q1[:, :], q1[:, :]))
            nc.vector.memset(nz[:, :], 1.0)
            link(nc.vector.memset(nrm[:, :], 0.0))
            for r in reversed(range(R)):
                link(nc.vector.scalar_tensor_tensor(out=wq[:, :], in0=cnt3[:, :, r], scalar=0.0, in1=nz[:, :],
                                                    op0=ALU.is_gt, op1=ALU.mult))
                nc.vector.tensor_tensor(nz[:, :], nz[:, :], wq[:, :], ALU.subtract)
                link(nc.vector.tensor_tensor(q2[:, 0:T], wq[:, :], q13[:, :, r], ALU.mult))
                link(nc.vector.tensor_tensor(nrm[:, :], nrm[:, :], q2[:, 0:T], ALU.add))
            block_coefficients(link, 0)

        def block_coefficients(link, l):
            for b in range(B):
                w = wcb[:, l * R * B:(l + 1) * R * B].rearrange("p (r b) -> p r b", b=B)[:, :, b]
                q23 = q2[:, :].rearrange("p (t r) -> p t r", r=R)
                link(nc.vector.tensor_tensor(q23, OH[:, :].rearrange("p (t r) -> p t r", r=R), bc_mid(w, T),
                                             ALU.mult))
                link(nc.vector.tensor_reduce(wq[:, :], q23, AX.X, ALU.add))
                link(nc.vector.tensor_tensor(C[l][:, :].rearrange("p (t b) -> p t b", b=B)[:, :, b],
                                             wq[:, :], nrm[:, :], ALU.mult))

        def edge_dve(v, link, dense):
            lc = LoopChain(v)

            def norm_chunk(z, n, rows_, own=False):
                k = z // CT
                for t in range(CT):
                    o = k * CT + t
                    last = nc.vector.bn_stats(st[:, 6 * o:6 * o + 6], rows_[:, t * D:(t + 1) * D])
                lc(last)
                v.sem_inc(dve_tick, 1)
                for t in range(CT):
                    o = k * CT + t
                    last = nc.vector.bn_aggr(mv[:, 2 * o:2 * o + 2], st[:, 6 * o:6 * o + 6])
                last.then_inc(stats_ready, 1)
                v.wait_ge(deviations_ready, n)
                lc(nc.vector.reciprocal(rs[:, k * CT:(k + 1) * CT], sd[:, k * CT:(k + 1) * CT]))
                if own:
                    for t in range(CT):
                        o, w = k * CT + t, rows_[:, t * D:(t + 1) * D]
                        nc.vector.tensor_scalar(w, w, mv[:, 2 * o:2 * o + 1], rs[:, o:o + 1], ALU.subtract,
                                                ALU.mult).then_inc(rows_ready, 1)
                    return
                nc.vector.scalar_tensor_tensor(
                    out=nb[:, k * CT:(k + 1) * CT], in0=mv[:, 2 * k * CT:2 * (k + 1) * CT:2], scalar=-1.0,
                    in1=rs[:, k * CT:(k + 1) * CT], op0=ALU.mult, op1=ALU.mult).then_inc(shift_ready, 1)

            def scores(rows_, m, c, k, to):
                lc(nc.vector.tensor_tensor(three(W1[:, 0:CW]), three(rows_), bc_mid(attb[:, m * D:(m + 1) * D], CT),
                                           ALU.mult))
                rd = red[k][:, m * CT * H:(m + 1) * CT * H]
                lc(nc.vector.tensor_reduce(rd, W1[:, 0:CW].rearrange("p (a d) -> p a d", d=HD), AX.X, ALU.add))
                return nc.vector.tensor_scalar(to.rearrange("p (h t) -> p t h", t=T)[:, ds(c * CT, CT), :],
                                               rd.rearrange("p (t h) -> p t h", h=H), 1.0, None, ALU.mult)

            def out_free(it, k, count, before):
                if not isinstance(it, int) or it >= 1:
                    v.wait_ge(results_stored[k], (before * IT + count * it) * 16)

            for r in range(3):
                lc.loop(4 if r == 1 else 0)

                def a_phase(i, s):
                    if r == 1:
                        lc.start(i, s)
                    a = at(i, s, SL, T)
                    it, z, q = a
                    k, j = z // CT, z % CT
                    equal(v, 1 + r, a, lambda n: (segments_made, r * T + n))
                    v.wait_ge(products_made, r * T + q + 1)
                    n = J[r]
                    v.wait_ge(first_terms, r * T + q + 1)
                    v.sem_inc(dve_tick, 1)
                    cm = sum(CM[:r]) * T + q * CM[r]
                    for m in range(2, n):
                        pj, b = product(r, z, m)
                        o = (MS, MT)[m % 2][z % CT % 4][:, 0:D]
                        if m >= 4:
                            v.wait_ge(terms_added, cm + m - 3)
                        nc.vector.scalar_tensor_tensor(out=o, in0=pj, scalar=C[r][:, ds(q * n + b, 1)], in1=o,
                                                       op0=ALU.mult, op1=ALU.add).then_inc(terms_added, 1)
                    v.wait_ge(terms_added, cm + n - 2)
                    nc.vector.tensor_tensor(MS[z % CT % 4][:, 0:D], MS[z % CT % 4][:, 0:D], MT[z % CT % 4][:, :],
                                            ALU.add).then_inc(terms_added, 1)
                    if r == 1:
                        if j in GT:
                            gs = 2 * k + (j >= GT[1])
                            _, g, _, w, _ = group_of(gs)
                            v.wait_ge(self_made, r * NG + it * GS + gs + 1)
                            if j == 0:
                                v.wait_ge(residual_loaded[k], (it + 1) * 16)
                                out_free(it, k, 2, ST["A"][r])
                            nc.vector.scalar_tensor_tensor(
                                out=HB[k][:, j * D:(j + w) * D], in0=BK[6][:, 0:w * D], scalar=0.0,
                                in1=XR[k][:, j * D:(j + w) * D], op0=ALU.max, op1=ALU.add).then_inc(self_taken, 1)
                        if j == CT - 1:
                            v.wait_ge(self_taken, r * NG + it * GS + 2 * k + 2)
                            norm_chunk(z, it * 2 + k + 1, HB[k])

                run(v, IT, SL, 0, 0, a_phase)
                if r == 0:
                    block_coefficients(link, 1)
                    link(nc.vector.tensor_tensor(C[2][:, :], OH[:, :], q1[:, :], ALU.mult))
                for z in range(RING):
                    dense(DU["C"][r], z)
                lc.loop((0, 6, 8)[r])

                def b_phase(i, s):
                    if r:
                        lc.start(i, s)
                    it, z, q = at(i, s, GS, NG)
                    k, g, j0, w, _ = group_of(z)
                    v.wait_ge(slots_made, r * NG + q + 1)
                    if g == 0:
                        v.wait_ge(sums_loaded[k], (r * IT + it + 1) * 48)
                        out_free(it, k, 1, ST["B"][r])
                    nc.vector.tensor_tensor(HB[k][:, j0 * D:(j0 + w) * D], BK[2 + g][:, 0:w * D],
                                            UB[k][:, j0 * D:(j0 + w) * D], ALU.add).then_inc(slots_added, 1)
                    if g == 1 and r == 1:
                        v.wait_ge(slots_added, r * NG + q + 1)
                        v.wait_ge(residual_loaded[k], (IT + it + 1) * 16)
                        lc(nc.vector.scalar_tensor_tensor(out=HB[k], in0=HB[k], scalar=0.0, in1=XR[k],
                                                          op0=ALU.max, op1=ALU.add))
                        norm_chunk(k * CT, CH + it * 2 + k + 1, HB[k], own=True)
                    if g == 1 and r == 2:
                        v.wait_ge(slots_added, r * NG + q + 1)
                        scores(HB[k], 0, it * 2 + k, k, AD[:, 0:H * T])
                        scores(HB[k], 1, it * 2 + k, k, AD[:, H * T:2 * H * T]).then_inc(rows_ready, CT)
                    dense(DU["B"][r] + it, z)

                run(v, IT, GS, 0, 0, b_phase)

            lc.loop(4)

            def s_phase(i, k):
                if k == 0:
                    lc.start(i, 0)
                dense(DU["S"] + i, 2 * k)
                for j in range(k * CT, (k + 1) * CT):
                    v.wait_ge(gathered[j], (6 * IT + i + 1) * 16)
                scores(G[:, k * CW:(k + 1) * CW], 0, i * 2 + k, k, AS[:, :]).then_inc(scores_ready, 1)
                dense(DU["S"] + i, 2 * k + 1)

            with v.Fori(0, IT - 1) as i:
                for k in range(2):
                    s_phase(i, k)
            for k in range(2):
                s_phase(IT - 1, k)
            rest(dense)

            hT3 = lambda a: a.rearrange("p (h t) -> p h t", t=T)
            v.wait_ge(scores_ready, CH)
            link(nc.vector.tensor_tensor(ES[:, :], AD[:, 0:H * T], AD[:, H * T:2 * H * T], ALU.add))
            link(nc.vector.scalar_tensor_tensor(out=ES[:, :], in0=ES[:, :], scalar=SLOPE, in1=ES[:, :],
                                                op0=ALU.mult, op1=ALU.max))
            link(nc.vector.tensor_tensor(AS[:, :], AS[:, :], AD[:, H * T:2 * H * T], ALU.add))
            nc.vector.tensor_tensor(wq[:, :], col(0), col(1), ALU.is_equal)
            link(nc.vector.scalar_tensor_tensor(out=AS[:, :], in0=AS[:, :], scalar=SLOPE, in1=AS[:, :],
                                                op0=ALU.mult, op1=ALU.max))
            nc.vector.scalar_tensor_tensor(out=hT3(AS[:, :]), in0=bc_mid(wq[:, :], H), scalar=NEG, in1=hT3(AS[:, :]),
                                           op0=ALU.mult, op1=ALU.add).then_inc(attention_dve, 1)
            v.wait_ge(attention_act, 1)
            v.wait_ge(results_stored[0], (ST["S"] + 1) * IT * 16)
            v.wait_ge(results_stored[1], (ST["S"] + 1) * IT * 16)
            m3, f3, b3 = (a.rearrange("t (h e) -> t h e", e=P) for a in (SMX, TF, TB))
            d = 1
            while d < P:
                w = P - d
                link(nc.vector.tensor_tensor(pen[:, 0:w], ef[:, d:P], ef[:, 0:w], ALU.not_equal))
                link(nc.vector.tensor_scalar(pen[:, 0:w], pen[:, 0:w], NEG, None, ALU.mult))
                nc.vector.tensor_tensor(f3[:, :, 0:w], m3[:, :, 0:w], bc_mid(pen[:, 0:w], H), ALU.add)
                link(nc.vector.tensor_tensor(b3[:, :, 0:w], m3[:, :, d:P], bc_mid(pen[:, 0:w], H), ALU.add))
                link(nc.vector.tensor_tensor(m3[:, :, d:P], m3[:, :, d:P], f3[:, :, 0:w], ALU.max))
                link(nc.vector.tensor_tensor(m3[:, :, 0:w], m3[:, :, 0:w], b3[:, :, 0:w], ALU.max))
                d *= 2
            for k, e in enumerate((P - 1, 0)):
                nc.vector.tensor_scalar(PN[k], BK[7][0:T, k * T:(k + 1) * T], 1.0, -NEG, ALU.subtract, ALU.mult)
                nc.vector.tensor_scalar(PF[k], fle[:, k * P:(k + 1) * P], 1.0, -NEG, ALU.subtract, ALU.mult)
                last = nc.vector.tensor_tensor(hT3(DG[k]), bc_mid(ident[0:T, 0:T], H), bc_in(m3[:, :, e], T), ALU.mult)
            last.then_inc(attention_dve, 1)
            v.wait_ge(attention_pe, 2)
            for k in range(2):
                link(nc.vector.tensor_tensor(hT3(CX[k]), hT3(BK[5 + k][0:T, 0:H * T]), bc_mid(PN[k], H), ALU.add))
                link(nc.vector.tensor_reduce(CI[k], hT3(CX[k]), AX.X, ALU.max))
                link(nc.vector.tensor_tensor(f3, bc_in(CI[k], P), bc_mid(PF[k], H), ALU.add))
                last = nc.vector.tensor_tensor(m3, m3, f3, ALU.max)
                if k == 0:
                    link(last)
            last.then_inc(attention_dve, 1)
            v.wait_ge(attention_pe, 3)
            link(nc.vector.tensor_tensor(MX[:, :], BK[3][:, 0:H * T], ES[:, :], ALU.max))
            nc.vector.tensor_tensor(EA[:, :], AS[:, :], MX[:, :], ALU.subtract)
            nc.vector.tensor_tensor(ES[:, :], ES[:, :], MX[:, :], ALU.subtract).then_inc(attention_dve, 1)
            v.wait_ge(attention_act, 2)

            def w_phase(i, k):
                c = i * 2 + k
                v.wait_ge(dst_loaded[k], (4 * IT + i + 1) * 16)
                v.sem_inc(dve_tick, 1)
                db = DB[k].rearrange("p (t e) -> p t e", e=P)
                nc.vector.tensor_tensor(db, db, bc_in(col(0)[:, ds(c * CT, CT)], P), ALU.is_equal)
                v.wait_ge(base_loaded[k], (LD["W"] * IT + i + 1) * 16)
                if not isinstance(i, int) or i >= 1:
                    v.wait_ge(segments_made, 3 * T + (c - 1) * 3)
                v.sem_inc(dve_tick, 1)
                e = EA[:, :].rearrange("p (h t) -> p t h", t=T)[:, ds(c * CT, CT), :]
                m3 = MG[k].rearrange("p (t f) -> p t f", f=UW)
                nc.vector.tensor_tensor(m3[:, :, 0:D].rearrange("p t (h d) -> p t h d", d=HD),
                                        G[:, k * CW:(k + 1) * CW].rearrange("p (t h d) -> p t h d", h=H, d=HD),
                                        e.unsqueeze(3).broadcast_to([P, CT, H, HD]), ALU.mult)
                nc.vector.tensor_scalar(m3[:, :, D:UW], e, 1.0, None, ALU.mult).then_inc(weighted_ready, 1)

            run(v, IT, 2, 0, 0, w_phase)
            lc.loop(12)

            def o_phase(it, k):
                lc.start(it, k)
                c = it * 2 + k
                v.wait_ge(sums_loaded[k], (3 * IT + it + 1) * 48)
                for g in range(3):
                    w = slice(GO[g] * UW, GO[g + 1] * UW)
                    v.wait_ge(slots_made, 3 * NG + c * 3 + g + 1)
                    nc.vector.tensor_tensor(UB[k][:, w], BK[1 + g][:, 0:w.stop - w.start], UB[k][:, w],
                                            ALU.add).then_inc(slots_added, 1)
                if not isinstance(it, int) or it >= 1:
                    for t in range(k * CT, (k + 1) * CT):
                        v.wait_ge(scatter_done[t], it * 16)
                u3 = UB[k].rearrange("p (t f) -> p t f", f=UW)
                h3 = HB[k].rearrange("p (a d) -> p a d", d=HD)
                es = ES[:, :].rearrange("p (h t) -> p t h", t=T)[:, ds(c * CT, CT), :]
                rd = red[k][:, 0:CT * H]
                v.wait_ge(slots_added, 3 * NG + (c + 1) * 3)
                lc(nc.vector.tensor_tensor(rd.rearrange("p (t h) -> p t h", h=H), u3[:, :, D:UW], es, ALU.add))
                nc.vector.reciprocal(rd, rd)
                v.wait_ge(self_loops_ready, c + 1)
                lc(nc.vector.tensor_tensor(three(HB[k]), three(G[:, k * CW:(k + 1) * CW]), u3[:, :, 0:D], ALU.add))
                lc(nc.vector.tensor_tensor(h3, h3, bc_in(rd, HD), ALU.mult))
                v.wait_ge(residual_made, c + 1)
                for n in range(2):
                    w = slice(GT[n] * D, GT[n + 1] * D)
                    last = nc.vector.tensor_tensor(HB[k][:, w], HB[k][:, w], BK[4 + 2 * k + n][:, 0:w.stop - w.start], ALU.add)
                lc(last)
                v.sem_inc(residual_taken, 1)
                norm_chunk(k * CT, 2 * CH + c + 1, HB[k])

            run(v, IT, 2, 0, 0, o_phase)
            assert lc.n == 12

        LE = T * P - P

        @block.sync
        def _(sp):
            sp.wait_ge(edge_tiles_set, 1)
            for k, a in enumerate((dst, src, etype)):
                sp.dma_start(ei[0:T - 1, k * P:(k + 1) * P],
                             a[0:LE].rearrange("(t e) -> t e", e=P)).then_inc(edges_loaded, 16)
                sp.dma_start(ei[T - 1:T, k * P:k * P + TAIL], a[LE:E].unsqueeze(0)).then_inc(edges_loaded, 16)
            sp.dma_start(ei[0:1, 3 * P + 1:4 * P], dst[0:P - 1].unsqueeze(0)).then_inc(edges_loaded, 16)
            sp.dma_start(ei[1:T - 1, 3 * P:4 * P],
                         dst[P - 1:LE - 1].rearrange("(t e) -> t e", e=P)).then_inc(edges_loaded, 16)
            sp.dma_start(ei[T - 1:T, 3 * P:3 * P + TAIL + 1], dst[LE - 1:E].unsqueeze(0)).then_inc(edges_loaded, 16)
            sp.wait_ge(edge_prep, 1)
            sp.dma_start(dstf_d.rearrange("(t e) -> t e", e=P), ef[:, 0:P]).then_inc(masks_stored, 16)
            for k in range(3):
                sp.dma_start(fl_d[k].rearrange("(t e) -> t e", e=P), fle[:, k * P:(k + 1) * P]).then_inc(masks_stored, 16)

            xv = x[0:NT * P, :].rearrange("(p j) d -> p (j d)", p=P)
            ov = out[0:NT * P, :].rearrange("(p j) d -> p (j d)", p=P)

            def dense(u, z):
                if (a := sub(u, z, 0)) and not (isinstance(u, int) and a[2] + RING > NSUB):
                    q = a[2]
                    sp.wait_ge(pre_y_ready, q + 1)
                    sp.sem_inc(sp_tick, 1)
                    if isinstance(u, int) and q + RING == NSUB:
                        sp.dma_start(XB[z][:, 0:D], x[N - P:N, :]).then_inc(x_loaded[z], 16)
                    else:
                        sp.dma_start(XB[z][:, :], xv[:, ds((q + RING) * SW, SW)]).then_inc(x_loaded[z], 16)
                if (a := sub(u, z, -3)):
                    _, y, q = a
                    sp.wait_ge(out_ready, q + 1)
                    sp.sem_inc(sp_tick, 1)
                    if isinstance(u, int) and q == NSUB:
                        sp.dma_start(out[NT * P:N, :], OB[y][P - REST:P, 0:D]).then_inc(out_stored[y], 16)
                    else:
                        sp.dma_start(ov[:, ds(q * SW, SW)], OB[y][:, :]).then_inc(out_stored[y], 16)

            for z in range(RING):
                sp.dma_start(XB[z][:, :], xv[:, z * SW:(z + 1) * SW]).then_inc(x_loaded[z], 16)
            counts_sp(sp)
            sp.wait_ge(dve_weights, 4)
            for k in range(3):
                sp.dma_start(B3[k:k + 1, :], B3h[0:1, k * BRW:(k + 1) * BRW]).then_inc(bias_ready, 16)
            edge_sp(sp, dense)

        @block.gpsimd
        def _(g):
            g.memset(ei[:, P:3 * P], 0)
            g.memset(ei[:, 0:P], int(SENT))
            g.memset(ei[:, 3 * P:4 * P], int(SENT)).then_inc(pool_tick, 1)
            g.wait_ge(pool_tick, 1)
            g.memset(ei[0:1, 3 * P:3 * P + 1], -1).then_inc(edge_tiles_set, 1)
            g.memset(ident[:, :], 0.0)
            g.memset(eps[:, :], LN_EPS)
            g.memset(ones[:, :], 1.0)
            g.memset(ones3[:, :], 1.0).then_inc(pool_tick, 1)
            g.wait_ge(pool_tick, 2)
            g.affine_select(out=ident[:, :], in_=ident[:, :], compare_op=ALU.not_equal, fill=1.0, base=0,
                            pattern=[[-1, P]], channel_multiplier=1).then_inc(ident_ready, 1)
            g.iota(iota_i[:, :], pattern=[[P, T]], base=0, channel_multiplier=1)
            g.memset(big_i[:, :], BIG).then_inc(index_consts, 1)
            g.wait_ge(index_consts, 1)
            g.dma_start(sm_d[0:NT * P, :].rearrange("(p j) o -> p (j o)", p=P), big_i[:, 0:NT]).then_inc(table_filled, 16)
            g.dma_start(sm_d[NT * P:N, :].rearrange("(p j) o -> p (j o)", p=REST),
                        big_i[0:REST, 0:1]).then_inc(table_filled, 16)
            g.wait_ge(edge_prep, 2)
            g.affine_select(out=mk_in[:, :], in_=mk_in[:, :], compare_op=ALU.is_gt, fill=0.0, base=0,
                            pattern=[[1, T]], channel_multiplier=-1)
            g.affine_select(out=mk_out[:, :], in_=mk_out[:, :], compare_op=ALU.is_gt, fill=0.0, base=0,
                            pattern=[[-1, T]], channel_multiplier=1).then_inc(carry_masks, 1)
            node_bound = g.to_reg(N - 1)
            slot_bound = g.to_reg(EP - 1)
            g.wait_ge(indices_ready, 1)

            def gate(sem_, value):
                g.wait_ge(sem_, value)
                g.sem_inc(pool_tick, 1)

            for n, (idx, rows_d) in enumerate(((src_i, xs_d), (dst_i, xd_d))):
                def finish(i, k):
                    a = k * CT
                    for j in range(a, a + CT):
                        gate(gathered[j], (n * IT + i) * 16 + 16)
                    g.dma_start(chunk(rows_d, i * 2 + k), three(XR2[:, a * D:(a + CT) * D])).then_inc(rows_stored[k], 16)

                def half(i, k, i0=None):
                    a = k * CT
                    if n or not isinstance(i, int):
                        gate(rows_stored[k], (n * IT + i) * 16)
                    g.tensor_copy(idx_s[:, a:a + CT], idx[:, ds(i * SL + a, CT)]).then_inc(index_staged, 1)
                    gate(index_staged, (n * IT + i) * 2 + k + 1)
                    for j in range(a, a + CT):
                        g.indirect_dma_start(
                            out=XR2[:, j * D:(j + 1) * D], out_offset=None, in_=x,
                            in_offset=bass.IndirectOffsetOnAxis(ap=idx_s[:, j:j + 1], axis=0),
                            bounds_check=node_bound, oob_is_err=False).then_inc(gathered[j], 16)
                        if j == a + 3 and i0 is not None:
                            finish(i0, 1 - k)

                half(0, 0)
                half(0, 1, 0)
                with g.Fori(1, IT) as i:
                    half(i, 0, i - 1)
                    half(i, 1, i)
                finish(IT - 1, 1)
            for k in range(2):
                g.wait_ge(rows_stored[k], 2 * IT * 16)
            g.wait_ge(table_filled, 32)
            with g.Fori(0, IT) as i:
                for a in (0, CT):
                    for j in range(a, a + CT):
                        gate(gathered[j], (2 * IT + i) * 16)
                    g.tensor_copy(idx_s[:, a:a + CT], lead_i[:, ds(i * SL + a, CT)])
                    g.tensor_copy(val_s[:, a:a + CT], iota_i[:, ds(i * SL + a, CT)]).then_inc(index_staged, 1)
                    gate(index_staged, 4 * IT + i * 2 + a // CT + 1)
                    for j in range(a, a + CT):
                        g.indirect_dma_start(
                            out=sm_d, out_offset=bass.IndirectOffsetOnAxis(ap=idx_s[:, j:j + 1], axis=0),
                            in_=val_s[:, j:j + 1], in_offset=None,
                            bounds_check=node_bound, oob_is_err=False).then_inc(gathered[j], 16)
            for j in range(SL):
                g.wait_ge(gathered[j], 3 * IT * 16)

            def slots_of(i, k):
                a = k * CT
                for j in range(a, a + CT):
                    gate(gathered[j], (3 * IT + i) * 16 + 16)
                g.tensor_copy(slot_i[:, ds(i * SL + a, CT)], val_s[:, a:a + CT]).then_inc(index_staged, 1)

            def look_up(i, k, before):
                a = k * CT
                g.tensor_copy(idx_s[:, a:a + CT], src_i[:, ds(i * SL + a, CT)]).then_inc(index_staged, 1)
                gate(index_staged, 6 * IT + 1 if before is None else 6 * IT + i * 4 + 2 * k)
                for j in range(a, a + CT):
                    g.indirect_dma_start(
                        out=val_s[:, j:j + 1], out_offset=None, in_=sm_d,
                        in_offset=bass.IndirectOffsetOnAxis(ap=idx_s[:, j:j + 1], axis=0),
                        bounds_check=node_bound, oob_is_err=False).then_inc(gathered[j], 16)
                    if j == a + 3 and before is not None:
                        slots_of(before, 1 - k)

            look_up(0, 0, None)
            look_up(0, 1, 0)
            with g.Fori(1, IT) as i:
                look_up(i, 0, i - 1)
                look_up(i, 1, i)
            slots_of(IT - 1, 1)
            g.wait_ge(index_staged, 10 * IT)
            edge_pool(g, node_bound, slot_bound, gate)

        @block.tensor
        def _(pe):
            pe.wait_ge(ident_ready, 1)
            pe.wait_ge(edge_prep, 1)
            nc.tensor.matmul(BK[5][:, 0:2 * T], ones[0:T, :], fld[:, :], start=True, stop=True)
            for k, a in enumerate((ef[:, 0:P], ef[:, P:2 * P], ef[:, 2 * P:3 * P], lead[:, :])):
                last = nc.tensor.transpose(BK[6][:, k * T:(k + 1) * T], a, ident[0:T, 0:T])
            last.then_inc(edge_columns, 1)

            def dense(u, z):
                if (a := sub(u, z, 2)):
                    it, y, q = a
                    pe.wait_ge(x_loaded[y], it * 16 + 16)
                    if past(q, 1):
                        pe.wait_ge(xT_copied, q)
                    if past(q, 4):
                        pe.wait_ge(yT_copied, q - 3)
                    for t in range(tiles(q)):
                        last = nc.tensor.transpose(BK[4][:, t * D:(t + 1) * D], XB[y][:, t * D:(t + 1) * D], ident[:, :])
                    last.then_inc(x_transposed, 1)
                if (a := sub(u, z, 1)):
                    _, y, q = a
                    w = tiles(q) * D
                    pe.wait_ge(xT_copied, q + 1)
                    if past(q, 1):
                        pe.wait_ge(hT_ready, q)
                    nc.tensor.matmul(BK[5][:, 0:w], M[0][:, :], xT[y % 2][:, 0:w], start=True, stop=True).then_inc(h1_made, 1)
                if (a := sub(u, z, 0)):
                    _, y, q = a
                    pe.wait_ge(hT_ready, q + 1)
                    if past(q, 1):
                        pe.wait_ge(pre_y_ready, q)
                    rows(BK[6], tiles(q), OFF_B + D, hT[y % 2], M[1]).then_inc(h2_made, 1)
                if (a := sub(u, z, -2)):
                    _, y, q = a
                    pe.wait_ge(yT_copied, q + 1)
                    if past(q, 1):
                        pe.wait_ge(z_ready, q)
                    rows(BK[7], tiles(q), OFF_DX, yT[y % 2], M[2]).then_inc(xl_made, 1)
                if (a := sub(u, z, -1)):
                    _, y, q = a
                    pe.wait_ge(y_ready, q + 1)
                    pe.wait_ge(xT_copied, min(q + 4, NSUB + 1) if isinstance(q, int) else q + 4)
                    if past(q, 1):
                        pe.wait_ge(yT_copied, q)
                    for t in range(tiles(q)):
                        last = nc.tensor.transpose(BK[4][:, t * D:(t + 1) * D], Y[y][:, t * D:(t + 1) * D], ident[:, :])
                    last.then_inc(y_transposed, 1)

            def rows(bank, n, off, lhs, w):
                b = B3[:, off:off + D]
                nc.tensor.matmul(bank[:, 0:n * D], ones3[:, :], b if n == 1 else bc_mid(b, n),
                                 start=True, stop=False)
                for t in range(n):
                    last = nc.tensor.matmul(bank[:, t * D:(t + 1) * D], lhs[:, t * D:(t + 1) * D], w[:, :],
                                            start=False, stop=(t == n - 1))
                return last

            edge_counts(pe)
            pe.wait_ge(weights_loaded, LOADS * 16)
            nc.tensor.transpose(BK[0][:, 0:D], Wemb[:, :], ident[:, :])
            nc.tensor.transpose(BK[0][:, D:2 * D], rt[:, :], ident[:, :]).then_inc(weight_products, 1)
            count_carries(pe)
            pe.wait_ge(counts_copied, CH)
            pe.wait_ge(act_weights, 2)
            nc.tensor.matmul(BK[1][:, :], wT[:, 0:D], bs[:, 0:B * D], start=True, stop=True)
            nc.tensor.matmul(BK[2][:, 0:D], wT[:, 0:D], slf[:, 0:D], start=True, stop=True)
            nc.tensor.matmul(BK[2][:, 2 * D:3 * D], wT[:, D:2 * D], gw[:, :], start=True, stop=True)
            pe.wait_ge(dve_weights, 1)
            nc.tensor.matmul(BK[2][:, D:2 * D], wbc[:, 0:P], slf[:, 0:D], start=True, stop=True)
            nc.tensor.matmul(BK[3][:, :], wbc[:, 0:P], bs[:, 0:B * D], start=True, stop=True)
            nc.tensor.matmul(BK[2][:, 3 * D:4 * D], wbc[:, P:2 * P], gw[:, :], start=True, stop=True).then_inc(weight_products, 1)
            pe.wait_ge(dve_weights, 3)
            nc.tensor.transpose(BK[4][:, 0:D], BR[:, OFF_B:OFF_B + D], ident[:, :]).then_inc(weight_products, 1)
            pe.wait_ge(bias_ready, 48)
            pe.wait_ge(dve_weights, 5)
            prelude(dense)
            edge_pe(pe, dense, rows)

        @block.scalar
        def _(act):
            for dst_ap, src_ap in LOAD_LIST:
                act.dma_start(dst_ap, src_ap).then_inc(weights_loaded, 16)
            def dense(u, z, between=None):
                if (a := sub(u, z, -3)):
                    it, y, q = a
                    n = tiles(q)
                    act.wait_ge(z_shift, q + 1)
                    if past(q, RING):
                        act.wait_ge(out_stored[y], it * 16)
                    for t in range(n):
                        last = nc.scalar.activation(OB[y][:, t * D:(t + 1) * D], Z[y][:, t * D:(t + 1) * D],
                                                    ACT.Identity, bias=dnb2[y % 2][:, t:t + 1],
                                                    scale=drs2[y % 2][:, t:t + 1])
                    last.then_inc(out_ready, 1)
                if (a := sub(u, z, 2)):
                    _, y, q = a
                    w = tiles(q) * D
                    act.wait_ge(x_transposed, q + 1)
                    if past(q, 2):
                        act.wait_ge(h1_made, q - 1)
                    nc.scalar.copy(xT[y % 2][:, 0:w], BK[4][:, 0:w]).then_inc(xT_copied, 1)
                if (a := sub(u, z, 1)):
                    _, y, q = a
                    w = tiles(q) * D
                    act.wait_ge(h1_made, q + 1)
                    if past(q, 2):
                        act.wait_ge(h2_made, q - 1)
                    nc.scalar.activation(hT[y % 2][:, 0:w], BK[5][:, 0:w], ACT.Relu, bias=b0c[:, 0:1]).then_inc(hT_ready, 1)
                if (a := sub(u, z, -1)):
                    _, y, q = a
                    w = tiles(q) * D
                    act.wait_ge(y_transposed, q + 1)
                    if past(q, 2):
                        act.wait_ge(xl_made, q - 1)
                    nc.scalar.copy(yT[y % 2][:, 0:w], BK[4][:, 0:w]).then_inc(yT_copied, 1)
                if between:
                    between()
                if (a := sub(u, z, 0)):
                    _, y, q = a
                    n = tiles(q)
                    act.wait_ge(y_stats, q + 1)
                    if past(q, 2):
                        act.wait_ge(y_ready, q - 1)
                    nc.scalar.activation(dsd1[y % 2][:, 0:n], dmv1[y % 2][:, 1:2 * n:2], ACT.Sqrt,
                                         bias=eps[:, 0:1]).then_inc(y_deviation, 1)
                if (a := sub(u, z, -2)):
                    it, y, q = a
                    n = tiles(q)
                    act.wait_ge(z_stats, q + 1)
                    if past(q, 2):
                        act.wait_ge(z_shift, q - 1)
                    nc.scalar.activation(dsd2[y % 2][:, 0:n], dmv2[y % 2][:, 1:2 * n:2], ACT.Sqrt,
                                         bias=eps[:, 0:1]).then_inc(z_deviation, 1)

            edge_counts_act(act)
            act.wait_ge(weight_products, 1)
            nc.scalar.copy(wT[:, :], BK[0][:, 0:2 * D]).then_inc(act_weights, 1)
            carries_act(act, -1, BK[6], R, cti)
            act.wait_ge(dve_weights, 1)
            nc.scalar.activation(vt[:, :], vt[:, :], ACT.Sqrt).then_inc(act_weights, 1)
            act.wait_ge(dve_weights, 5)
            prelude(dense)
            edge_act(act, dense)

        @block.vector
        def _(v):
            chain = [0]

            def link(ins):
                chain[0] += 1
                ins.then_inc(dve_order, 1)
                v.wait_ge(dve_order, chain[0])

            v.wait_ge(edges_loaded, 9 * 16)
            link(nc.vector.tensor_copy(ef[:, :], ei[:, :]))
            v.wait_ge(ident_ready, 1)
            for k, c in enumerate((0, P - 1)):
                nc.vector.tensor_scalar(fle[:, k * P:(k + 1) * P], ef[:, 0:P], ef[:, c:c + 1], None, ALU.is_equal)
                nc.vector.tensor_scalar(fld[:, k * T:(k + 1) * T], ident[0:T, 0:T], ef[:, c:c + 1], None, ALU.mult)
            nc.vector.memset(fle[:, 2 * P:3 * P], 1.0)
            link(nc.vector.tensor_tensor(lead[:, :], ef[:, 0:P], ef[:, 3 * P:4 * P], ALU.is_equal))
            nc.vector.scalar_tensor_tensor(out=lead[:, :], in0=lead[:, :], scalar=float(BIG), in1=ef[:, 0:P],
                                           op0=ALU.mult, op1=ALU.add).then_inc(edge_prep, 1)
            v.wait_ge(edge_columns, 1)
            nc.vector.tensor_copy(FBC[:, :], BK[5][:, 0:2 * T])
            link(nc.vector.tensor_copy(EC[:, :], BK[6][:, 0:4 * T]))
            nc.vector.tensor_copy(src_i[:, :], col(1))
            nc.vector.tensor_scalar(dst_i[:, :], col(0), float(N - 1), None, ALU.min)
            nc.vector.tensor_copy(lead_i[:, :], col(3)).then_inc(indices_ready, 1)
            nc.vector.tensor_scalar(mk_in[:, :], FBC[0:T, 0:T], ef[:, P - 1:P], None, ALU.is_equal)
            nc.vector.tensor_scalar(mk_out[:, :], FBC[0:T, T:2 * T], ef[:, 0:1], None, ALU.is_equal).then_inc(edge_prep, 1)
            nc.vector.tensor_tensor(eqc[:, 0:T], col(0), FBC[:, 0:T], ALU.is_equal)
            nc.vector.tensor_tensor(eqc[:, T:2 * T], col(0), FBC[:, T:2 * T], ALU.is_equal)
            for r in range(R):
                last = nc.vector.tensor_scalar(OH[:, :].rearrange("p (t r) -> p t r", r=R)[:, :, r], col(2), float(r), None, ALU.is_equal)
            link(last)

            count_tiles(v)
            v.wait_ge(weights_loaded, LOADS * 16)
            nc.vector.tensor_copy(wbc[:, 0:P], bemb[:, 0:1].broadcast_to([P, P]))
            nc.vector.tensor_copy(wbc[:, P:2 * P], b1c[:, 0:1].broadcast_to([P, P]))
            nc.vector.tensor_scalar_add(vt[:, :], bnv[:, :], BN_EPS).then_inc(dve_weights, 1)
            v.wait_ge(act_weights, 2)
            link(nc.vector.reciprocal(vt[:, :], vt[:, :]))
            link(nc.vector.tensor_tensor(sc[:, :], bng[:, :], vt[:, :], ALU.mult))
            nc.vector.tensor_tensor(four(V[1]), four(bs[:, B * D:2 * B * D]), bc_mid(sc[:, D:2 * D], B), ALU.mult)
            nc.vector.tensor_tensor(M[1][:, :], slf[:, D:2 * D], sc[:, D:2 * D], ALU.mult)
            link(nc.vector.tensor_tensor(vt[:, :], bnm[:, :], sc[:, :], ALU.mult))
            link(nc.vector.tensor_tensor(vt[:, :], bnb[:, :], vt[:, :], ALU.subtract))
            v.wait_ge(weight_products, 2)
            nc.vector.tensor_tensor(four(V[0]), four(BK[1][:, :]), bc_mid(sc[:, 0:D], B), ALU.mult)
            nc.vector.tensor_tensor(four(BR[:, 0:B * D]), four(BK[3][:, :]), bc_mid(sc[:, 0:D], B), ALU.mult)
            nc.vector.tensor_tensor(M[0][:, :], BK[2][:, 0:D], sc[:, 0:D], ALU.mult)
            nc.vector.tensor_copy(M[2][:, :], BK[2][:, 2 * D:3 * D])
            nc.vector.tensor_tensor(BR[:, OFF_B:OFF_B + D], BK[2][:, D:2 * D], sc[:, 0:D], ALU.mult)
            nc.vector.tensor_copy(BR[:, OFF_B + D:OFF_B + 2 * D], vt[:, D:2 * D])
            nc.vector.tensor_copy(BR[:, OFF_B + 2 * D:OFF_B + 3 * D], BK[2][:, 3 * D:4 * D])
            nc.vector.tensor_copy(BR[:, OFF_GB:OFF_GB + D], gbb[:, :])
            link(nc.vector.tensor_tensor(BR[:, OFF_DX:OFF_DX + D], BK[2][:, 3 * D:4 * D], gbb[:, :], ALU.add))
            link(nc.vector.tensor_tensor(BR[:, OFF_B:OFF_B + D], BR[:, OFF_B:OFF_B + D], vt[:, 0:D], ALU.add))
            link(nc.vector.tensor_copy(B3h[0:1, 0:BRW], BR[0:1, :]))
            nc.vector.tensor_tensor(bsp[0], BR[0:1, :], B3h[0:1, 0:BRW], ALU.subtract).then_inc(dve_weights, 2)
            v.wait_ge(dve_weights, 3)
            link(nc.vector.tensor_copy(B3h[0:1, BRW:2 * BRW], bsp[0]))
            link(nc.vector.tensor_tensor(bsp[1], bsp[0], B3h[0:1, BRW:2 * BRW], ALU.subtract))
            nc.vector.tensor_copy(B3h[0:1, 2 * BRW:3 * BRW], bsp[1]).then_inc(dve_weights, 1)
            v.wait_ge(weight_products, 3)
            nc.vector.tensor_copy(b0c[:, :], BK[4][:, 0:1]).then_inc(dve_weights, 1)

            coefficients(v, link)

            def dense(u, z):
                a, b = sub(u, z, 0), sub(u, z, -2)
                if a:
                    _, y, q = a
                    w = tiles(q) * D
                    v.wait_ge(h2_made, q + 1)
                    if past(q, RING):
                        v.wait_ge(z_ready, q - 3)
                    nc.vector.scalar_tensor_tensor(out=Y[y][:, 0:w], in0=BK[6][:, 0:w], scalar=0.0, in1=XB[y][:, 0:w],
                                                   op0=ALU.max, op1=ALU.add).then_inc(pre_y_ready, 1)
                if b:
                    _, y, q = b
                    w = tiles(q) * D
                    v.wait_ge(xl_made, q + 1)
                    if past(q, RING):
                        v.wait_ge(out_ready, q - 3)
                    nc.vector.tensor_tensor(Z[y][:, 0:w], BK[7][:, 0:w], Y[y][:, 0:w], ALU.add).then_inc(z_ready, 1)
                both = [(a, pre_y_ready, Y, dst1, dmv1, y_moments, y_stats), (b, z_ready, Z, dst2, dmv2, z_moments, z_stats)]
                for c, ready, rows_, bn, _, moments, _ in both:
                    if c:
                        _, y, q = c
                        v.wait_ge(ready, q + 1)
                        for t in range(tiles(q)):
                            last = nc.vector.bn_stats(bn[y % 2][:, 6 * t:6 * t + 6], rows_[y][:, t * D:(t + 1) * D])
                        last.then_inc(moments, 1)
                for c, _, _, bn, mv_, moments, stats in both:
                    if c:
                        _, y, q = c
                        v.wait_ge(moments, q + 1)
                        v.sem_inc(dve_tick, 1)
                        for t in range(tiles(q)):
                            last = nc.vector.bn_aggr(mv_[y % 2][:, 2 * t:2 * t + 2], bn[y % 2][:, 6 * t:6 * t + 6])
                        last.then_inc(stats, 1)
                for c, deviation_ready, rs_, sd_, scale_ready in ((a, y_deviation, drs1, dsd1, y_scale), (b, z_deviation, drs2, dsd2, z_scale)):
                    if c:
                        _, y, q = c
                        n = tiles(q)
                        v.wait_ge(deviation_ready, q + 1)
                        nc.vector.reciprocal(rs_[y % 2][:, 0:n], sd_[y % 2][:, 0:n]).then_inc(scale_ready, 1)
                if a:
                    _, y, q = a
                    v.wait_ge(y_scale, q + 1)
                    for t in range(tiles(q)):
                        o = Y[y][:, t * D:(t + 1) * D]
                        last = nc.vector.tensor_scalar(o, o, dmv1[y % 2][:, 2 * t:2 * t + 1], drs1[y % 2][:, t:t + 1],
                                                       ALU.subtract, ALU.mult)
                    last.then_inc(y_ready, 1)
                if b:
                    _, y, q = b
                    n = tiles(q)
                    v.wait_ge(z_scale, q + 1)
                    nc.vector.scalar_tensor_tensor(out=dnb2[y % 2][:, 0:n], in0=dmv2[y % 2][:, 0:2 * n:2], scalar=-1.0,
                                                   in1=drs2[y % 2][:, 0:n], op0=ALU.mult, op1=ALU.mult).then_inc(z_shift, 1)

            prelude(dense)
            edge_dve(v, link, dense)

_INS = ["x", "src", "dst", "edge_type_8", "L0_gnn_W_emb", "L0_gnn_b_emb", "L0_gnn_bases", "L0_gnn_w_coe",
        "L0_gnn_self_loop", "L0_gnn_bn_gamma", "L0_gnn_bn_beta", "L0_gnn_bn_mean", "L0_gnn_bn_var",
        "L1_gnn_comp", "L1_gnn_basis", "L1_gnn_root", "L1_gnn_bias1", "L1_gnn_gat_w", "L1_gnn_att_src",
        "L1_gnn_att_dst", "L1_gnn_gat_bias"]


def kernel(**inputs):
    import numpy as np
    import concourse.bacc as bacc
    from concourse.bass_utils import run_bass_kernel_spmd

    nc = bacc.Bacc("TRN2", target_bir_lowering=False, num_devices=1)
    arrays, args = {}, []
    for name in _INS:
        a = np.ascontiguousarray(inputs[name])
        arrays[f"in_{name}"] = a
        args.append(nc.dram_tensor(f"in_{name}", a.shape, mybir.dt.from_np(a.dtype), kind="ExternalInput").ap())
    out = nc.dram_tensor("out", arrays["in_x"].shape, mybir.dt.float32, kind="ExternalOutput").ap()
    gnn_program(nc, *args, out)
    r = run_bass_kernel_spmd(nc, [arrays], core_ids=[0])
    return r.results[0]["out"]
```
